# Optimizing a Trainium2 kernel written in Bass

```python
import numpy as np
import jax
import jax.numpy as jnp

def _softmax(x, axis=-1):
    return jax.nn.softmax(x, axis=axis)

def _gelu(x):
    return jax.nn.gelu(x, approximate=True)

def _silu(x):
    return jax.nn.silu(x)

def _sigmoid(x):
    return jax.nn.sigmoid(x)

def _layernorm(x, axis=-1, eps=1e-05):
    m = jnp.mean(x, axis=axis, keepdims=True)
    v = jnp.var(x, axis=axis, keepdims=True)
    return (x - m) / jnp.sqrt(v + eps)

def _scatter_add(tgt, idx, src, axis=0):
    return tgt.at[idx].add(src)

def _segment_sum(src, seg, n):
    return jax.ops.segment_sum(src, seg, n)
kernel_name = 'mk_lm_tower_d1_tok_ids256_r4_29c906'

def setup_inputs(seed: int=0):
    np.random.seed(seed)
    _w = jnp.asarray

    def _rec_inputs():
        import jax
        import jax.numpy as jnp
        _rk = jax.random.key(seed)
        x = jax.random.randint(jax.random.fold_in(_rk, 1), (8, 512), 0, 64, jnp.int32)
        return x
    x = _rec_inputs()

    def _L0_tok_setup():
        import jax, jax.numpy as jnp
        import numpy as np
        BATCH = 32
        SEQ = 1024
        HID = 64
        VOCAB = 8000
        NEXT_ID = 5
        EPS = 1e-05

        def _positions(state):
            eq = state == NEXT_ID
            starts = jnp.pad(eq[:, :-1], ((0, 0), (1, 0)))
            instr = jnp.cumsum(starts.astype(jnp.int32), axis=-1)
            pos = jnp.arange(state.shape[-1], dtype=jnp.int32)
            seg_start = jnp.where(starts, pos[None, :], 0)
            last_start = jax.lax.cummax(seg_start, axis=1)
            args = pos[None, :] - last_start
            return (instr, args)
        key = jax.random.key(seed)
        ks = jax.random.split(key, 6)
        state = jax.random.randint(ks[0], (BATCH, SEQ), 0, 64, dtype=jnp.int64)
        token_emb = jax.random.normal(ks[1], (VOCAB, HID), dtype=jnp.float32) * 0.02
        instr_emb = jax.random.normal(ks[2], (SEQ, HID), dtype=jnp.float32) * 0.02
        arg_emb = jax.random.normal(ks[3], (SEQ, HID), dtype=jnp.float32) * 0.02
        gamma = jnp.ones((HID,), dtype=jnp.float32)
        beta = jnp.zeros((HID,), dtype=jnp.float32)
        return {'state': state, 'token_emb': token_emb, 'instr_emb': instr_emb, 'arg_emb': arg_emb, 'gamma': gamma, 'beta': beta}
    _L0_tok_all = _L0_tok_setup()
    _L0_tok_in = {k: v for k, v in _L0_tok_all.items() if k in ('token_emb', 'instr_emb', 'arg_emb', 'gamma', 'beta')}
    del _L0_tok_all

    def _L0_attn_setup():
        import jax, jax.numpy as jnp
        import numpy as np
        N_HEAD = 16
        NOPE = 32
        ROPE = 64
        VDIM = 32
        HD = NOPE + ROPE
        WINDOW = 128
        KEEP = 128
        EPS = 1e-06

        def _freqs(T, dim=ROPE, theta=10000.0):
            f = 1.0 / theta ** (np.arange(0, dim, 2, dtype=np.float32) / dim)
            ang = np.outer(np.arange(T, dtype=np.float32), f)
            return (jnp.asarray(np.cos(ang)), jnp.asarray(np.sin(ang)))

        def _rms(x, w):
            return x * jax.lax.rsqrt(jnp.mean(x * x, -1, keepdims=True) + EPS) * w

        def _rope(x, cos, sin):
            T = x.shape[-2]
            c = cos[:T][None, None]
            s = sin[:T][None, None]
            xr, xi = jnp.split(x, 2, -1)
            return jnp.concatenate([xr * c - xi * s, xr * s + xi * c], -1)

        def _attn(q, k, v, mask=None):
            s = jnp.einsum('bhqd,bhkd->bhqk', q, k) / np.float32(np.sqrt(HD))
            if mask is not None:
                s = jnp.where(mask, s, jnp.float32(-1000000000.0))
            return jnp.einsum('bhqk,bhkd->bhqd', jax.nn.softmax(s, -1), v)
        key = jax.random.key(seed)
        ks = jax.random.split(key, 16)
        w = lambda k, shape: jax.random.normal(k, shape, jnp.float32) * 0.02
        B, T, C = (2, 512, 64)
        return {'x': jax.random.normal(ks[0], (B, T, C), jnp.float32), 'Wcq': w(ks[1], (C, 96)), 'q_norm_w': jnp.ones((96,), jnp.float32), 'Wq_nope': w(ks[2], (96, N_HEAD * NOPE)), 'Wq_rope': w(ks[3], (96, N_HEAD * ROPE)), 'Wckv': w(ks[4], (C, 32)), 'kv_norm_w': jnp.ones((32,), jnp.float32), 'Wk_nope': w(ks[5], (32, N_HEAD * NOPE)), 'Wv': w(ks[6], (32, N_HEAD * VDIM)), 'Wk_rope': w(ks[7], (C, ROPE)), 'W_imp': w(ks[8], (C, 1)), 'Wsel_k': w(ks[9], (C, N_HEAD * HD)), 'Wsel_v': w(ks[10], (C, N_HEAD * VDIM)), 'Wwin_k': w(ks[11], (C, N_HEAD * HD)), 'Wwin_v': w(ks[12], (C, N_HEAD * VDIM)), 'Wgate': w(ks[13], (C, 3)), 'Wproj': w(ks[14], (N_HEAD * VDIM, C))}
    _L0_attn_all = _L0_attn_setup()
    _L0_attn_in = {k: v for k, v in _L0_attn_all.items() if k in ('Wcq', 'q_norm_w', 'Wq_nope', 'Wq_rope', 'Wckv', 'kv_norm_w', 'Wk_nope', 'Wv', 'Wk_rope', 'W_imp', 'Wsel_k', 'Wsel_v', 'Wwin_k', 'Wwin_v', 'Wgate', 'Wproj')}
    del _L0_attn_all

    def _L0_ffn_setup():
        import jax, jax.numpy as jnp
        import numpy as np
        NUM_EXPERTS = 8
        TOP_K = 2
        B, S, D = (8, 2048, 64)

        def _moe(tokens, router_w, w1, b1, w2, b2):
            N = tokens.shape[0]
            E = router_w.shape[0]
            logits = tokens.astype(jnp.float32) @ router_w.astype(jnp.float32).T
            probs = jax.nn.softmax(logits, axis=-1)
            rw, re = jax.lax.top_k(probs, TOP_K)
            if TOP_K > 1:
                rw = rw / jnp.maximum(rw.sum(-1, keepdims=True), 1e-12)
            rw = rw.astype(tokens.dtype)
            combine = jnp.zeros((N, E), tokens.dtype).at[jnp.arange(N)[:, None], re].set(rw)
            out = tokens
            for e in range(E):
                h = jax.nn.gelu(tokens @ w1[e] + b1[e], approximate=False)
                y = h @ w2[e] + b2[e]
                out = out + combine[:, e:e + 1] * y
            return out
        key = jax.random.key(seed)
        ks = jax.random.split(key, 4)
        scale = 1.0 / np.sqrt(D).astype(np.float32)
        return {'input_embeddings': jax.random.normal(ks[0], (B, S, D), jnp.float32), 'router_w': jax.random.normal(ks[1], (NUM_EXPERTS, D), jnp.float32) * scale, 'w1': jax.random.normal(ks[2], (NUM_EXPERTS, D, D), jnp.float32) * scale, 'b1': jnp.zeros((NUM_EXPERTS, D), jnp.float32), 'w2': jax.random.normal(ks[3], (NUM_EXPERTS, D, D), jnp.float32) * scale, 'b2': jnp.zeros((NUM_EXPERTS, D), jnp.float32)}
    _L0_ffn_all = _L0_ffn_setup()
    _L0_ffn_in = {k: v for k, v in _L0_ffn_all.items() if k in ('router_w', 'w1', 'b1', 'w2', 'b2')}
    del _L0_ffn_all
    return {'x': x, 'L0_tok_token_emb': _L0_tok_in['token_emb'], 'L0_tok_instr_emb': _L0_tok_in['instr_emb'], 'L0_tok_arg_emb': _L0_tok_in['arg_emb'], 'L0_tok_gamma': _L0_tok_in['gamma'], 'L0_tok_beta': _L0_tok_in['beta'], 'L0_attn_Wcq': _L0_attn_in['Wcq'], 'L0_attn_q_norm_w': _L0_attn_in['q_norm_w'], 'L0_attn_Wq_nope': _L0_attn_in['Wq_nope'], 'L0_attn_Wq_rope': _L0_attn_in['Wq_rope'], 'L0_attn_Wckv': _L0_attn_in['Wckv'], 'L0_attn_kv_norm_w': _L0_attn_in['kv_norm_w'], 'L0_attn_Wk_nope': _L0_attn_in['Wk_nope'], 'L0_attn_Wv': _L0_attn_in['Wv'], 'L0_attn_Wk_rope': _L0_attn_in['Wk_rope'], 'L0_attn_W_imp': _L0_attn_in['W_imp'], 'L0_attn_Wsel_k': _L0_attn_in['Wsel_k'], 'L0_attn_Wsel_v': _L0_attn_in['Wsel_v'], 'L0_attn_Wwin_k': _L0_attn_in['Wwin_k'], 'L0_attn_Wwin_v': _L0_attn_in['Wwin_v'], 'L0_attn_Wgate': _L0_attn_in['Wgate'], 'L0_attn_Wproj': _L0_attn_in['Wproj'], 'L0_ffn_router_w': _L0_ffn_in['router_w'], 'L0_ffn_w1': _L0_ffn_in['w1'], 'L0_ffn_b1': _L0_ffn_in['b1'], 'L0_ffn_w2': _L0_ffn_in['w2'], 'L0_ffn_b2': _L0_ffn_in['b2']}

def reference(x, L0_tok_token_emb, L0_tok_instr_emb, L0_tok_arg_emb, L0_tok_gamma, L0_tok_beta, L0_attn_Wcq, L0_attn_q_norm_w, L0_attn_Wq_nope, L0_attn_Wq_rope, L0_attn_Wckv, L0_attn_kv_norm_w, L0_attn_Wk_nope, L0_attn_Wv, L0_attn_Wk_rope, L0_attn_W_imp, L0_attn_Wsel_k, L0_attn_Wsel_v, L0_attn_Wwin_k, L0_attn_Wwin_v, L0_attn_Wgate, L0_attn_Wproj, L0_ffn_router_w, L0_ffn_w1, L0_ffn_b1, L0_ffn_w2, L0_ffn_b2):
    import jax
    import jax.numpy as jnp

    def _L0_tok_ref(state, token_emb, instr_emb, arg_emb, gamma, beta):
        import jax, jax.numpy as jnp
        import numpy as np
        BATCH = 32
        SEQ = 1024
        HID = 64
        VOCAB = 8000
        NEXT_ID = 5
        EPS = 1e-05

        def _positions(state):
            eq = state == NEXT_ID
            starts = jnp.pad(eq[:, :-1], ((0, 0), (1, 0)))
            instr = jnp.cumsum(starts.astype(jnp.int32), axis=-1)
            pos = jnp.arange(state.shape[-1], dtype=jnp.int32)
            seg_start = jnp.where(starts, pos[None, :], 0)
            last_start = jax.lax.cummax(seg_start, axis=1)
            args = pos[None, :] - last_start
            return (instr, args)
        instr, args = _positions(state)
        embedded = token_emb[state] + instr_emb[instr] + arg_emb[args]
        mean = jnp.mean(embedded, axis=-1, keepdims=True)
        var = jnp.mean(jnp.square(embedded - mean), axis=-1, keepdims=True)
        normed = (embedded - mean) * jax.lax.rsqrt(var + EPS)
        return normed * gamma + beta

    def _L0_attn_ref(x, Wcq, q_norm_w, Wq_nope, Wq_rope, Wckv, kv_norm_w, Wk_nope, Wv, Wk_rope, W_imp, Wsel_k, Wsel_v, Wwin_k, Wwin_v, Wgate, Wproj):
        import jax, jax.numpy as jnp
        import numpy as np
        N_HEAD = 16
        NOPE = 32
        ROPE = 64
        VDIM = 32
        HD = NOPE + ROPE
        WINDOW = 128
        KEEP = 128
        EPS = 1e-06

        def _freqs(T, dim=ROPE, theta=10000.0):
            f = 1.0 / theta ** (np.arange(0, dim, 2, dtype=np.float32) / dim)
            ang = np.outer(np.arange(T, dtype=np.float32), f)
            return (jnp.asarray(np.cos(ang)), jnp.asarray(np.sin(ang)))

        def _rms(x, w):
            return x * jax.lax.rsqrt(jnp.mean(x * x, -1, keepdims=True) + EPS) * w

        def _rope(x, cos, sin):
            T = x.shape[-2]
            c = cos[:T][None, None]
            s = sin[:T][None, None]
            xr, xi = jnp.split(x, 2, -1)
            return jnp.concatenate([xr * c - xi * s, xr * s + xi * c], -1)

        def _attn(q, k, v, mask=None):
            s = jnp.einsum('bhqd,bhkd->bhqk', q, k) / np.float32(np.sqrt(HD))
            if mask is not None:
                s = jnp.where(mask, s, jnp.float32(-1000000000.0))
            return jnp.einsum('bhqk,bhkd->bhqd', jax.nn.softmax(s, -1), v)
        B, T, C = x.shape
        cos, sin = _freqs(T)
        cq = _rms(x @ Wcq, q_norm_w)
        qn = (cq @ Wq_nope).reshape(B, T, N_HEAD, NOPE).transpose(0, 2, 1, 3)
        qr = _rope((cq @ Wq_rope).reshape(B, T, N_HEAD, ROPE).transpose(0, 2, 1, 3), cos, sin)
        q = jnp.concatenate([qn, qr], -1)
        gate = jax.nn.softmax((x @ Wgate).mean(1), -1)
        ckv = _rms(x @ Wckv, kv_norm_w)
        kn = (ckv @ Wk_nope).reshape(B, T, N_HEAD, NOPE).transpose(0, 2, 1, 3)
        v1 = (ckv @ Wv).reshape(B, T, N_HEAD, VDIM).transpose(0, 2, 1, 3)
        kr = (x @ Wk_rope / N_HEAD).reshape(B, T, 1, ROPE).transpose(0, 2, 1, 3)
        kr = _rope(kr, cos, sin)
        k1 = jnp.concatenate([kn, jnp.broadcast_to(kr, (B, N_HEAD, T, ROPE))], -1)
        ii = jnp.arange(T)
        causal = ii[:, None] >= ii[None, :]
        o1 = _attn(q, k1, v1, causal[None, None])
        scores = (x @ W_imp)[..., 0]
        _, idx = jax.lax.top_k(scores, KEEP)
        idx = jnp.sort(idx, 1)
        sel = jnp.take_along_axis(x, idx[..., None], 1)
        ks = (sel @ Wsel_k).reshape(B, KEEP, N_HEAD, HD).transpose(0, 2, 1, 3)
        vs = (sel @ Wsel_v).reshape(B, KEEP, N_HEAD, VDIM).transpose(0, 2, 1, 3)
        ks = jnp.concatenate([ks[..., :NOPE], _rope(ks[..., NOPE:], cos, sin)], -1)
        o2 = _attn(q, ks, vs)
        kw = (x @ Wwin_k).reshape(B, T, N_HEAD, HD).transpose(0, 2, 1, 3)
        vw = (x @ Wwin_v).reshape(B, T, N_HEAD, VDIM).transpose(0, 2, 1, 3)
        kw = jnp.concatenate([kw[..., :NOPE], _rope(kw[..., NOPE:], cos, sin)], -1)
        winmask = causal & (ii[:, None] - ii[None, :] < WINDOW)
        o3 = _attn(q, kw, vw, winmask[None, None])
        g = gate[:, :, None, None, None]
        o = g[:, 0] * o1 + g[:, 1] * o2 + g[:, 2] * o3
        o = o.transpose(0, 2, 1, 3).reshape(B, T, N_HEAD * VDIM)
        return o @ Wproj

    def _L0_ffn_ref(input_embeddings, router_w, w1, b1, w2, b2):
        import jax, jax.numpy as jnp
        import numpy as np
        NUM_EXPERTS = 8
        TOP_K = 2
        B, S, D = (8, 2048, 64)

        def _moe(tokens, router_w, w1, b1, w2, b2):
            N = tokens.shape[0]
            E = router_w.shape[0]
            logits = tokens.astype(jnp.float32) @ router_w.astype(jnp.float32).T
            probs = jax.nn.softmax(logits, axis=-1)
            rw, re = jax.lax.top_k(probs, TOP_K)
            if TOP_K > 1:
                rw = rw / jnp.maximum(rw.sum(-1, keepdims=True), 1e-12)
            rw = rw.astype(tokens.dtype)
            combine = jnp.zeros((N, E), tokens.dtype).at[jnp.arange(N)[:, None], re].set(rw)
            out = tokens
            for e in range(E):
                h = jax.nn.gelu(tokens @ w1[e] + b1[e], approximate=False)
                y = h @ w2[e] + b2[e]
                out = out + combine[:, e:e + 1] * y
            return out
        b, s, d = input_embeddings.shape
        tokens = input_embeddings.reshape(b * s, d)
        return _moe(tokens, router_w, w1, b1, w2, b2).reshape(b, s, d)
    h = _L0_tok_ref(x, L0_tok_token_emb, L0_tok_instr_emb, L0_tok_arg_emb, L0_tok_gamma, L0_tok_beta)
    h = h + _L0_attn_ref(_layernorm(h, axis=-1), L0_attn_Wcq, L0_attn_q_norm_w, L0_attn_Wq_nope, L0_attn_Wq_rope, L0_attn_Wckv, L0_attn_kv_norm_w, L0_attn_Wk_nope, L0_attn_Wv, L0_attn_Wk_rope, L0_attn_W_imp, L0_attn_Wsel_k, L0_attn_Wsel_v, L0_attn_Wwin_k, L0_attn_Wwin_v, L0_attn_Wgate, L0_attn_Wproj)
    h = h + _L0_ffn_ref(_layernorm(h, axis=-1), L0_ffn_router_w, L0_ffn_w1, L0_ffn_b1, L0_ffn_w2, L0_ffn_b2)
    return h

_drawn_inputs = setup_inputs


def setup_inputs(seed=0):
    import zlib

    import numpy as np

    out = dict(_drawn_inputs(seed))
    spreads = {'L0_tok_gamma': (1.0, 0.2),
     'L0_tok_beta': (0.0, 0.1),
     'L0_attn_q_norm_w': (1.0, 0.6),
     'L0_attn_kv_norm_w': (1.0, 0.6),
     'L0_ffn_b1': (0.0, 0.326),
     'L0_ffn_b2': (0.0, 0.1)}
    factors = {'L0_attn_Wcq': 8.0,
     'L0_attn_Wq_nope': 8.0,
     'L0_attn_Wq_rope': 8.0,
     'L0_attn_Wckv': 4.391,
     'L0_attn_Wk_nope': 8.0,
     'L0_attn_Wv': 4.765,
     'L0_attn_Wk_rope': 64.0,
     'L0_attn_W_imp': 5.081,
     'L0_attn_Wsel_k': 8.0,
     'L0_attn_Wsel_v': 3.382,
     'L0_attn_Wwin_k': 8.0,
     'L0_attn_Wwin_v': 2.913,
     'L0_attn_Wgate': 8.0}
    for name, (base, spread) in spreads.items():
        noise = np.random.default_rng([zlib.crc32(name.encode()), seed]).standard_normal(out[name].shape)
        drawn = base * np.exp(spread * noise) if base else spread * noise
        out[name] = jnp.asarray(drawn.astype(out[name].dtype))
    for name, factor in factors.items():
        out[name] = (out[name] * factor).astype(out[name].dtype)
    return out
```

```python
import concourse.bass as bass
from concourse import mybir
from contextlib import ExitStack

B, T, C = 8, 512, 64
P = 128
NT = T // P
TILES = B * NT
NH, NOPE, ROPE, VD = 16, 32, 64, 32
HD = NOPE + ROPE
CQ, CKV = 96, 32
KEEP = 128
QW = NOPE + ROPE + NOPE
LAT = CQ + CKV + ROPE
LATP = LAT + NOPE
NE = 8
NEXT_ID = 5
NEG = -3.0e38

K_ID, K_MASK, K_COS, K_SIN, K_IOTA, K_TRI, K_END = 0, 128, 384, 704, 1024, 1152, 1216

ARGS = ["x", "L0_tok_token_emb", "L0_tok_instr_emb", "L0_tok_arg_emb", "L0_tok_gamma", "L0_tok_beta",
        "L0_attn_Wcq", "L0_attn_q_norm_w", "L0_attn_Wq_nope", "L0_attn_Wq_rope", "L0_attn_Wckv",
        "L0_attn_kv_norm_w", "L0_attn_Wk_nope", "L0_attn_Wv", "L0_attn_Wk_rope", "L0_attn_W_imp",
        "L0_attn_Wsel_k", "L0_attn_Wsel_v", "L0_attn_Wwin_k", "L0_attn_Wwin_v", "L0_attn_Wgate",
        "L0_attn_Wproj", "L0_ffn_router_w", "L0_ffn_w1", "L0_ffn_b1", "L0_ffn_w2", "L0_ffn_b2"]


def tower(nc, d, out):
    fp32, bf16, i32 = mybir.dt.float32, mybir.dt.bfloat16, mybir.dt.int32
    ALU, ACT, AX = mybir.AluOpType, mybir.ActivationFunctionType, mybir.AxisListType
    ds = bass.ds
    ctx = ExitStack()
    with ctx:
        def sb(name, shape, dt=fp32):
            return ctx.enter_context(nc.sbuf_tensor(name, shape, dt))

        def ps(name, shape):
            return ctx.enter_context(nc.psum_tensor(name, shape, fp32))

        def sem(name):
            return ctx.enter_context(nc.semaphore(name))

        cst = sb("cst", [P, K_END])
        ident = cst[:, K_ID:K_ID + P]
        cos5 = cst[:, K_COS:K_COS + 5 * ROPE].rearrange("p (t r) -> p t r", t=5)
        sin5 = cst[:, K_SIN:K_SIN + 5 * ROPE].rearrange("p (t r) -> p t r", t=5)
        iota_row = cst[:, K_IOTA:K_IOTA + P]
        tri = cst[:, K_TRI:K_TRI + NE * NE].rearrange("p (a b) -> p a b", a=NE)
        identb = sb("identb", [P, P], bf16)
        maskb = sb("maskb", [P, 2 * P], bf16)
        ones = sb("ones", [P, P])
        gamma_b = sb("gamma_b", [P, C])
        beta_b = sb("beta_b", [P, C])
        wlat = sb("wlat", [C, LAT + 3])
        wimp = sb("wimp", [C, 2 * B - 1])
        wq = sb("wq", [CQ, NH, QW])
        qw_col = sb("qw_col", [CQ, 1])
        kvw_col = sb("kvw_col", [CKV, 1])
        wqn_raw = sb("wqn_raw", [CQ, NH * NOPE])
        wkn = sb("wkn", [CKV, NH * NOPE])
        wqnT = sb("wqnT", [P, 4, CQ])
        wknBD = sb("wknBD", [P, 4, P])
        wv = sb("wv", [CKV, NH * VD])
        wkw = sb("wkw", [C, NH, HD])
        wks = sb("wks", [C, NH, HD])
        wvw = sb("wvw", [C, NH * VD])
        wvs = sb("wvs", [C, NH * VD])
        wproj = sb("wproj", [P, 4, C])
        rwT = sb("rwT", [C, NE])
        w1 = sb("w1", [C, NE, C])
        w2 = sb("w2", [P, NE // 2, C])
        b1 = sb("b1", [P, NE // 2])
        b2 = sb("b2", [NE, C])
        pairsel = sb("pairsel", [NE, NE // 2, P])

        h_all = sb("h_all", [P, TILES * C])
        xn_all = sb("xn_all", [P, TILES * C])
        xnT_all = sb("xnT_all", [C, B * T])
        lat_all = sb("lat_all", [P, TILES, LATP])
        gl_all = sb("gl_all", [P, TILES, 3])
        gate_all = sb("gate_all", [P, B, 3])
        rankT = sb("rankT", [P, B, NT])
        cT_all = lat_all[0:NE].rearrange("p n c -> p (n c)")[:, 0:B * T]
        big = sb("big", [P, 3, TILES * C])
        cur = big[:, 0, :]
        scr = big[:, 1:3, :].rearrange("p a n -> p (a n)")
        st = sb("st", [P, 6, 2 * TILES])

        vall = sb("vall", [P, 9, NH * VD])
        o_b = sb("o_b", [P, NT, NH * VD])
        oT = sb("oT", [P, 4, T])
        xi = vall[0:B, 0, :].bitcast(i32)
        xf, starts, instr, segst, lastst, argsf, onesr, pos = (vall[0:B, i, :] for i in range(1, 9))
        sc0, sc1, selm, rank = (o_b[0:B, i, :] for i in range(4))
        rankm = oT[0:B, 0, :]
        top8 = oT[0:B, 1, 0:KEEP]
        idx = sb("idx", [P, 3, NT, B], i32)

        lat_b = sb("lat_b", [P, NT, LATP])
        xn_b = sb("xn_b", [P, NT, C])
        xnT_b = sb("xnT_b", [C, T])
        rank_b = sb("rank_b", [P, NT])
        gate_b = sb("gate_b", [P, 3])
        onehot = sb("onehot", [P, NT, KEEP])
        cqT = sb("cqT", [CQ, T])
        k1T = sb("k1T", [P, T])
        selxT = sb("selxT", [C, KEEP])

        qs = [sb(f"qs{i}", [P, NT, QW]) for i in range(2)]
        kk = [sb(f"kk{i}", [P, 5, P]) for i in range(2)]
        work = big[:].rearrange("p a n -> p (a n)")
        NPR, NRT, NOB = 7 * P, 2 * 5 * ROPE, NT * 3 * VD
        pr = [work[:, i * NPR:(i + 1) * NPR] for i in range(2)]
        pT = [work[:, (2 + i) * NPR:(3 + i) * NPR].rearrange("p (a q) -> p a q", a=7) for i in range(2)]
        rt = [work[:, 4 * NPR + i * NRT:4 * NPR + (i + 1) * NRT].rearrange("p (a t r) -> p a t r", a=2, t=5)
              for i in range(2)]
        obr = [work[:, 4 * NPR + 2 * NRT + i * NOB:4 * NPR + 2 * NRT + (i + 1) * NOB].rearrange("p (t k d) -> p t k d", t=NT, k=3)
               for i in range(2)]
        qT = [sb(f"qT{i}", [P, T]) for i in range(2)]
        kwT = [sb(f"kwT{i}", [P, T]) for i in range(2)]
        ksT = [sb(f"ksT{i}", [P, KEEP]) for i in range(2)]
        negm = [sb(f"negm{i}", [P, 3]) for i in range(2)]
        sums = [sb(f"sums{i}", [P, NT, 3]) for i in range(2)]
        rinv = sb("rinv", [P, NT, 3])
        coef = sb("coef", [P, NT, 3])
        osum = sb("osum", [P, NT, VD])

        hT = [vall[:, i, :] for i in range(4)]
        hs = [vall[:, 4 + i, :] for i in range(4)]
        cTb = vall[0:NE, 8, :]
        y1 = o_b[:, 0, 0:NT * C]
        y2 = [o_b[:, 1 + i, 0:NT * C] for i in range(2)]

        S = [ps(f"S{i}", [P, 1024]) for i in range(2)]
        PT = ps("PT", [P, 1024])
        O = ps("O", [P, 512])
        X = ps("X", [P, 512])

        s = {n: sem(n) for n in [
            "ld_x", "ld_cst", "ld_w", "ld_wimp", "ld_emb", "gathered", "kconst",
            "dve_chain", "pool_chain", "act_chain", "pe_chain",
            "pos_ready", "posT", "idx_ready", "emb_summed", "var_ready", "std_ready", "xn_ready",
            "xnT_psum", "xnT_sb", "lat_psum", "lat_sb", "imp_psum", "rank_ready", "rank_psum", "rank_sb",
            "gsum_psum", "gexp_in", "gexp_out", "wq_scaled", "wT_psum", "wT_sb", "wabs_psum", "wabs_sb",
            "phaseA",
            "b_loaded", "onehot_ready", "cqk_psum", "cq_sb", "k1_sb", "selx_psum", "selx_sb",
            "v_psum", "v_act", "v_dve",
            "scores_ready", "max_ready", "probs_ready", "pT_psum", "pT_sb", "pv_done", "comb_done",
            "coef_chain", "osum_part", "osum_done",
            "x_ready", "x_evac", "rope_tmp", "rope_q", "rope_k",
            "oT_psum", "oT_act", "oT_dve", "attn_psum", "h_done",
            "t2_psum", "t2_sb", "rl_psum", "rexp_in", "rexp_out", "comb_ready", "cT_psum", "cT_sb",
            "ffn_h", "ffn_gelu", "ffn_cb", "ffn_hs", "ffn_cTb", "ffn_y", "ffn_out1", "ffn_out", "stored0", "stored1"]}
        block = ctx.enter_context(nc.Block())

        class Chain:

            def __init__(self, eng, name):
                self.eng, self.sem, self.n = eng, s[name], 0

            def link(self, ins):
                ins.then_inc(self.sem, 1)
                self.n += 1
                self.eng.wait_ge(self.sem, self.n)

        VBANK = [S[1][:, 512:1024], PT[:, 0:512], PT[:, 512:1024], O[:, 0:512]]
        TBANK = [X[0:C, :], S[0][0:C, 0:512]]
        XPRE = ["qp0", "kp0", "qT0", "kT0", "sT0", "qp1", "kp1"]

        def x_index(p, kind):
            return 7 + 5 * p + ["qT", "kT", "sT", "qp", "kp"].index(kind)

        def kblocks(t):
            return (t + 1) * P, KEEP, (P if t == 0 else 2 * P)

        @block.sync
        def _(sp):
            def ld(dst, src, name):
                sp.dma_start(dst, src).then_inc(s[name], 16)

            ld(xi[:], d["x"], "ld_x")
            ld(pos[:], d["c_pos"], "ld_x")
            ld(cst[:], d["c_cst"], "ld_cst")
            w = "ld_w"
            ld(wqn_raw[:], d["L0_attn_Wq_nope"], w)
            ld(wkn[:], d["L0_attn_Wk_nope"], w)
            ld(qw_col[:], d["L0_attn_q_norm_w"].rearrange("(p o) -> p o", o=1), w)
            ld(kvw_col[:], d["L0_attn_kv_norm_w"].rearrange("(p o) -> p o", o=1), w)
            ld(gamma_b[:], d["L0_tok_gamma"].partition_broadcast(P), w)
            ld(beta_b[:], d["L0_tok_beta"].partition_broadcast(P), w)
            ld(wlat[:, 0:CQ], d["L0_attn_Wcq"], w)
            ld(wlat[:, CQ:CQ + CKV], d["L0_attn_Wckv"], w)
            ld(wlat[:, CQ + CKV:LAT], d["L0_attn_Wk_rope"], w)
            ld(wlat[:, LAT:LAT + 3], d["L0_attn_Wgate"], w)
            ld(wq[:, :, NOPE:HD], d["L0_attn_Wq_rope"].rearrange("c (h r) -> c h r", h=NH), w)
            ld(wq[:, :, HD:QW], d["L0_attn_Wq_nope"].rearrange("c (h r) -> c h r", h=NH), w)
            ld(wv[:], d["L0_attn_Wv"], w)
            for dst, name in ((wkw, "L0_attn_Wwin_k"), (wks, "L0_attn_Wsel_k")):
                src = d[name].rearrange("c (h r) -> c h r", h=NH)
                ld(dst[:, :, 0:ROPE], src[:, :, NOPE:HD], w)
                ld(dst[:, :, ROPE:HD], src[:, :, 0:NOPE], w)
            ld(wvw[:], d["L0_attn_Wwin_v"], w)
            ld(wvs[:], d["L0_attn_Wsel_v"], w)
            ld(wproj[:], d["L0_attn_Wproj"].rearrange("(c p) n -> p c n", p=P), w)
            ld(rwT[:], d["c_rwT"], w)
            ld(w1[:], d["L0_ffn_w1"].rearrange("e i o -> i e o"), w)
            ld(w2[:], d["L0_ffn_w2"].rearrange("(c e) i o -> (e i) c o", e=2), w)
            ld(b1[:], d["c_b1T"], w)
            ld(b2[:], d["L0_ffn_b2"], w)
            ld(pairsel[:], d["c_pair"].rearrange("e (c m) -> e c m", c=NE // 2), w)
            sp.wait_ge(s["kconst"], 3)
            ld(wimp[:, B - 1:B], d["L0_attn_W_imp"], "ld_wimp")

            sp.wait_ge(s["phaseA"], 1)
            sp.wait_ge(s["xnT_sb"], B)
            with sp.Fori(0, B) as b:
                sp.wait_ge(s["h_done"], b + 1)
                sp.dma_start(lat_b[:], lat_all[:, ds(b * NT, NT), :]).then_inc(s["b_loaded"], 16)
                sp.dma_start(xn_b[:], xn_all[:, ds(b * NT * C, NT * C)].rearrange("p (t c) -> p t c", t=NT)).then_inc(s["b_loaded"], 16)
                sp.dma_start(xnT_b[:], xnT_all[:, ds(b * T, T)]).then_inc(s["b_loaded"], 16)
                sp.dma_start(rank_b[:], rankT[:, ds(b, 1), :].rearrange("p a t -> p (a t)")).then_inc(s["b_loaded"], 16)
                sp.dma_start(gate_b[:], gate_all[:, ds(b, 1), :].rearrange("p a t -> p (a t)")).then_inc(s["b_loaded"], 16)

            out_v = out.rearrange("b (t p) c -> b p t c", p=P)
            with sp.Fori(0, B // 2) as hb:
                for k in range(2):
                    sp.wait_ge(s["ffn_out"], hb * 2 + k + 1)
                    sp.dma_start(out_v[ds(hb * 2 + k, 1)].rearrange("a p t c -> (a p) t c"),
                                 y2[k][:].rearrange("p (t c) -> p t c", t=NT)).then_inc(s[f"stored{k}"], 16)
            for k in range(2):
                sp.wait_ge(s[f"stored{k}"], 16 * (B // 2) + 16)

        @block.gpsimd
        def _(g):
            ch = Chain(g, "pool_chain")
            g.memset(ones[:], 1.0).then_inc(s["kconst"], 1)
            g.memset(wknBD[:], 0.0).then_inc(s["kconst"], 1)
            g.memset(wimp[:], 0.0).then_inc(s["kconst"], 1)
            for i in range(2):
                g.memset(kk[i][:, :, 0:NOPE], 0.0).then_inc(s["kconst"], 1)
            g.memset(lat_all[:, :, LAT:LATP], 0.0).then_inc(s["kconst"], 1)
            g.sem_inc(s["osum_done"], 2)

            g.wait_ge(s["idx_ready"], 1)
            tables = [d["L0_tok_token_emb"], d["L0_tok_instr_emb"], d["L0_tok_arg_emb"]]
            for b in range(B):
                for t in range(NT):
                    for a in range(3):
                        r = (b * NT + t) * C
                        g.indirect_dma_start(
                            out=big[:, a, r:r + C], out_offset=None, in_=tables[a],
                            in_offset=bass.IndirectOffsetOnAxis(ap=idx[:, a, t, b:b + 1], axis=0),
                        ).then_inc(s["gathered"], 16)

            def rope(src, tmp, done, tiles, base_tmp, u):
                v = src[:, 0:tiles, NOPE:HD]
                g.tensor_tensor(tmp[:, 0, 0:tiles, :], v, cos5[:, 0:tiles, :], ALU.mult)
                g.tensor_tensor(tmp[:, 1, 0:tiles, :], v, sin5[:, 0:tiles, :], ALU.mult).then_inc(s["rope_tmp"], 1)
                g.wait_ge(s["rope_tmp"], base_tmp)
                hf = ROPE // 2
                g.tensor_tensor(src[:, 0:tiles, NOPE:NOPE + hf], tmp[:, 0, 0:tiles, 0:hf], tmp[:, 1, 0:tiles, hf:ROPE], ALU.subtract)
                g.tensor_tensor(src[:, 0:tiles, NOPE + hf:HD], tmp[:, 0, 0:tiles, hf:ROPE], tmp[:, 1, 0:tiles, 0:hf], ALU.add).then_inc(done, 1)

            def rope_head(par, b, hh, xq, xk):
                g.wait_ge(s["x_evac"], b * 80 + xq + 2)
                rope(qs[par], rt[0], s["rope_q"], NT, b * 32 + hh * 2 + 1, hh)
                g.wait_ge(s["x_evac"], b * 80 + xk + 2)
                rope(kk[par], rt[1], s["rope_k"], 5, b * 32 + hh * 2 + 2, hh)

            def branch_sum(par, b, hh):
                g.wait_ge(s["comb_done"], b * NH + hh + 2)
                g.wait_ge(s["osum_done"], b * NH + hh + 2)
                g.tensor_tensor(osum[:], obr[par][:, :, 0, :], obr[par][:, :, 1, :], ALU.add).then_inc(s["osum_part"], 1)
                g.wait_ge(s["osum_part"], b * NH + hh + 1)
                g.tensor_tensor(o_b[:, :, ds(hh * VD, VD)], osum[:], obr[par][:, :, 2, :], ALU.add).then_inc(s["osum_done"], 1)

            with g.Fori(0, B) as b:
                rope_head(0, b, 0, 0, 1)
                rope_head(1, b, 1, 5, 6)
                with g.Fori(0, NH // 2 - 1) as hp:
                    for par in range(2):
                        rope_head(par, b, hp * 2 + (par + 2), hp * 10 + x_index(par, "qp"), hp * 10 + x_index(par, "kp"))
                        branch_sum(par, b, hp * 2 + par)
                for par in range(2):
                    branch_sum(par, b, NH - 2 + par)

        @block.scalar
        def _(act):
            def copy(dst, src):
                return nc.scalar.activation(dst, src, ACT.Copy)

            act.sem_inc(s["x_evac"], 1)
            act.sem_inc(s["probs_ready"], 2)
            for k in range(2):
                act.wait_ge(s["var_ready"], k + 1)
                nc.scalar.activation(st[:, 1, 0:TILES], st[:, 0, 0:TILES], ACT.Sqrt).then_inc(s["std_ready"], 1)
            for b in range(B):
                act.wait_ge(s["xnT_psum"], b + 1)
                copy(xnT_all[:, b * T:(b + 1) * T], TBANK[b % 2]).then_inc(s["xnT_sb"], 1)
            act.wait_ge(s["var_ready"], 3)
            nc.scalar.activation(st[:, 1, :], st[:, 0, :], ACT.Sqrt).then_inc(s["std_ready"], 1)
            act.wait_ge(s["gexp_in"], 1)
            nc.scalar.activation(gate_all[:], gate_all[:], ACT.Exp).then_inc(s["gexp_out"], 1)

            def evac(dst, src, xi_, b):
                act.wait_ge(s["x_ready"], b * 80 + xi_ + 1)
                copy(dst, src).then_inc(s["x_evac"], 1)

            def evac_q(par, xi_, b):
                evac(qs[par][:], X[:, 0:512].rearrange("p (t q) -> p t q", t=NT), xi_, b)

            def evac_k(par, xi_, b):
                evac(kk[par][:, :, NOPE:P], X[:, 0:5 * HD].rearrange("p (t q) -> p t q", t=5), xi_, b)

            def probs(u, t, b, U):
                n1, n2, n3 = kblocks(t)
                par, hp2 = u % 2, (u // 4) % 2
                act.wait_ge(s["max_ready"], U + 1)
                act.wait_ge(s["pT_psum"], U + 1)
                for k, (lo, n) in enumerate(((0, n1), (4 * P, n2), (5 * P, n3))):
                    last = nc.scalar.activation(pr[par][:, lo:lo + n], S[par][:, lo:lo + n], ACT.Exp,
                                                bias=negm[par][:, k:k + 1], accum_out=sums[hp2][:, t, k:k + 1])
                last.then_inc(s["probs_ready"], 1)

            def turn(b, base, p, last):
                hb, ub, xb = base
                for t in range(NT):
                    u = p * NT + t
                    if t == 0 and last < 2:
                        evac(qT[1 - p][:], X[:, 0:T], xb + x_index(p, "qT"), b)
                    if t == 1 and last < 2:
                        evac(ksT[1 - p][:], X[:, 0:KEEP], xb + x_index(p, "sT"), b)
                    if t == 2 and last < 1:
                        evac_q(p, xb + x_index(p, "qp"), b)
                    if t == 3 and last < 1:
                        evac_k(p, xb + x_index(p, "kp"), b)
                    if last < 2 or t < 2:
                        probs(u + 2, (t + 2) % NT, b, ub + u + 2)
                    if t == 0 and last < 2:
                        evac(kwT[1 - p][:], X[:, 0:T], xb + x_index(p, "kT"), b)

            with act.Fori(0, B) as b:
                act.wait_ge(s["cqk_psum"], b * 2 + 1)
                copy(cqT[:], S[0][0:CQ, 0:512]).then_inc(s["cq_sb"], 1)
                act.wait_ge(s["cqk_psum"], b * 2 + 2)
                copy(k1T[:], S[0][:, 512:1024]).then_inc(s["k1_sb"], 1)
                act.wait_ge(s["selx_psum"], b + 1)
                copy(selxT[:], S[1][0:C, 0:KEEP]).then_inc(s["selx_sb"], 1)
                for i in range(0, 9, 2):
                    act.wait_ge(s["v_psum"], b * 9 + i + 1)
                    copy(vall[:, i, :], VBANK[i % 4]).then_inc(s["v_act"], 1)
                evac_q(0, 0, b)
                evac_k(0, 1, b)
                evac(qT[0][:], X[:, 0:T], 2, b)
                evac(kwT[0][:], X[:, 0:T], 3, b)
                evac(ksT[0][:], X[:, 0:KEEP], 4, b)
                evac_q(1, 5, b)
                evac_k(1, 6, b)
                ub = b * (NH * NT)
                probs(0, 0, b, ub)
                probs(1, 1, b, ub + 1)
                with act.Fori(0, NH // 2 - 1) as hp:
                    base = (hp * 2, b * (NH * NT) + hp * 8, hp * 10)
                    turn(b, base, 0, 0)
                    turn(b, base, 1, 0)
                base = (NH - 2, b * (NH * NT) + (NH - 2) * NT, (NH // 2 - 1) * 10)
                turn(b, base, 0, 1)
                turn(b, base, 1, 2)
                for c in range(0, 4, 2):
                    act.wait_ge(s["oT_psum"], b * 4 + c + 1)
                    copy(oT[:, c, :], S[c // 2][:, 0:512]).then_inc(s["oT_act"], 1)

            act.wait_ge(s["var_ready"], 4)
            nc.scalar.activation(st[:, 1, 0:TILES], st[:, 0, 0:TILES], ACT.Sqrt).then_inc(s["std_ready"], 1)
            for b in range(B):
                act.wait_ge(s["t2_psum"], b + 1)
                copy(xnT_all[:, b * T:(b + 1) * T], TBANK[b % 2]).then_inc(s["t2_sb"], 1)
            act.wait_ge(s["rexp_in"], 1)
            nc.scalar.activation(scr[:, 0:TILES * NE], scr[:, 0:TILES * NE], ACT.Exp).then_inc(s["rexp_out"], 1)
            for b in range(B):
                act.wait_ge(s["cT_psum"], b + 1)
                copy(cT_all[:, b * T:(b + 1) * T], [S[0], S[1]][b % 2][0:NE, 0:512]).then_inc(s["cT_sb"], 1)
            with act.Fori(0, B) as b:
                act.wait_ge(s["ffn_y"], b + 1)
                copy(cTb[:], cT_all[:, ds(b * T, T)]).then_inc(s["ffn_cTb"], 1)
                for c in range(4):
                    act.wait_ge(s["ffn_h"], b * 4 + c + 1)
                    act.wait_ge(s["ffn_hs"], b * 4 + c + 1)
                    nc.scalar.activation(hT[c][:], S[c // 2][:, (c % 2) * 512:(c % 2) * 512 + 512], ACT.Gelu,
                                         bias=b1[:, c:c + 1]).then_inc(s["ffn_gelu"], 1)

        @block.vector
        def _(dve):
            v = nc.vector
            ch = Chain(dve, "dve_chain")
            L = ch.link
            dve.sem_inc(s["comb_done"], 1)
            dve.sem_inc(s["pT_sb"], 1)
            dve.sem_inc(s["ffn_out1"], 1)
            dve.sem_inc(s["h_done"], 1)
            dve.sem_inc(s["ffn_hs"], 4)
            for k in range(2):
                dve.sem_inc(s[f"stored{k}"], 16)

            L(v.memset(onesr[:], 1.0))
            L(v.memset(starts[:, 0:1], 0.0))
            dve.wait_ge(s["ld_x"], 32)
            L(v.tensor_copy(xf[:], xi[:]))
            L(v.tensor_scalar(starts[:, 1:T], xf[:, 0:T - 1], float(NEXT_ID), None, ALU.is_equal))
            v.tensor_tensor_scan(instr[:], onesr[:], starts[:], 0.0, ALU.mult, ALU.add)
            L(v.tensor_tensor(segst[:], starts[:], pos[:], ALU.mult))
            L(v.tensor_tensor_scan(lastst[:], onesr[:], segst[:], 0.0, ALU.mult, ALU.max))
            v.tensor_tensor(argsf[:], pos[:], lastst[:], ALU.subtract).then_inc(s["pos_ready"], 1)
            dve.wait_ge(s["posT"], 1)
            v.tensor_copy(idx[:], X[:, 0:3 * NT * B].rearrange("p (a t b) -> p a t b", a=3, t=NT)).then_inc(s["idx_ready"], 1)

            dve.wait_ge(s["ld_cst"], 16)
            v.tensor_copy(identb[:], ident)
            L(v.tensor_copy(maskb[:], cst[:, K_MASK:K_MASK + 2 * P]))
            dve.wait_ge(s["ld_w"], 16 * N_W)
            sm = float(HD) ** -0.5
            L(v.tensor_scalar(qw_col[:], qw_col[:], sm, None, ALU.mult))
            v.tensor_scalar(wq[:, :, NOPE:QW], wq[:, :, NOPE:QW], qw_col[:], None, ALU.mult)
            v.tensor_scalar(wqn_raw[:], wqn_raw[:], qw_col[:], None, ALU.mult)
            v.tensor_scalar(wkn[:], wkn[:], kvw_col[:], None, ALU.mult)
            v.tensor_scalar(wv[:], wv[:], kvw_col[:], None, ALU.mult)
            v.tensor_scalar(wlat[:, CQ + CKV:LAT], wlat[:, CQ + CKV:LAT], 1.0 / NH, None, ALU.mult).then_inc(s["wq_scaled"], 1)
            dve.wait_ge(s["wT_psum"], 1)
            v.tensor_copy(wqnT[:], S[0][:, 0:4 * CQ].rearrange("p (c q) -> p c q", c=4))
            dve.wait_ge(s["kconst"], 6)
            for g_ in range(4):
                last = v.tensor_copy(wknBD[32 * g_:32 * g_ + 32, :, 32 * g_:32 * g_ + 32],
                                     S[0][32 * g_:32 * g_ + 32, 512:512 + 4 * CKV].rearrange("p (c q) -> p c q", c=4))
            last.then_inc(s["wT_sb"], 1)
            dve.wait_ge(s["wabs_psum"], 1)
            v.tensor_copy(wq[:, :, 0:NOPE], S[1][0:CQ, 0:512].rearrange("p (h q) -> p h q", h=NH)).then_inc(s["wabs_sb"], 1)

            def bc(ap, shape):
                return ap.to_broadcast(shape)

            def rsqrt(n, k):
                a, r, y, z = (st[:, i, 0:n] for i in (0, 1, 2, 3))
                dve.wait_ge(s["std_ready"], k)
                L(v.reciprocal(y, r))
                L(v.tensor_tensor(z, y, y, ALU.mult))
                L(v.tensor_tensor(z, z, a, ALU.mult))
                L(v.tensor_scalar(z, z, -0.5, 1.5, ALU.mult, ALU.add))
                L(v.tensor_tensor(y, y, z, ALU.mult))

            def layernorm(dst, src, k):
                s3, d3 = (x.rearrange("p (n c) -> p n c", c=C) for x in (src, dst))
                q3 = scr[:, 0:TILES * C].rearrange("p (n c) -> p n c", c=C)
                m = st[:, 4, 0:TILES]
                L(v.tensor_reduce(m, s3, op=ALU.add, axis=AX.X))
                L(v.tensor_scalar(m, m, 1.0 / C, None, ALU.mult))
                L(v.tensor_tensor(d3, s3, bc(m.unsqueeze(2), [P, TILES, C]), ALU.subtract))
                L(v.tensor_tensor(q3, d3, d3, ALU.mult))
                L(v.tensor_reduce(st[:, 0, 0:TILES], q3, op=ALU.add, axis=AX.X))
                ins = v.tensor_scalar(st[:, 0, 0:TILES], st[:, 0, 0:TILES], 1.0 / C, 1e-5, ALU.mult, ALU.add)
                ins.then_inc(s["var_ready"], 1)
                rsqrt(TILES, k)
                return v.tensor_tensor(d3, d3, bc(st[:, 2, 0:TILES].unsqueeze(2), [P, TILES, C]), ALU.mult)

            dve.wait_ge(s["gathered"], 16 * 3 * TILES)
            L(v.tensor_tensor(cur, cur, big[:, 1, :], ALU.add))
            L(v.tensor_tensor(cur, cur, big[:, 2, :], ALU.add))
            L(layernorm(h_all[:], cur, 1))
            h3 = h_all[:].rearrange("p (n c) -> p n c", c=C)
            L(v.tensor_tensor(h3, h3, bc(gamma_b[:].unsqueeze(1), [P, TILES, C]), ALU.mult))
            L(v.tensor_tensor(h3, h3, bc(beta_b[:].unsqueeze(1), [P, TILES, C]), ALU.add))
            layernorm(xn_all[:], h_all[:], 2).then_inc(s["xn_ready"], 1)

            for b in range(B):
                for k in range(2):
                    i = 2 * b + k
                    dve.wait_ge(s["lat_psum"], i + 1)
                    src = [S[1], PT][b % 2][:, 512 * k:512 * k + 2 * (LAT + 3)].rearrange("p (t c) -> p t c", t=2)
                    n = b * NT + 2 * k
                    v.tensor_copy(lat_all[:, n:n + 2, 0:LAT], src[:, :, 0:LAT])
                    last = v.tensor_copy(gl_all[:, n:n + 2, :], src[:, :, LAT:LAT + 3])
                    last.then_inc(s["lat_sb"], 1)

            dve.wait_ge(s["imp_psum"], 1)
            L(v.tensor_copy(sc0[:], O[0:B, :]))
            a, z = sc0, sc1
            for r in range(KEEP // 8):
                m8 = top8[:, 8 * r:8 * r + 8]
                L(v.max(m8, a[:]))
                L(v.match_replace(z[:], m8, a[:], NEG))
                a, z = z, a
            L(v.tensor_scalar(selm[:], a[:], NEG, None, ALU.is_equal))
            L(v.tensor_tensor_scan(rank[:], onesr[:], selm[:], 0.0, ALU.mult, ALU.add))
            L(v.tensor_tensor(rankm[:], rank[:], selm[:], ALU.mult))
            v.tensor_scalar(rankm[:], rankm[:], -1.0, None, ALU.add).then_inc(s["rank_ready"], 1)
            dve.wait_ge(s["rank_psum"], 1)
            L(v.tensor_copy(rankT[:], X[:, 0:NT * B].rearrange("p (t b) -> p b t", t=NT)))

            dve.wait_ge(s["gsum_psum"], 1)
            L(v.tensor_reduce(gate_all[:], O[:, 0:TILES * 3].rearrange("p (b t g) -> p b g t", b=B, t=NT), op=ALU.add, axis=AX.X))
            L(v.tensor_reduce(st[:, 4, 0:B], gate_all[:], op=ALU.max, axis=AX.X))
            L(v.tensor_tensor(gate_all[:], gate_all[:], bc(st[:, 4, 0:B].unsqueeze(2), [P, B, 3]), ALU.subtract))
            v.tensor_scalar(gate_all[:], gate_all[:], 1.0 / T, None, ALU.mult).then_inc(s["gexp_in"], 1)

            nc4 = TILES * P
            q3 = scr[:, 0:nc4].rearrange("p (n c) -> p n c", c=P)
            L(v.tensor_tensor(q3, lat_all[:, :, 0:P], lat_all[:, :, 0:P], ALU.mult))
            L(v.tensor_reduce(st[:, 5, 0:TILES], q3[:, :, 0:CQ], op=ALU.add, axis=AX.X))
            L(v.tensor_reduce(st[:, 5, TILES:2 * TILES], q3[:, :, CQ:P], op=ALU.add, axis=AX.X))
            v.tensor_scalar(st[:, 0, 0:TILES], st[:, 5, 0:TILES], 1.0 / CQ, 1e-6, ALU.mult, ALU.add)
            v.tensor_scalar(st[:, 0, TILES:], st[:, 5, TILES:], 1.0 / CKV, 1e-6, ALU.mult, ALU.add).then_inc(s["var_ready"], 1)
            kr = lat_all[:, :, CQ + CKV:LAT].rearrange("p (b t) r -> p b t r", b=B)
            krc = scr[:, 0:2048].rearrange("p (b t r) -> p b t r", b=B, t=NT)
            krs = scr[:, 2048:4096].rearrange("p (b t r) -> p b t r", b=B, t=NT)
            hf = ROPE // 2
            for b in range(B):
                v.tensor_tensor(krc[:, b], kr[:, b], cos5[:, 0:NT, :], ALU.mult)
                last = v.tensor_tensor(krs[:, b], kr[:, b], sin5[:, 0:NT, :], ALU.mult)
            L(last)
            for b in range(B):
                v.tensor_tensor(kr[:, b, :, 0:hf], krc[:, b, :, 0:hf], krs[:, b, :, hf:], ALU.subtract)
                last = v.tensor_tensor(kr[:, b, :, hf:], krc[:, b, :, hf:], krs[:, b, :, 0:hf], ALU.add)
            L(last)
            rsqrt(2 * TILES, 3)
            v.tensor_tensor(lat_all[:, :, 0:CQ], lat_all[:, :, 0:CQ], bc(st[:, 2, 0:TILES].unsqueeze(2), [P, TILES, CQ]), ALU.mult)
            v.tensor_tensor(lat_all[:, :, CQ:P], lat_all[:, :, CQ:P], bc(st[:, 2, TILES:].unsqueeze(2), [P, TILES, CKV]), ALU.mult)
            dve.wait_ge(s["gexp_out"], 1)
            L(v.tensor_reduce(st[:, 4, 0:B], gate_all[:], op=ALU.add, axis=AX.X))
            L(v.reciprocal(st[:, 5, 0:B], st[:, 4, 0:B]))
            v.tensor_tensor(gate_all[:], gate_all[:], bc(st[:, 5, 0:B].unsqueeze(2), [P, B, 3]), ALU.mult).then_inc(s["phaseA"], 1)

            def maxima(u, t, U):
                par = u % 2
                n1, n2, n3 = kblocks(t)
                dve.wait_ge(s["scores_ready"], U + 1)
                v.tensor_reduce(negm[par][:, 0:1], S[par][:, 0:n1], op=ALU.max, axis=AX.X, negate=True)
                v.tensor_reduce(negm[par][:, 1:2], S[par][:, 4 * P:4 * P + n2], op=ALU.max, axis=AX.X, negate=True)
                v.tensor_reduce(negm[par][:, 2:3], S[par][:, 5 * P:5 * P + n3], op=ALU.max, axis=AX.X, negate=True).then_inc(s["max_ready"], 1)

            def take_pT(u, t, U):
                par = u % 2
                n1, n2, n3 = kblocks(t)
                dve.wait_ge(s["pT_psum"], U + 3)
                dve.wait_ge(s["pv_done"], U + 1)
                dst = pT[par][:].rearrange("p a q -> p (a q)")
                v.tensor_copy(dst[:, 0:n1], PT[:, 0:n1])
                v.tensor_copy(dst[:, 4 * P:5 * P + n3], PT[:, 4 * P:5 * P + n3]).then_inc(s["pT_sb"], 1)

            def combine(par, b, H):
                dve.wait_ge(s["probs_ready"], H * NT + 6)
                v.reciprocal(rinv[:], sums[par][:]).then_inc(s["coef_chain"], 1)
                dve.wait_ge(s["coef_chain"], H * 2 + 1)
                v.tensor_tensor(coef[:], rinv[:], bc(gate_b[:].unsqueeze(1), [P, NT, 3]), ALU.mult).then_inc(s["coef_chain"], 1)
                dve.wait_ge(s["coef_chain"], H * 2 + 2)
                dve.wait_ge(s["osum_done"], H + 1)
                dve.wait_ge(s["pv_done"], H * NT + 6)
                v.tensor_tensor(obr[par][:].rearrange("p t k d -> p (t k) d"),
                                O[:, 0:NT * 3 * VD].rearrange("p (a d) -> p a d", d=VD),
                                bc(coef[:].rearrange("p t k -> p (t k)").unsqueeze(2), [P, NT * 3, VD]),
                                ALU.mult).then_inc(s["comb_done"], 1)

            def turn(b, H, p, last):
                U = H * NT
                for t in range(NT):
                    u = p * NT + t
                    if last < 2 or t < 2:
                        maxima(u + 2, (t + 2) % NT, U + t + 2)
                    if t == 3:
                        combine(p, b, H)
                    if last < 2 or t < 3:
                        take_pT(u + 1, (t + 1) % NT, U + t + 1)

            with dve.Fori(0, B) as b:
                dve.wait_ge(s["b_loaded"], b * 80 + 80)
                v.tensor_tensor(onehot[:], bc(iota_row.unsqueeze(1), [P, NT, KEEP]),
                                bc(rank_b[:].unsqueeze(2), [P, NT, KEEP]), ALU.is_equal).then_inc(s["onehot_ready"], 1)
                for i in range(1, 9, 2):
                    dve.wait_ge(s["v_psum"], b * 9 + i + 1)
                    v.tensor_copy(vall[:, i, :], VBANK[i % 4]).then_inc(s["v_dve"], 1)
                maxima(0, 0, b * (NH * NT))
                maxima(1, 1, b * (NH * NT) + 1)
                take_pT(0, 0, b * (NH * NT))
                with dve.Fori(0, NH // 2 - 1) as hp:
                    turn(b, b * NH + hp * 2, 0, 0)
                    turn(b, b * NH + hp * 2 + 1, 1, 0)
                turn(b, b * NH + (NH - 2), 0, 1)
                turn(b, b * NH + (NH - 1), 1, 2)
                for c in range(1, 4, 2):
                    dve.wait_ge(s["oT_psum"], b * 4 + c + 1)
                    v.tensor_copy(oT[:, c, :], S[c // 2][:, 512:1024]).then_inc(s["oT_dve"], 1)
                dve.wait_ge(s["attn_psum"], b + 1)
                hb = h_all[:, ds(b * (NT * C), NT * C)]
                v.tensor_tensor(hb, O[:, 0:NT * C], hb, ALU.add).then_inc(s["h_done"], 1)

            dve.wait_ge(s["h_done"], B + 1)
            layernorm(xn_all[:], h_all[:], 4).then_inc(s["xn_ready"], 1)
            n = TILES * NE
            e3 = scr[:, 0:n].rearrange("p (n e) -> p n e", e=NE)
            c3 = scr[:, n:2 * n].rearrange("p (n e) -> p n e", e=NE)
            big4 = big[:, 0, :].rearrange("p (n a e) -> p n a e", n=TILES, a=NE)
            eq4 = big[:, 2, :].rearrange("p (n a e) -> p n a e", n=TILES, a=NE)
            m = st[:, 4, 0:TILES]
            r3 = st[:, 5, 0:TILES]
            dve.wait_ge(s["rl_psum"], 1)
            l3 = X[:, 0:n].rearrange("p (n e) -> p n e", e=NE)
            L(v.tensor_reduce(m, l3, op=ALU.max, axis=AX.X))
            v.tensor_tensor(e3, l3, bc(m.unsqueeze(2), [P, TILES, NE]), ALU.subtract).then_inc(s["rexp_in"], 1)
            dve.wait_ge(s["rexp_out"], 1)
            L(v.tensor_reduce(m, e3, op=ALU.add, axis=AX.X))
            L(v.reciprocal(r3, m))
            L(v.tensor_tensor(e3, e3, bc(r3.unsqueeze(2), [P, TILES, NE]), ALU.mult))
            for a_ in range(NE):
                mine = bc(e3[:, :, a_:a_ + 1], [P, TILES, NE])
                v.tensor_tensor(big4[:, :, a_, :], e3, mine, ALU.is_gt)
                last = v.tensor_tensor(eq4[:, :, a_, :], e3, mine, ALU.is_equal)
            L(last)
            for a_ in range(NE):
                last = v.tensor_tensor(eq4[:, :, a_, :], eq4[:, :, a_, :], bc(tri[:, a_:a_ + 1, :], [P, TILES, NE]), ALU.mult)
            L(last)
            L(v.tensor_tensor(big[:, 0, :], big[:, 0, :], big[:, 2, :], ALU.add))
            L(v.tensor_reduce(c3, big4, op=ALU.add, axis=AX.X))
            L(v.tensor_scalar(c3, c3, 2.0, None, ALU.is_lt))
            L(v.tensor_tensor(c3, c3, e3, ALU.mult))
            L(v.tensor_reduce(m, c3, op=ALU.add, axis=AX.X))
            L(v.tensor_scalar(m, m, 1e-12, None, ALU.max))
            L(v.reciprocal(r3, m))
            v.tensor_tensor(c3, c3, bc(r3.unsqueeze(2), [P, TILES, NE]), ALU.mult).then_inc(s["comb_ready"], 1)

            with dve.Fori(0, B // 2) as hb:
                for k in range(2):
                    b = hb * 2 + k
                    for c in range(4):
                        dve.wait_ge(s["ffn_cb"], b * 4 + c + 1)
                        dve.wait_ge(s["ffn_gelu"], b * 4 + c + 1)
                        dve.wait_ge(s["ffn_y"], b + 1)
                        v.tensor_tensor(hs[c][:], hT[c][:], PT[:, (c % 2) * 512:(c % 2) * 512 + 512], ALU.mult).then_inc(s["ffn_hs"], 1)
                    dve.wait_ge(s["ffn_y"], b + 2)
                    v.tensor_tensor(y1[:], O[:, 0:NT * C], xn_all[:, ds(b * (NT * C), NT * C)], ALU.add).then_inc(s["ffn_out1"], 1)
                    dve.wait_ge(s["ffn_out1"], b + 2)
                    dve.wait_ge(s[f"stored{k}"], hb * 16 + 16)
                    v.tensor_tensor(y2[k][:], y1[:], h_all[:, ds(b * (NT * C), NT * C)], ALU.add).then_inc(s["ffn_out"], 1)

        @block.tensor
        def _(pe):
            mm, tp = nc.tensor.matmul, nc.tensor.transpose
            pe.sem_inc(s["pv_done"], 2)
            pe.sem_inc(s["pT_psum"], 2)
            pe.sem_inc(s["ffn_y"], 1)

            pe.wait_ge(s["ld_cst"], 16)
            pe.wait_ge(s["pos_ready"], 1)
            for a, src in enumerate((xf, instr, argsf)):
                for t in range(NT):
                    o = (a * NT + t) * B
                    last = tp(X[:, o:o + B], src[:, t * P:(t + 1) * P], cst[0:B, 0:B])
            last.then_inc(s["posT"], 1)

            pe.wait_ge(s["wq_scaled"], 1)
            for c in range(4):
                tp(S[0][:, c * CQ:(c + 1) * CQ], wqn_raw[:, c * P:(c + 1) * P], cst[0:CQ, 0:CQ])
            for c in range(4):
                last = tp(S[0][:, 512 + c * CKV:512 + (c + 1) * CKV], wkn[:, c * P:(c + 1) * P], cst[0:CKV, 0:CKV])
            last.then_inc(s["wT_psum"], 1)
            pe.wait_ge(s["wT_sb"], 1)
            for c in range(4):
                last = mm(S[1][0:CQ, c * P:(c + 1) * P], wqnT[:, c, :], wknBD[:, c, :], start=True, stop=True)
            last.then_inc(s["wabs_psum"], 1)
            pe.wait_ge(s["wabs_sb"], 1)

            def transposes(ready, name, sb_name):
                pe.wait_ge(s["xn_ready"], ready)
                for b in range(B):
                    if b >= 2:
                        pe.wait_ge(s[sb_name], b - 1)
                    for t in range(NT):
                        n_ = (b * NT + t) * C
                        last = tp(TBANK[b % 2][:, t * P:(t + 1) * P], xn_all[:, n_:n_ + C], ident)
                    last.then_inc(s[name], 1)

            pe.wait_ge(s["idx_ready"], 1)
            transposes(1, "xnT_psum", "xnT_sb")
            pe.wait_ge(s["ld_wimp"], 16)
            pe.wait_ge(s["xnT_sb"], B)
            for b in range(B):
                last = mm(O[0:B, :], wimp[:, B - 1 - b:2 * B - 1 - b], xnT_all[:, b * T:(b + 1) * T], start=(b == 0), stop=(b == B - 1))
            last.then_inc(s["imp_psum"], 1)
            for b in range(B):
                if b >= 2:
                    pe.wait_ge(s["lat_sb"], 2 * (b - 1))
                for t in range(NT):
                    n_ = (b * NT + t) * P
                    o = (t // 2) * 512 + (t % 2) * (LAT + 3)
                    last = mm([S[1], PT][b % 2][:, o:o + LAT + 3], xnT_all[:, n_:n_ + P], wlat[:], start=True, stop=True)
                    if t % 2:
                        last.then_inc(s["lat_psum"], 1)
            pe.wait_ge(s["rank_ready"], 1)
            for t in range(NT):
                last = tp(X[:, t * B:(t + 1) * B], rankm[:, t * P:(t + 1) * P], cst[0:B, 0:B])
            last.then_inc(s["rank_psum"], 1)
            pe.wait_ge(s["lat_sb"], 2 * B)
            mm(O[:, 0:TILES * 3], ones[:], gl_all[:].rearrange("p n g -> p (n g)"), start=True, stop=True).then_inc(s["gsum_psum"], 1)
            pe.wait_ge(s["phaseA"], 1)

            def x_wait(b, xi_):
                pe.wait_ge(s["x_evac"], b * 80 + xi_ + 1)

            def q_proj(b, h, xi_):
                x_wait(b, xi_)
                for t in range(NT):
                    last = mm(X[:, t * QW:(t + 1) * QW], cqT[:, t * P:(t + 1) * P],
                              wq[:].rearrange("c h q -> c (h q)")[:, ds(h * QW, QW)], start=True, stop=True)
                last.then_inc(s["x_ready"], 1)

            def k_proj(b, h, xi_):
                x_wait(b, xi_)
                pe.nop(nofuse=True)
                for t in range(NT):
                    mm(X[:, t * HD:(t + 1) * HD], xnT_b[:, t * P:(t + 1) * P],
                       wkw[:].rearrange("c h q -> c (h q)")[:, ds(h * HD, HD)], start=True, stop=True)
                mm(X[:, NT * HD:5 * HD], selxT[:], wks[:].rearrange("c h q -> c (h q)")[:, ds(h * HD, HD)],
                   start=True, stop=True).then_inc(s["x_ready"], 1)

            def q_turn(b, par, xi_, H):
                x_wait(b, xi_)
                pe.wait_ge(s["rope_q"], H + 1)
                for t in range(NT):
                    last = tp(X[:, t * P:(t + 1) * P], qs[par][:, t, :], ident)
                last.then_inc(s["x_ready"], 1)

            def k_turn(b, par, xi_, H):
                x_wait(b, xi_)
                pe.wait_ge(s["rope_k"], H + 1)
                for t in range(NT):
                    last = tp(X[:, t * P:(t + 1) * P], kk[par][:, t, :], ident)
                last.then_inc(s["x_ready"], 1)

            def s_turn(b, par, xi_):
                x_wait(b, xi_)
                tp(X[:, 0:P], kk[par][:, 4, :], ident).then_inc(s["x_ready"], 1)

            def scores(u, t, par, U):
                pe.wait_ge(s["probs_ready"], U + 1)
                z = S[u % 2]
                n1, n2, n3 = kblocks(t)
                q = qT[par][:, t * P:(t + 1) * P]
                mm(z[:, 0:n1], q, k1T[:, 0:n1], start=True, stop=True)
                mm(z[:, n1 - P:n1], identb[:], maskb[:, P:2 * P], start=False, stop=True, skip_group_check=True)
                mm(z[:, 4 * P:5 * P], q, ksT[par][:], start=True, stop=True)
                mm(z[:, 5 * P:5 * P + n3], q, kwT[par][:, (t + 1) * P - n3:(t + 1) * P], start=True, stop=True)
                mm(z[:, 5 * P:5 * P + n3], identb[:], maskb[:, 2 * P - n3:2 * P], start=False, stop=True, skip_group_check=True).then_inc(s["scores_ready"], 1)

            def turn_probs(u, t, U):
                pe.wait_ge(s["probs_ready"], U + 3)
                pe.wait_ge(s["pT_sb"], U + 1)
                n1, n2, n3 = kblocks(t)
                src = pr[u % 2]
                for lo in list(range(0, n1, P)) + list(range(4 * P, 5 * P + n3, P)):
                    last = tp(PT[:, lo:lo + P], src[:, lo:lo + P], ident)
                last.then_inc(s["pT_psum"], 1)

            def values(u, t, h, U, first):
                pe.wait_ge(s["pT_sb"], U + 2)
                if t == 0:
                    pe.wait_ge(s["comb_done"], first + 1)
                w = pT[u % 2]
                for k, (blocks, v0) in enumerate((([0, 1, 2, 3][:t + 1], 0), ([4], 8),
                                                  ([5] if t == 0 else [5, 6], 4 + max(t - 1, 0)))):
                    o = O[:, (t * 3 + k) * VD:(t * 3 + k + 1) * VD]
                    for i, blk in enumerate(blocks):
                        last = mm(o, w[:, blk, :], vall[:].rearrange("p n q -> p (n q)")[:, ds(h * VD + (v0 + i) * NH * VD, VD)],
                                  start=(i == 0), stop=(i == len(blocks) - 1))
                last.then_inc(s["pv_done"], 1)

            def turn(b, h, H, xb, p, last):
                U = H * NT
                for t in range(NT):
                    u = p * NT + t
                    values(u, t, h, U + t, H)
                    if last < 2 and t == 0:
                        q_turn(b, 1 - p, xb + x_index(p, "qT"), H + 1)
                    if last < 2 and t == 1:
                        s_turn(b, 1 - p, xb + x_index(p, "sT"))
                    if last < 1 and t == 2:
                        q_proj(b, h + 2, xb + x_index(p, "qp"))
                    if last < 1 and t == 3:
                        k_proj(b, h + 2, xb + x_index(p, "kp"))
                    if last < 2 or t < 2:
                        if t == 2:
                            pe.wait_ge(s["x_evac"], b * 80 + xb + x_index(p, "sT") + 2)
                        scores(u + 2, (t + 2) % NT, p if t < 2 else 1 - p, U + t + 2)
                    if last < 2 and t == 0:
                        k_turn(b, 1 - p, xb + x_index(p, "kT"), H + 1)
                    if last < 2 or t < 3:
                        turn_probs(u + 1, (t + 1) % NT, U + t + 1)

            with pe.Fori(0, B) as b:
                pe.wait_ge(s["b_loaded"], b * 80 + 80)
                for t in range(NT):
                    last = tp(S[0][0:CQ, t * P:(t + 1) * P], lat_b[:, t, 0:CQ], ident)
                last.then_inc(s["cqk_psum"], 1)
                for t in range(NT):
                    last = tp(S[0][:, 512 + t * P:512 + (t + 1) * P], lat_b[:, t, CQ:LATP], ident)
                last.then_inc(s["cqk_psum"], 1)
                pe.wait_ge(s["onehot_ready"], b + 1)
                for t in range(NT):
                    last = mm(S[1][0:C, 0:KEEP], xn_b[:, t, :], onehot[:, t, :], start=(t == 0), stop=(t == NT - 1))
                last.then_inc(s["selx_psum"], 1)
                for i in range(9):
                    if i == 0:
                        pe.wait_ge(s["k1_sb"], b + 1)
                    if i == 8:
                        pe.wait_ge(s["selx_sb"], b + 1)
                    if i >= 4 and i % 2 == 0:
                        pe.wait_ge(s["v_act"], b * 5 + (i - 4) // 2 + 1)
                    if i >= 4 and i % 2 == 1:
                        pe.wait_ge(s["v_dve"], b * 4 + (i - 5) // 2 + 1)
                    if i < 4:
                        lhs, rhs = k1T[0:CKV, i * P:(i + 1) * P], wv[:]
                    elif i < 8:
                        lhs, rhs = xnT_b[:, (i - 4) * P:(i - 3) * P], wvw[:]
                    else:
                        lhs, rhs = selxT[:], wvs[:]
                    mm(VBANK[i % 4], lhs, rhs, start=True, stop=True).then_inc(s["v_psum"], 1)
                pe.wait_ge(s["v_act"], b * 5 + 5)
                pe.wait_ge(s["v_dve"], b * 4 + 4)
                pe.wait_ge(s["cq_sb"], b + 1)
                q_proj(b, 0, 0)
                k_proj(b, 0, 1)
                q_turn(b, 0, 2, b * NH)
                k_turn(b, 0, 3, b * NH)
                s_turn(b, 0, 4)
                q_proj(b, 1, 5)
                k_proj(b, 1, 6)
                scores(0, 0, 0, b * (NH * NT))
                scores(1, 1, 0, b * (NH * NT) + 1)
                turn_probs(0, 0, b * (NH * NT))
                with pe.Fori(0, NH // 2 - 1) as hp:
                    turn(b, hp * 2, b * NH + hp * 2, hp * 10, 0, 0)
                    turn(b, hp * 2 + 1, b * NH + hp * 2 + 1, hp * 10, 1, 0)
                turn(b, NH - 2, b * NH + (NH - 2), (NH // 2 - 1) * 10, 0, 1)
                turn(b, NH - 1, b * NH + (NH - 1), (NH // 2 - 1) * 10, 1, 2)
                pe.wait_ge(s["osum_done"], b * NH + NH + 2)
                for c in range(4):
                    for t in range(NT):
                        last = tp(S[c // 2][:, (c % 2) * 512 + t * P:(c % 2) * 512 + (t + 1) * P], o_b[:, t, c * P:(c + 1) * P], ident)
                    last.then_inc(s["oT_psum"], 1)
                pe.wait_ge(s["comb_done"], b * NH + NH + 1)
                pe.wait_ge(s["oT_act"], b * 2 + 2)
                pe.wait_ge(s["oT_dve"], b * 2 + 2)
                for t in range(NT):
                    for c in range(4):
                        last = mm(O[:, t * C:(t + 1) * C], oT[:, c, t * P:(t + 1) * P], wproj[:, c, :], start=(c == 0), stop=(c == 3))
                last.then_inc(s["attn_psum"], 1)
                pe.wait_ge(s["h_done"], b + 2)

            pe.wait_ge(s["x_evac"], B * 80 + 1)
            transposes(2, "t2_psum", "t2_sb")
            pe.wait_ge(s["t2_sb"], B)
            for n_ in range(TILES):
                last = mm(X[:, n_ * NE:(n_ + 1) * NE], xnT_all[:, n_ * P:(n_ + 1) * P], rwT[:], start=True, stop=True)
            last.then_inc(s["rl_psum"], 1)
            pe.wait_ge(s["comb_ready"], 1)
            for b in range(B):
                if b >= 2:
                    pe.wait_ge(s["cT_sb"], b - 1)
                for t in range(NT):
                    n_ = (b * NT + t) * NE + TILES * NE
                    last = tp([S[0], S[1]][b % 2][0:NE, t * P:(t + 1) * P], scr[:, n_:n_ + NE], ident)
                last.then_inc(s["cT_psum"], 1)
            pe.wait_ge(s["cT_sb"], B)
            with pe.Fori(0, B) as b:
                for c in range(4):
                    pe.wait_ge(s["ffn_hs"], b * 4 + c + 1)
                    pe.nop(nofuse=True)
                    mm(S[c // 2][:, (c % 2) * 512:(c % 2) * 512 + 512], w1[:, 2 * c:2 * c + 2, :].rearrange("i e o -> i (e o)"),
                       xnT_all[:, ds(b * T, T)], start=True, stop=True).then_inc(s["ffn_h"], 1)
                for c in range(4):
                    pe.wait_ge(s["ffn_hs"], b * 4 + c + 3)
                    pe.nop(nofuse=True)
                    mm(PT[:, (c % 2) * 512:(c % 2) * 512 + 512], pairsel[:, c, :], cT_all[:, ds(b * T, T)],
                       start=True, stop=True).then_inc(s["ffn_cb"], 1)
                pe.wait_ge(s["ffn_hs"], b * 4 + 8)
                pe.wait_ge(s["ffn_cTb"], b + 1)
                pe.wait_ge(s["ffn_out1"], b + 1)
                for t in range(NT):
                    for c in range(4):
                        mm(O[:, t * C:(t + 1) * C], hs[c][:, t * P:(t + 1) * P], w2[:, c, :], start=(c == 0), stop=False)
                    last = mm(O[:, t * C:(t + 1) * C], cTb[:, t * P:(t + 1) * P], b2[:], start=False, stop=True)
                last.then_inc(s["ffn_y"], 1)


N_W = 26


def _constants():
    import numpy as np
    c = np.zeros((P, K_END), np.float32)
    c[:, K_ID:K_ID + P] = np.eye(P)
    q, k = np.arange(P)[:, None], np.arange(P)[None, :]
    c[:, K_MASK:K_MASK + P] = np.where(k > q, 0.0, -1e30)
    c[:, K_MASK + P:K_MASK + 2 * P] = np.where(k <= q, 0.0, -1e30)
    f = 1.0 / 10000.0 ** (np.arange(0, ROPE, 2, dtype=np.float32) / ROPE)
    ang = np.outer(np.arange(T, dtype=np.float32), f)
    for col, tab in ((K_COS, np.cos(ang)), (K_SIN, np.sin(ang))):
        for t in range(5):
            rows = tab[(t % NT) * P:(t % NT) * P + P]
            c[:, col + t * ROPE:col + (t + 1) * ROPE] = np.concatenate([rows, rows], 1)
    c[:, K_IOTA:K_IOTA + P] = np.arange(P)
    c[:, K_TRI:K_TRI + NE * NE] = (np.arange(NE)[None, :] < np.arange(NE)[:, None]).astype(np.float32).reshape(-1)
    pos = np.tile(np.arange(T, dtype=np.float32), (B, 1))
    pair = np.zeros((NE, NE // 2, 2, P // 2), np.float32)
    for e in range(NE):
        pair[e, e // 2, e % 2] = 1.0
    return {"c_cst": c, "c_pos": pos, "c_pair": pair.reshape(NE, -1)}


def kernel(**inputs):
    import numpy as _np
    import concourse.bacc as _bacc
    from concourse import mybir as _mybir
    from concourse.bass_utils import run_bass_kernel_spmd as _run

    nc = _bacc.Bacc("TRN2", target_bir_lowering=False, num_devices=1)
    arrays, aps = {}, {}
    given = {n: _np.ascontiguousarray(inputs[n]) for n in ARGS}
    given.update(_constants())
    given["c_rwT"] = _np.ascontiguousarray(given["L0_ffn_router_w"].T)
    given["c_b1T"] = _np.ascontiguousarray(given["L0_ffn_b1"].reshape(NE // 2, P).T)
    for name, a in given.items():
        arrays[f"in_{name}_dram"] = a
        aps[name] = nc.dram_tensor(f"in_{name}_dram", a.shape, _mybir.dt.from_np(a.dtype), kind="ExternalInput").ap()
    out = nc.dram_tensor("out_0_dram", (B, T, C), _mybir.dt.float32, kind="ExternalOutput").ap()
    tower(nc, aps, out)
    r = _run(nc, [arrays], core_ids=[0])
    return r.results[0]["out_0_dram"]
```

```python
import concourse.bass as bass
from concourse import mybir
from contextlib import ExitStack

B, T, C = 8, 512, 64
P = 128
NT = T // P
TILES = B * NT
NH, NOPE, ROPE, VD = 16, 32, 64, 32
HD = NOPE + ROPE
CQ, CKV = 96, 32
KEEP = 128
QW = NOPE + ROPE + NOPE
LAT = CQ + CKV + ROPE
LATP = LAT + NOPE
NE = 8
NEXT_ID = 5
NEG = -3.0e38

K_ID, K_MASK, K_COS, K_SIN, K_IOTA, K_TRI, K_END = 0, 128, 384, 704, 1024, 1152, 1216

ARGS = ["x", "L0_tok_token_emb", "L0_tok_instr_emb", "L0_tok_arg_emb", "L0_tok_gamma", "L0_tok_beta",
        "L0_attn_Wcq", "L0_attn_q_norm_w", "L0_attn_Wq_nope", "L0_attn_Wq_rope", "L0_attn_Wckv",
        "L0_attn_kv_norm_w", "L0_attn_Wk_nope", "L0_attn_Wv", "L0_attn_Wk_rope", "L0_attn_W_imp",
        "L0_attn_Wsel_k", "L0_attn_Wsel_v", "L0_attn_Wwin_k", "L0_attn_Wwin_v", "L0_attn_Wgate",
        "L0_attn_Wproj", "L0_ffn_router_w", "L0_ffn_w1", "L0_ffn_b1", "L0_ffn_w2", "L0_ffn_b2"]


def tower(nc, d, out):
    fp32, bf16, i32 = mybir.dt.float32, mybir.dt.bfloat16, mybir.dt.int32
    ALU, ACT, AX = mybir.AluOpType, mybir.ActivationFunctionType, mybir.AxisListType
    ds = bass.ds
    ctx = ExitStack()
    with ctx:
        def sb(name, shape, dt=fp32):
            return ctx.enter_context(nc.sbuf_tensor(name, shape, dt))

        def ps(name, shape):
            return ctx.enter_context(nc.psum_tensor(name, shape, fp32))

        def sem(name):
            return ctx.enter_context(nc.semaphore(name))

        cst = sb("cst", [P, K_END])
        ident = cst[:, K_ID:K_ID + P]
        cos5 = cst[:, K_COS:K_COS + 5 * ROPE].rearrange("p (t r) -> p t r", t=5)
        sin5 = cst[:, K_SIN:K_SIN + 5 * ROPE].rearrange("p (t r) -> p t r", t=5)
        iota_row = cst[:, K_IOTA:K_IOTA + P]
        tri = cst[:, K_TRI:K_TRI + NE * NE].rearrange("p (a b) -> p a b", a=NE)
        identb = sb("identb", [P, P], bf16)
        maskb = sb("maskb", [P, 2 * P], bf16)
        ones = sb("ones", [P, P])
        gamma_b = sb("gamma_b", [P, C])
        beta_b = sb("beta_b", [P, C])
        wlat = sb("wlat", [C, LAT + 3])
        wimp = sb("wimp", [C, 2 * B - 1])
        wq = sb("wq", [CQ, NH, QW])
        qw_col = sb("qw_col", [CQ, 1])
        kvw_col = sb("kvw_col", [CKV, 1])
        wqn_raw = sb("wqn_raw", [CQ, NH * NOPE])
        wkn = sb("wkn", [CKV, NH * NOPE])
        wqnT = sb("wqnT", [P, 4, CQ])
        wknBD = sb("wknBD", [P, 4, P])
        wv = sb("wv", [CKV, NH * VD])
        wkw = sb("wkw", [C, NH, HD])
        wks = sb("wks", [C, NH, HD])
        wvw = sb("wvw", [C, NH * VD])
        wvs = sb("wvs", [C, NH * VD])
        wproj = sb("wproj", [P, 4, C])
        rwT = sb("rwT", [C, NE])
        w1 = sb("w1", [C, NE, C])
        w2 = sb("w2", [P, NE // 2, C])
        b1 = sb("b1", [P, NE // 2])
        b2 = sb("b2", [NE, C])
        pairsel = sb("pairsel", [NE, NE // 2, P])

        h_all = sb("h_all", [P, TILES * C])
        xn_all = sb("xn_all", [P, TILES * C])
        xnT_all = sb("xnT_all", [C, B * T])
        lat_all = sb("lat_all", [P, TILES, LATP])
        gl_all = sb("gl_all", [P, TILES, 3])
        gate_all = sb("gate_all", [P, B, 3])
        rankT = sb("rankT", [P, B, NT])
        cT_all = lat_all[0:NE].rearrange("p n c -> p (n c)")[:, 0:B * T]
        big = sb("big", [P, 3, TILES * C])
        cur = big[:, 0, :]
        scr = big[:, 1:3, :].rearrange("p a n -> p (a n)")
        st = sb("st", [P, 6, 2 * TILES])

        vall = sb("vall", [P, 9, NH * VD])
        o_b = sb("o_b", [P, NT, NH * VD])
        oT = sb("oT", [P, 4, T])
        xi = vall[0:B, 0, :].bitcast(i32)
        xf, starts, instr, segst, lastst, argsf, onesr, pos = (vall[0:B, i, :] for i in range(1, 9))
        sc0, sc1, selm, rank = (o_b[0:B, i, :] for i in range(4))
        rankm = oT[0:B, 0, :]
        top8 = oT[0:B, 1, 0:KEEP]
        idx = sb("idx", [P, 3, NT, B], i32)

        lat_b = sb("lat_b", [P, NT, LATP])
        xn_b = sb("xn_b", [P, NT, C])
        xnT_b = sb("xnT_b", [C, T])
        rank_b = sb("rank_b", [P, NT])
        onehot = sb("onehot", [P, NT, KEEP])
        cqT = sb("cqT", [CQ, T])
        k1n = sb("k1n", [P, T])
        k1T = sb("k1T", [P, T])
        selxT = sb("selxT", [C, KEEP])

        qs = [sb(f"qs{i}", [P, NT, QW]) for i in range(2)]
        kk = [sb(f"kk{i}", [P, 5, P]) for i in range(2)]
        work = big[:].rearrange("p a n -> p (a n)")
        NPR, NRT, NOB = 7 * P, 2 * 5 * ROPE, NT * 3 * VD
        pr = [work[:, i * NPR:(i + 1) * NPR] for i in range(2)]
        pT = [work[:, (2 + i) * NPR:(3 + i) * NPR].rearrange("p (a q) -> p a q", a=7) for i in range(2)]
        rt = [work[:, 4 * NPR + i * NRT:4 * NPR + (i + 1) * NRT].rearrange("p (a t r) -> p a t r", a=2, t=5)
              for i in range(2)]
        obr = [work[:, 4 * NPR + 2 * NRT + i * NOB:4 * NPR + 2 * NRT + (i + 1) * NOB].rearrange("p (t k d) -> p t k d", t=NT, k=3)
               for i in range(2)]
        qT = [sb(f"qT{i}", [P, T]) for i in range(2)]
        kwT = [sb(f"kwT{i}", [P, T]) for i in range(2)]
        ksT = [sb(f"ksT{i}", [P, KEEP]) for i in range(2)]
        negm = [sb(f"negm{i}", [P, 3]) for i in range(2)]
        sums = [sb(f"sums{i}", [P, NT, 3]) for i in range(2)]
        rinv = sb("rinv", [P, NT, 3])
        coef = sb("coef", [P, NT, 3])
        osum = sb("osum", [P, NT, VD])

        hT = [vall[:, i, :] for i in range(4)]
        hs = [vall[:, 4 + i, :] for i in range(4)]
        cTb = vall[0:NE, 8, :]
        y1 = o_b[:, 0, 0:NT * C]
        y2 = [o_b[:, 1 + i, 0:NT * C] for i in range(2)]

        S = [ps(f"S{i}", [P, 1024]) for i in range(2)]
        PT = ps("PT", [P, 1024])
        O = ps("O", [P, 512])
        X = ps("X", [P, 512])

        s = {n: sem(n) for n in [
            "ld_x", "ld_cst", "ld_w", "ld_wimp", "ld_emb", "gathered", "kconst",
            "dve_chain", "pool_chain", "act_chain", "pe_chain",
            "pos_ready", "posT", "idx_ready", "emb_summed", "var_ready", "std_ready", "xn_ready",
            "xnT_psum", "xnT_sb", "lat_psum", "lat_sb", "imp_psum", "rank_ready", "rank_psum", "rank_sb",
            "gsum_psum", "gexp_in", "gexp_out", "wq_scaled", "wT_psum", "wT_sb", "wabs_psum", "wabs_sb",
            "phaseA",
            "ld_lat", "ld_xnT", "onehot_ready", "k1_moved",
            "v_psum", "v_act", "v_dve",
            "scores_ready", "max_ready", "probs_ready", "pT_psum", "pT_sb", "pv_done", "comb_done",
            "coef_chain", "osum_part", "osum_done",
            "x_ready", "x_evac", "rope_tmp", "rope_q", "rope_k",
            "oT_psum", "oT_act", "oT_dve", "attn_psum", "h_done",
            "t2_psum", "t2_sb", "rl_psum", "rexp_in", "rexp_out", "comb_ready", "cT_psum", "cT_sb",
            "ffn_h", "ffn_gelu", "ffn_cb", "ffn_hs", "ffn_cTb", "ffn_y", "ffn_out1", "ffn_out", "stored"]}
        block = ctx.enter_context(nc.Block())

        class Chain:

            def __init__(self, eng, name):
                self.eng, self.sem, self.n = eng, s[name], 0

            def link(self, ins):
                ins.then_inc(self.sem, 1)
                self.n += 1
                self.eng.wait_ge(self.sem, self.n)

        VBANK = [S[0][:, 0:512], S[0][:, 512:1024], S[1][:, 0:512], S[1][:, 512:1024]]
        TBANK = [X[0:C, :], S[0][0:C, 0:512]]
        LEAD = ["cq", "k1", "sel", "qp0", "kp0", "qp1", "kp1", "qT0", "kT0", "sT0"]
        NX = (NH - 2) * 5 + 3 + len(LEAD)

        def x_index(p, kind):
            return 5 * p + ["qT", "kT", "sT", "qp", "kp"].index(kind)

        def x_lead(kind):
            return LEAD.index(kind) - len(LEAD)

        def xbase(b):
            return b * NX + len(LEAD)

        def kblocks(t):
            return (t + 1) * P, KEEP, (P if t == 0 else 2 * P)

        @block.sync
        def _(sp):
            def ld(dst, src, name):
                sp.dma_start(dst, src).then_inc(s[name], 16)

            ld(xi[:], d["x"], "ld_x")
            ld(pos[:], d["c_pos"], "ld_x")
            ld(cst[:], d["c_cst"], "ld_cst")
            w = "ld_w"
            ld(wqn_raw[:], d["L0_attn_Wq_nope"], w)
            ld(wkn[:], d["L0_attn_Wk_nope"], w)
            ld(qw_col[:], d["L0_attn_q_norm_w"].rearrange("(p o) -> p o", o=1), w)
            ld(kvw_col[:], d["L0_attn_kv_norm_w"].rearrange("(p o) -> p o", o=1), w)
            ld(gamma_b[:], d["L0_tok_gamma"].partition_broadcast(P), w)
            ld(beta_b[:], d["L0_tok_beta"].partition_broadcast(P), w)
            ld(wlat[:, 0:CQ], d["L0_attn_Wcq"], w)
            ld(wlat[:, CQ:CQ + CKV], d["L0_attn_Wckv"], w)
            ld(wlat[:, CQ + CKV:LAT], d["L0_attn_Wk_rope"], w)
            ld(wlat[:, LAT:LAT + 3], d["L0_attn_Wgate"], w)
            ld(wq[:, :, NOPE:HD], d["L0_attn_Wq_rope"].rearrange("c (h r) -> c h r", h=NH), w)
            ld(wq[:, :, HD:QW], d["L0_attn_Wq_nope"].rearrange("c (h r) -> c h r", h=NH), w)
            ld(wv[:], d["L0_attn_Wv"], w)
            for dst, name in ((wkw, "L0_attn_Wwin_k"), (wks, "L0_attn_Wsel_k")):
                src = d[name].rearrange("c (h r) -> c h r", h=NH)
                ld(dst[:, :, 0:ROPE], src[:, :, NOPE:HD], w)
                ld(dst[:, :, ROPE:HD], src[:, :, 0:NOPE], w)
            ld(wvw[:], d["L0_attn_Wwin_v"], w)
            ld(wvs[:], d["L0_attn_Wsel_v"], w)
            ld(wproj[:], d["L0_attn_Wproj"].rearrange("(c p) n -> p c n", p=P), w)
            ld(rwT[:], d["c_rwT"], w)
            ld(w1[:], d["L0_ffn_w1"].rearrange("e i o -> i e o"), w)
            ld(w2[:], d["L0_ffn_w2"].rearrange("(c e) i o -> (e i) c o", e=2), w)
            ld(b1[:], d["c_b1T"], w)
            ld(b2[:], d["L0_ffn_b2"], w)
            ld(pairsel[:], d["c_pair"].rearrange("e (c m) -> e c m", c=NE // 2), w)
            sp.wait_ge(s["kconst"], 3)
            ld(wimp[:, B - 1:B], d["L0_attn_W_imp"], "ld_wimp")

            sp.wait_ge(s["phaseA"], 1)
            sp.wait_ge(s["xnT_sb"], B)

            def load_latents(b):
                sp.dma_start(lat_b[:], lat_all[:, ds(b * NT, NT), :]).then_inc(s["ld_lat"], 16)
                sp.dma_start(xn_b[:], xn_all[:, ds(b * NT * C, NT * C)].rearrange("p (t c) -> p t c", t=NT)).then_inc(s["ld_lat"], 16)
                sp.dma_start(rank_b[:], rankT[:, ds(b, 1), :].rearrange("p a t -> p (a t)")).then_inc(s["ld_lat"], 16)

            def load_rows(b):
                sp.dma_start(xnT_b[:], xnT_all[:, ds(b * T, T)]).then_inc(s["ld_xnT"], 16)

            load_latents(0)
            load_rows(0)
            with sp.Fori(0, B - 1) as b:
                sp.wait_ge(s["x_ready"], xbase(b) + x_lead("sel") + 1)
                load_latents(b + 1)
                sp.wait_ge(s["x_ready"], xbase(b) + x_index(NH - 3, "kp") + 1)
                load_rows(b + 1)

            out_v = out.rearrange("b (t p) c -> b p t c", p=P)
            with sp.Fori(0, B) as b:
                sp.wait_ge(s["ffn_out"], b + 1)
                sp.dma_start(out_v[ds(b, 1)].rearrange("a p t c -> (a p) t c"),
                             h_all[:, ds(b * NT * C, NT * C)].rearrange("p (t c) -> p t c", t=NT)).then_inc(s["stored"], 16)
            sp.wait_ge(s["stored"], 16 * B)

        @block.gpsimd
        def _(g):
            ch = Chain(g, "pool_chain")
            g.memset(ones[:], 1.0).then_inc(s["kconst"], 1)
            g.memset(wknBD[:], 0.0).then_inc(s["kconst"], 1)
            g.memset(wimp[:], 0.0).then_inc(s["kconst"], 1)
            for i in range(2):
                g.memset(kk[i][:, :, 0:NOPE], 0.0).then_inc(s["kconst"], 1)
            g.memset(lat_all[:, :, LAT:LATP], 0.0).then_inc(s["kconst"], 1)
            g.sem_inc(s["osum_done"], 2)

            g.wait_ge(s["idx_ready"], 1)
            tables = [d["L0_tok_token_emb"], d["L0_tok_instr_emb"], d["L0_tok_arg_emb"]]
            for b in range(B):
                for t in range(NT):
                    for a in range(3):
                        r = (b * NT + t) * C
                        g.indirect_dma_start(
                            out=big[:, a, r:r + C], out_offset=None, in_=tables[a],
                            in_offset=bass.IndirectOffsetOnAxis(ap=idx[:, a, t, b:b + 1], axis=0),
                        ).then_inc(s["gathered"], 16)

            def rope(src, tmp, done, tiles, base_tmp):
                v = src[:, 0:tiles, NOPE:HD]
                g.tensor_tensor(tmp[:, 0, 0:tiles, :], v, cos5[:, 0:tiles, :], ALU.mult)
                g.tensor_tensor(tmp[:, 1, 0:tiles, :], v, sin5[:, 0:tiles, :], ALU.mult).then_inc(s["rope_tmp"], 1)
                g.wait_ge(s["rope_tmp"], base_tmp)
                hf = ROPE // 2
                g.tensor_tensor(src[:, 0:tiles, NOPE:NOPE + hf], tmp[:, 0, 0:tiles, 0:hf], tmp[:, 1, 0:tiles, hf:ROPE], ALU.subtract)
                g.tensor_tensor(src[:, 0:tiles, NOPE + hf:HD], tmp[:, 0, 0:tiles, hf:ROPE], tmp[:, 1, 0:tiles, 0:hf], ALU.add).then_inc(done, 1)

            def rope_q(par, b, hh, x):
                g.wait_ge(s["x_evac"], x + 2)
                rope(qs[par], rt[0], s["rope_q"], NT, b * (2 * NH) + hh * 2 + 1)

            def rope_k(par, b, hh, x):
                g.wait_ge(s["x_evac"], x + 2)
                rope(kk[par], rt[1], s["rope_k"], 5, b * (2 * NH) + hh * 2 + 2)

            def branch_sum(par, b, hh):
                g.wait_ge(s["comb_done"], b * NH + hh + 2)
                g.wait_ge(s["osum_done"], b * NH + hh + 2)
                g.tensor_tensor(osum[:], obr[par][:, :, 0, :], obr[par][:, :, 1, :], ALU.add).then_inc(s["osum_part"], 1)
                g.wait_ge(s["osum_part"], b * NH + hh + 1)
                g.tensor_tensor(o_b[:, :, ds(hh * VD, VD)], osum[:], obr[par][:, :, 2, :], ALU.add).then_inc(s["osum_done"], 1)

            rope_q(0, 0, 0, xbase(0) + x_lead("qp0"))
            rope_k(0, 0, 0, xbase(0) + x_lead("kp0"))
            rope_q(1, 0, 1, xbase(0) + x_lead("qp1"))
            rope_k(1, 0, 1, xbase(0) + x_lead("kp1"))

            def heads(b):
                with g.Fori(0, NH // 2 - 1) as hp:
                    for par in range(2):
                        rope_q(par, b, hp * 2 + (par + 2), xbase(b) + hp * 10 + x_index(par, "qp"))
                        rope_k(par, b, hp * 2 + (par + 2), xbase(b) + hp * 10 + x_index(par, "kp"))
                        branch_sum(par, b, hp * 2 + par)

            with g.Fori(0, B - 1) as b:
                heads(b)
                branch_sum(0, b, NH - 2)
                rope_q(0, b + 1, 0, xbase(b + 1) + x_lead("qp0"))
                rope_k(0, b + 1, 0, xbase(b + 1) + x_lead("kp0"))
                rope_q(1, b + 1, 1, xbase(b + 1) + x_lead("qp1"))
                branch_sum(1, b, NH - 1)
                rope_k(1, b + 1, 1, xbase(b + 1) + x_lead("kp1"))
            heads(B - 1)
            branch_sum(0, B - 1, NH - 2)
            branch_sum(1, B - 1, NH - 1)

        @block.scalar
        def _(act):
            def copy(dst, src):
                return nc.scalar.activation(dst, src, ACT.Copy)

            act.sem_inc(s["x_evac"], 1)
            act.sem_inc(s["probs_ready"], 2)
            for k in range(2):
                act.wait_ge(s["var_ready"], k + 1)
                nc.scalar.activation(st[:, 1, 0:TILES], st[:, 0, 0:TILES], ACT.Sqrt).then_inc(s["std_ready"], 1)
            for b in range(B):
                act.wait_ge(s["xnT_psum"], b + 1)
                copy(xnT_all[:, b * T:(b + 1) * T], TBANK[b % 2]).then_inc(s["xnT_sb"], 1)
            act.wait_ge(s["var_ready"], 3)
            nc.scalar.activation(st[:, 1, :], st[:, 0, :], ACT.Sqrt).then_inc(s["std_ready"], 1)
            act.wait_ge(s["gexp_in"], 1)
            nc.scalar.activation(gate_all[:], gate_all[:], ACT.Exp).then_inc(s["gexp_out"], 1)

            def evac(dst, src, x):
                act.wait_ge(s["x_ready"], x + 1)
                copy(dst, src).then_inc(s["x_evac"], 1)

            def evac_q(par, x):
                evac(qs[par][:], X[:, 0:512].rearrange("p (t q) -> p t q", t=NT), x)

            def evac_k(par, x):
                evac(kk[par][:, :, NOPE:P], X[:, 0:5 * HD].rearrange("p (t q) -> p t q", t=5), x)

            def probs(u, t, b, U):
                n1, n2, n3 = kblocks(t)
                par, hp2 = u % 2, (u // 4) % 2
                act.wait_ge(s["max_ready"], U + 1)
                act.wait_ge(s["pT_psum"], U + 1)
                for k, (lo, n) in enumerate(((0, n1), (4 * P, n2), (5 * P, n3))):
                    last = nc.scalar.activation(pr[par][:, lo:lo + n], S[par][:, lo:lo + n], ACT.Exp,
                                                bias=negm[par][:, k:k + 1], accum_out=sums[hp2][:, t, k:k + 1])
                last.then_inc(s["probs_ready"], 1)

            def turn(b, U, xb, p, last, nxt=None):
                for t in range(NT):
                    u = p * NT + t
                    if t == 0 and last < 2:
                        evac(qT[1 - p][:], X[:, 0:T], xb + x_index(0, "qT"))
                        evac(kwT[1 - p][:], X[:, 0:T], xb + x_index(0, "kT"))
                    if t == 1 and last < 2:
                        evac(ksT[1 - p][:], X[:, 0:KEEP], xb + x_index(0, "sT"))
                    if t == 2 and last < 1:
                        evac_q(p, xb + x_index(0, "qp"))
                    if t == 3 and last < 1:
                        evac_k(p, xb + x_index(0, "kp"))
                    if nxt is not None and last in (1, 2):
                        lead(["cq", "k1", "sel", "qp0", "kp0", "qp1"], (t - 2 if last == 1 else t + 2), nxt)
                    if last < 2 or t < 2:
                        probs(u + 2, (t + 2) % NT, b, U + t + 2)

            def lead(kinds, i, nxt):
                if not 0 <= i < len(kinds):
                    return
                kind = kinds[i]
                x = nxt + LEAD.index(kind)
                if kind == "cq":
                    evac(cqT[:], X[0:CQ, 0:T], x)
                elif kind == "k1":
                    evac(k1n[:], X[:, 0:T], x)
                elif kind == "sel":
                    evac(selxT[:], X[0:C, 0:KEEP], x)
                elif kind[:2] == "qp":
                    evac_q(int(kind[2]), x)
                elif kind[:2] == "kp":
                    evac_k(int(kind[2]), x)

            def behind(b, nxt, U, first):
                def value(i):
                    act.wait_ge(s["v_psum"], b * 9 + i + 1)
                    copy(vall[:, i, :], VBANK[i % 4]).then_inc(s["v_act"], 1)

                def attended(c):
                    act.wait_ge(s["oT_psum"], (b - 1) * 4 + c + 1)
                    copy(oT[:, c, :], PT[:, 0:512]).then_inc(s["oT_act"], 1)

                lead(["kp1"], 0, nxt)
                value(0)
                evac(qT[0][:], X[:, 0:T], nxt + LEAD.index("qT0"))
                value(2)
                evac(kwT[0][:], X[:, 0:T], nxt + LEAD.index("kT0"))
                value(4)
                evac(ksT[0][:], X[:, 0:KEEP], nxt + LEAD.index("sT0"))
                value(6)
                value(8)
                if not first:
                    attended(0)
                probs(0, 0, b, U)
                if not first:
                    attended(2)
                probs(1, 1, b, U + 1)

            for i in range(6):
                lead(LEAD, i, 0)
            behind(0, 0, 0, True)

            def heads(b):
                with act.Fori(0, NH // 2 - 1) as hp:
                    for p in range(2):
                        turn(b, b * (NH * NT) + hp * 8 + p * NT, xbase(b) + hp * 10 + p * 5, p, 0)

            def last_heads(b, nxt):
                for p in range(2):
                    turn(b, b * (NH * NT) + (NH - 2 + p) * NT, xbase(b) + (NH - 2 + p) * 5, p, 1 + p, nxt)

            with act.Fori(0, B - 1) as b:
                heads(b)
                nxt = xbase(b + 1) - len(LEAD)
                last_heads(b, nxt)
                behind(b + 1, nxt, (b + 1) * (NH * NT), False)
            heads(B - 1)
            last_heads(B - 1, None)
            for c in range(0, 4, 2):
                act.wait_ge(s["oT_psum"], (B - 1) * 4 + c + 1)
                copy(oT[:, c, :], PT[:, 0:512]).then_inc(s["oT_act"], 1)

            act.wait_ge(s["var_ready"], 4)
            nc.scalar.activation(st[:, 1, 0:TILES], st[:, 0, 0:TILES], ACT.Sqrt).then_inc(s["std_ready"], 1)
            for b in range(B):
                act.wait_ge(s["t2_psum"], b + 1)
                copy(xnT_all[:, b * T:(b + 1) * T], TBANK[b % 2]).then_inc(s["t2_sb"], 1)
            act.wait_ge(s["rexp_in"], 1)
            nc.scalar.activation(scr[:, 0:TILES * NE], scr[:, 0:TILES * NE], ACT.Exp).then_inc(s["rexp_out"], 1)
            for b in range(B):
                act.wait_ge(s["cT_psum"], b + 1)
                copy(cT_all[:, b * T:(b + 1) * T], [S[0], S[1]][b % 2][0:NE, 0:512]).then_inc(s["cT_sb"], 1)
            def experts(b, first):
                for c in range(4):
                    act.wait_ge(s["ffn_h"], b * 4 + c + 1)
                    act.wait_ge(s["ffn_hs"], b * 4 + c + 1)
                    nc.scalar.activation(hT[c], S[c // 2][:, (c % 2) * 512:(c % 2) * 512 + 512], ACT.Gelu,
                                         bias=b1[:, c:c + 1]).then_inc(s["ffn_gelu"], 1)
                if not first:
                    act.wait_ge(s["ffn_y"], b)
                copy(cTb, cT_all[:, ds(b * T, T)]).then_inc(s["ffn_cTb"], 1)

            experts(0, True)
            with act.Fori(0, B - 1) as b:
                experts(b + 1, False)

        @block.vector
        def _(dve):
            v = nc.vector
            ch = Chain(dve, "dve_chain")
            L = ch.link
            dve.sem_inc(s["comb_done"], 1)
            dve.sem_inc(s["pT_sb"], 1)
            dve.sem_inc(s["ffn_hs"], 4)

            L(v.memset(onesr[:], 1.0))
            L(v.memset(starts[:, 0:1], 0.0))
            dve.wait_ge(s["ld_x"], 32)
            L(v.tensor_copy(xf[:], xi[:]))
            L(v.tensor_scalar(starts[:, 1:T], xf[:, 0:T - 1], float(NEXT_ID), None, ALU.is_equal))
            v.tensor_tensor_scan(instr[:], onesr[:], starts[:], 0.0, ALU.mult, ALU.add)
            L(v.tensor_tensor(segst[:], starts[:], pos[:], ALU.mult))
            L(v.tensor_tensor_scan(lastst[:], onesr[:], segst[:], 0.0, ALU.mult, ALU.max))
            v.tensor_tensor(argsf[:], pos[:], lastst[:], ALU.subtract).then_inc(s["pos_ready"], 1)
            dve.wait_ge(s["posT"], 1)
            v.tensor_copy(idx[:], X[:, 0:3 * NT * B].rearrange("p (a t b) -> p a t b", a=3, t=NT)).then_inc(s["idx_ready"], 1)

            dve.wait_ge(s["ld_cst"], 16)
            v.tensor_copy(identb[:], ident)
            L(v.tensor_copy(maskb[:], cst[:, K_MASK:K_MASK + 2 * P]))
            dve.wait_ge(s["ld_w"], 16 * N_W)
            sm = float(HD) ** -0.5
            L(v.tensor_scalar(qw_col[:], qw_col[:], sm, None, ALU.mult))
            v.tensor_scalar(wq[:, :, NOPE:QW], wq[:, :, NOPE:QW], qw_col[:], None, ALU.mult)
            v.tensor_scalar(wqn_raw[:], wqn_raw[:], qw_col[:], None, ALU.mult)
            v.tensor_scalar(wkn[:], wkn[:], kvw_col[:], None, ALU.mult)
            v.tensor_scalar(wv[:], wv[:], kvw_col[:], None, ALU.mult)
            v.tensor_scalar(wlat[:, CQ + CKV:LAT], wlat[:, CQ + CKV:LAT], 1.0 / NH, None, ALU.mult).then_inc(s["wq_scaled"], 1)
            dve.wait_ge(s["wT_psum"], 1)
            v.tensor_copy(wqnT[:], S[0][:, 0:4 * CQ].rearrange("p (c q) -> p c q", c=4))
            dve.wait_ge(s["kconst"], 6)
            for g_ in range(4):
                last = v.tensor_copy(wknBD[32 * g_:32 * g_ + 32, :, 32 * g_:32 * g_ + 32],
                                     S[0][32 * g_:32 * g_ + 32, 512:512 + 4 * CKV].rearrange("p (c q) -> p c q", c=4))
            last.then_inc(s["wT_sb"], 1)
            dve.wait_ge(s["wabs_psum"], 1)
            v.tensor_copy(wq[:, :, 0:NOPE], S[1][0:CQ, 0:512].rearrange("p (h q) -> p h q", h=NH)).then_inc(s["wabs_sb"], 1)

            def bc(ap, shape):
                return ap.to_broadcast(shape)

            def rsqrt(n, k):
                a, r, y, z = (st[:, i, 0:n] for i in (0, 1, 2, 3))
                dve.wait_ge(s["std_ready"], k)
                L(v.reciprocal(y, r))
                L(v.tensor_tensor(z, y, y, ALU.mult))
                L(v.tensor_tensor(z, z, a, ALU.mult))
                L(v.tensor_scalar(z, z, -0.5, 1.5, ALU.mult, ALU.add))
                L(v.tensor_tensor(y, y, z, ALU.mult))

            def layernorm(dst, src, k):
                s3, d3 = (x.rearrange("p (n c) -> p n c", c=C) for x in (src, dst))
                q3 = scr[:, 0:TILES * C].rearrange("p (n c) -> p n c", c=C)
                m = st[:, 4, 0:TILES]
                L(v.tensor_reduce(m, s3, op=ALU.add, axis=AX.X))
                L(v.tensor_scalar(m, m, 1.0 / C, None, ALU.mult))
                L(v.tensor_tensor(d3, s3, bc(m.unsqueeze(2), [P, TILES, C]), ALU.subtract))
                L(v.tensor_tensor(q3, d3, d3, ALU.mult))
                L(v.tensor_reduce(st[:, 0, 0:TILES], q3, op=ALU.add, axis=AX.X))
                ins = v.tensor_scalar(st[:, 0, 0:TILES], st[:, 0, 0:TILES], 1.0 / C, 1e-5, ALU.mult, ALU.add)
                ins.then_inc(s["var_ready"], 1)
                rsqrt(TILES, k)
                return v.tensor_tensor(d3, d3, bc(st[:, 2, 0:TILES].unsqueeze(2), [P, TILES, C]), ALU.mult)

            dve.wait_ge(s["gathered"], 16 * 3 * TILES)
            L(v.tensor_tensor(cur, cur, big[:, 1, :], ALU.add))
            L(v.tensor_tensor(cur, cur, big[:, 2, :], ALU.add))
            L(layernorm(h_all[:], cur, 1))
            h3 = h_all[:].rearrange("p (n c) -> p n c", c=C)
            L(v.tensor_tensor(h3, h3, bc(gamma_b[:].unsqueeze(1), [P, TILES, C]), ALU.mult))
            L(v.tensor_tensor(h3, h3, bc(beta_b[:].unsqueeze(1), [P, TILES, C]), ALU.add))
            layernorm(xn_all[:], h_all[:], 2).then_inc(s["xn_ready"], 1)

            for b in range(B):
                for k in range(2):
                    i = 2 * b + k
                    dve.wait_ge(s["lat_psum"], i + 1)
                    src = [S[1], PT][b % 2][:, 512 * k:512 * k + 2 * (LAT + 3)].rearrange("p (t c) -> p t c", t=2)
                    n = b * NT + 2 * k
                    v.tensor_copy(lat_all[:, n:n + 2, 0:LAT], src[:, :, 0:LAT])
                    last = v.tensor_copy(gl_all[:, n:n + 2, :], src[:, :, LAT:LAT + 3])
                    last.then_inc(s["lat_sb"], 1)

            dve.wait_ge(s["imp_psum"], 1)
            L(v.tensor_copy(sc0[:], O[0:B, :]))
            a, z = sc0, sc1
            for r in range(KEEP // 8):
                m8 = top8[:, 8 * r:8 * r + 8]
                L(v.max(m8, a[:]))
                L(v.match_replace(z[:], m8, a[:], NEG))
                a, z = z, a
            L(v.tensor_scalar(selm[:], a[:], NEG, None, ALU.is_equal))
            L(v.tensor_tensor_scan(rank[:], onesr[:], selm[:], 0.0, ALU.mult, ALU.add))
            L(v.tensor_tensor(rankm[:], rank[:], selm[:], ALU.mult))
            v.tensor_scalar(rankm[:], rankm[:], -1.0, None, ALU.add).then_inc(s["rank_ready"], 1)
            dve.wait_ge(s["rank_psum"], 1)
            L(v.tensor_copy(rankT[:], X[:, 0:NT * B].rearrange("p (t b) -> p b t", t=NT)))

            dve.wait_ge(s["gsum_psum"], 1)
            L(v.tensor_reduce(gate_all[:], O[:, 0:TILES * 3].rearrange("p (b t g) -> p b g t", b=B, t=NT), op=ALU.add, axis=AX.X))
            L(v.tensor_reduce(st[:, 4, 0:B], gate_all[:], op=ALU.max, axis=AX.X))
            L(v.tensor_tensor(gate_all[:], gate_all[:], bc(st[:, 4, 0:B].unsqueeze(2), [P, B, 3]), ALU.subtract))
            v.tensor_scalar(gate_all[:], gate_all[:], 1.0 / T, None, ALU.mult).then_inc(s["gexp_in"], 1)

            nc4 = TILES * P
            q3 = scr[:, 0:nc4].rearrange("p (n c) -> p n c", c=P)
            L(v.tensor_tensor(q3, lat_all[:, :, 0:P], lat_all[:, :, 0:P], ALU.mult))
            L(v.tensor_reduce(st[:, 5, 0:TILES], q3[:, :, 0:CQ], op=ALU.add, axis=AX.X))
            L(v.tensor_reduce(st[:, 5, TILES:2 * TILES], q3[:, :, CQ:P], op=ALU.add, axis=AX.X))
            v.tensor_scalar(st[:, 0, 0:TILES], st[:, 5, 0:TILES], 1.0 / CQ, 1e-6, ALU.mult, ALU.add)
            v.tensor_scalar(st[:, 0, TILES:], st[:, 5, TILES:], 1.0 / CKV, 1e-6, ALU.mult, ALU.add).then_inc(s["var_ready"], 1)
            kr = lat_all[:, :, CQ + CKV:LAT].rearrange("p (b t) r -> p b t r", b=B)
            krc = scr[:, 0:2048].rearrange("p (b t r) -> p b t r", b=B, t=NT)
            krs = scr[:, 2048:4096].rearrange("p (b t r) -> p b t r", b=B, t=NT)
            hf = ROPE // 2
            for b in range(B):
                v.tensor_tensor(krc[:, b], kr[:, b], cos5[:, 0:NT, :], ALU.mult)
                last = v.tensor_tensor(krs[:, b], kr[:, b], sin5[:, 0:NT, :], ALU.mult)
            L(last)
            for b in range(B):
                v.tensor_tensor(kr[:, b, :, 0:hf], krc[:, b, :, 0:hf], krs[:, b, :, hf:], ALU.subtract)
                last = v.tensor_tensor(kr[:, b, :, hf:], krc[:, b, :, hf:], krs[:, b, :, 0:hf], ALU.add)
            L(last)
            rsqrt(2 * TILES, 3)
            v.tensor_tensor(lat_all[:, :, 0:CQ], lat_all[:, :, 0:CQ], bc(st[:, 2, 0:TILES].unsqueeze(2), [P, TILES, CQ]), ALU.mult)
            v.tensor_tensor(lat_all[:, :, CQ:P], lat_all[:, :, CQ:P], bc(st[:, 2, TILES:].unsqueeze(2), [P, TILES, CKV]), ALU.mult)
            dve.wait_ge(s["gexp_out"], 1)
            L(v.tensor_reduce(st[:, 4, 0:B], gate_all[:], op=ALU.add, axis=AX.X))
            L(v.reciprocal(st[:, 5, 0:B], st[:, 4, 0:B]))
            v.tensor_tensor(gate_all[:], gate_all[:], bc(st[:, 5, 0:B].unsqueeze(2), [P, B, 3]), ALU.mult).then_inc(s["phaseA"], 1)

            def maxima(u, t, U):
                par = u % 2
                n1, n2, n3 = kblocks(t)
                dve.wait_ge(s["scores_ready"], U + 1)
                v.tensor_reduce(negm[par][:, 0:1], S[par][:, 0:n1], op=ALU.max, axis=AX.X, negate=True)
                v.tensor_reduce(negm[par][:, 1:2], S[par][:, 4 * P:4 * P + n2], op=ALU.max, axis=AX.X, negate=True)
                v.tensor_reduce(negm[par][:, 2:3], S[par][:, 5 * P:5 * P + n3], op=ALU.max, axis=AX.X, negate=True).then_inc(s["max_ready"], 1)

            def take_pT(u, t, U):
                par = u % 2
                n1, n2, n3 = kblocks(t)
                dve.wait_ge(s["pT_psum"], U + 3)
                dve.wait_ge(s["pv_done"], U + 1)
                dst = pT[par][:].rearrange("p a q -> p (a q)")
                v.tensor_copy(dst[:, 0:n1], PT[:, 0:n1])
                v.tensor_copy(dst[:, 4 * P:5 * P + n3], PT[:, 4 * P:5 * P + n3]).then_inc(s["pT_sb"], 1)

            def combine(par, b, H):
                dve.wait_ge(s["probs_ready"], H * NT + 6)
                v.reciprocal(rinv[:], sums[par][:]).then_inc(s["coef_chain"], 1)
                dve.wait_ge(s["coef_chain"], H * 2 + 1)
                v.tensor_tensor(coef[:], rinv[:], bc(gate_all[:, ds(b, 1), :], [P, NT, 3]), ALU.mult).then_inc(s["coef_chain"], 1)
                dve.wait_ge(s["coef_chain"], H * 2 + 2)
                dve.wait_ge(s["osum_done"], H + 1)
                dve.wait_ge(s["pv_done"], H * NT + 6)
                v.tensor_tensor(obr[par][:].rearrange("p t k d -> p (t k) d"),
                                O[:, 0:NT * 3 * VD].rearrange("p (a d) -> p a d", d=VD),
                                bc(coef[:].rearrange("p t k -> p (t k)").unsqueeze(2), [P, NT * 3, VD]),
                                ALU.mult).then_inc(s["comb_done"], 1)

            def turn(b, H, p, last):
                U = H * NT
                for t in range(NT):
                    u = p * NT + t
                    take_pT(u, t, U + t)
                    if last < 2 or t < 2:
                        maxima(u + 2, (t + 2) % NT, U + t + 2)
                combine(p, b, H)

            def mark_selected(b):
                dve.wait_ge(s["ld_lat"], b * 48 + 48)
                v.tensor_tensor(onehot[:], bc(iota_row.unsqueeze(1), [P, NT, KEEP]),
                                bc(rank_b[:].unsqueeze(2), [P, NT, KEEP]), ALU.is_equal).then_inc(s["onehot_ready"], 1)

            def attended(b, c):
                dve.wait_ge(s["oT_psum"], b * 4 + c + 1)
                v.tensor_copy(oT[:, c, :], PT[:, 512:1024]).then_inc(s["oT_dve"], 1)

            def residual(b):
                dve.wait_ge(s["attn_psum"], b + 1)
                hb = h_all[:, ds(b * (NT * C), NT * C)]
                v.tensor_tensor(hb, O[:, 0:NT * C], hb, ALU.add).then_inc(s["h_done"], 1)

            def behind(b, U, first):
                dve.wait_ge(s["x_evac"], xbase(b) + x_lead("k1") + 2)
                v.tensor_copy(k1T[:], k1n[:]).then_inc(s["k1_moved"], 1)
                for i in range(1, 9, 2):
                    dve.wait_ge(s["v_psum"], b * 9 + i + 1)
                    v.tensor_copy(vall[:, i, :], VBANK[i % 4]).then_inc(s["v_dve"], 1)
                if not first:
                    attended(b - 1, 1)
                maxima(0, 0, U)
                if not first:
                    attended(b - 1, 3)
                maxima(1, 1, U + 1)
                if not first:
                    residual(b - 1)

            mark_selected(0)
            behind(0, 0, True)

            def heads(b):
                with dve.Fori(0, NH // 2 - 1) as hp:
                    turn(b, b * NH + hp * 2, 0, 0)
                    turn(b, b * NH + hp * 2 + 1, 1, 0)

            with dve.Fori(0, B - 1) as b:
                heads(b)
                mark_selected(b + 1)
                turn(b, b * NH + (NH - 2), 0, 1)
                turn(b, b * NH + (NH - 1), 1, 2)
                behind(b + 1, (b + 1) * (NH * NT), False)
            heads(B - 1)
            turn(B - 1, B * NH - 2, 0, 1)
            turn(B - 1, B * NH - 1, 1, 2)
            attended(B - 1, 1)
            attended(B - 1, 3)
            residual(B - 1)

            dve.wait_ge(s["h_done"], B)
            layernorm(xn_all[:], h_all[:], 4).then_inc(s["xn_ready"], 1)
            n = TILES * NE
            e3 = scr[:, 0:n].rearrange("p (n e) -> p n e", e=NE)
            c3 = scr[:, n:2 * n].rearrange("p (n e) -> p n e", e=NE)
            big4 = big[:, 0, :].rearrange("p (n a e) -> p n a e", n=TILES, a=NE)
            eq4 = big[:, 2, :].rearrange("p (n a e) -> p n a e", n=TILES, a=NE)
            m = st[:, 4, 0:TILES]
            r3 = st[:, 5, 0:TILES]
            dve.wait_ge(s["rl_psum"], 1)
            l3 = X[:, 0:n].rearrange("p (n e) -> p n e", e=NE)
            L(v.tensor_reduce(m, l3, op=ALU.max, axis=AX.X))
            v.tensor_tensor(e3, l3, bc(m.unsqueeze(2), [P, TILES, NE]), ALU.subtract).then_inc(s["rexp_in"], 1)
            dve.wait_ge(s["rexp_out"], 1)
            L(v.tensor_reduce(m, e3, op=ALU.add, axis=AX.X))
            L(v.reciprocal(r3, m))
            L(v.tensor_tensor(e3, e3, bc(r3.unsqueeze(2), [P, TILES, NE]), ALU.mult))
            for a_ in range(NE):
                mine = bc(e3[:, :, a_:a_ + 1], [P, TILES, NE])
                v.tensor_tensor(big4[:, :, a_, :], e3, mine, ALU.is_gt)
                last = v.tensor_tensor(eq4[:, :, a_, :], e3, mine, ALU.is_equal)
            L(last)
            for a_ in range(NE):
                last = v.tensor_tensor(eq4[:, :, a_, :], eq4[:, :, a_, :], bc(tri[:, a_:a_ + 1, :], [P, TILES, NE]), ALU.mult)
            L(last)
            L(v.tensor_tensor(big[:, 0, :], big[:, 0, :], big[:, 2, :], ALU.add))
            L(v.tensor_reduce(c3, big4, op=ALU.add, axis=AX.X))
            L(v.tensor_scalar(c3, c3, 2.0, None, ALU.is_lt))
            L(v.tensor_tensor(c3, c3, e3, ALU.mult))
            L(v.tensor_reduce(m, c3, op=ALU.add, axis=AX.X))
            L(v.tensor_scalar(m, m, 1e-12, None, ALU.max))
            L(v.reciprocal(r3, m))
            v.tensor_tensor(c3, c3, bc(r3.unsqueeze(2), [P, TILES, NE]), ALU.mult).then_inc(s["comb_ready"], 1)

            def expert_scale(b):
                for c in range(4):
                    dve.wait_ge(s["ffn_cb"], b * 4 + c + 1)
                    dve.wait_ge(s["ffn_gelu"], b * 4 + c + 1)
                    v.tensor_tensor(hs[c], hT[c], PT[:, (c % 2) * 512:(c % 2) * 512 + 512], ALU.mult).then_inc(s["ffn_hs"], 1)

            def finish(b):
                dve.wait_ge(s["ffn_y"], b + 1)
                v.tensor_tensor(y1, O[:, 0:NT * C], xn_all[:, ds(b * (NT * C), NT * C)], ALU.add).then_inc(s["ffn_out1"], 1)
                dve.wait_ge(s["ffn_out1"], b + 1)
                hb = h_all[:, ds(b * (NT * C), NT * C)]
                v.tensor_tensor(hb, y1, hb, ALU.add).then_inc(s["ffn_out"], 1)

            expert_scale(0)
            with dve.Fori(0, B - 1) as b:
                finish(b)
                expert_scale(b + 1)
            finish(B - 1)

        @block.tensor
        def _(pe):
            mm, tp = nc.tensor.matmul, nc.tensor.transpose
            pe.sem_inc(s["pv_done"], 2)
            pe.sem_inc(s["pT_psum"], 2)

            pe.wait_ge(s["ld_cst"], 16)
            pe.wait_ge(s["pos_ready"], 1)
            for a, src in enumerate((xf, instr, argsf)):
                for t in range(NT):
                    o = (a * NT + t) * B
                    last = tp(X[:, o:o + B], src[:, t * P:(t + 1) * P], cst[0:B, 0:B])
            last.then_inc(s["posT"], 1)

            pe.wait_ge(s["wq_scaled"], 1)
            for c in range(4):
                tp(S[0][:, c * CQ:(c + 1) * CQ], wqn_raw[:, c * P:(c + 1) * P], cst[0:CQ, 0:CQ])
            for c in range(4):
                last = tp(S[0][:, 512 + c * CKV:512 + (c + 1) * CKV], wkn[:, c * P:(c + 1) * P], cst[0:CKV, 0:CKV])
            last.then_inc(s["wT_psum"], 1)
            pe.wait_ge(s["wT_sb"], 1)
            for c in range(4):
                last = mm(S[1][0:CQ, c * P:(c + 1) * P], wqnT[:, c, :], wknBD[:, c, :], start=True, stop=True)
            last.then_inc(s["wabs_psum"], 1)
            pe.wait_ge(s["wabs_sb"], 1)

            def transposes(ready, name, sb_name):
                pe.wait_ge(s["xn_ready"], ready)
                for b in range(B):
                    if b >= 2:
                        pe.wait_ge(s[sb_name], b - 1)
                    for t in range(NT):
                        n_ = (b * NT + t) * C
                        last = tp(TBANK[b % 2][:, t * P:(t + 1) * P], xn_all[:, n_:n_ + C], ident)
                    last.then_inc(s[name], 1)

            pe.wait_ge(s["idx_ready"], 1)
            transposes(1, "xnT_psum", "xnT_sb")
            pe.wait_ge(s["ld_wimp"], 16)
            pe.wait_ge(s["xnT_sb"], B)
            for b in range(B):
                last = mm(O[0:B, :], wimp[:, B - 1 - b:2 * B - 1 - b], xnT_all[:, b * T:(b + 1) * T], start=(b == 0), stop=(b == B - 1))
            last.then_inc(s["imp_psum"], 1)
            for b in range(B):
                if b >= 2:
                    pe.wait_ge(s["lat_sb"], 2 * (b - 1))
                for t in range(NT):
                    n_ = (b * NT + t) * P
                    o = (t // 2) * 512 + (t % 2) * (LAT + 3)
                    last = mm([S[1], PT][b % 2][:, o:o + LAT + 3], xnT_all[:, n_:n_ + P], wlat[:], start=True, stop=True)
                    if t % 2:
                        last.then_inc(s["lat_psum"], 1)
            pe.wait_ge(s["rank_ready"], 1)
            for t in range(NT):
                last = tp(X[:, t * B:(t + 1) * B], rankm[:, t * P:(t + 1) * P], cst[0:B, 0:B])
            last.then_inc(s["rank_psum"], 1)
            pe.wait_ge(s["lat_sb"], 2 * B)
            mm(O[:, 0:TILES * 3], ones[:], gl_all[:].rearrange("p n g -> p (n g)"), start=True, stop=True).then_inc(s["gsum_psum"], 1)
            pe.wait_ge(s["phaseA"], 1)

            def x_wait(x):
                pe.wait_ge(s["x_evac"], x + 1)

            def q_proj(h, x):
                x_wait(x)
                for t in range(NT):
                    last = mm(X[:, t * QW:(t + 1) * QW], cqT[:, t * P:(t + 1) * P],
                              wq[:].rearrange("c h q -> c (h q)")[:, ds(h * QW, QW)], start=True, stop=True)
                last.then_inc(s["x_ready"], 1)

            def k_proj(h, x):
                x_wait(x)
                pe.nop(nofuse=True)
                for t in range(NT):
                    mm(X[:, t * HD:(t + 1) * HD], xnT_b[:, t * P:(t + 1) * P],
                       wkw[:].rearrange("c h q -> c (h q)")[:, ds(h * HD, HD)], start=True, stop=True)
                mm(X[:, NT * HD:5 * HD], selxT[:], wks[:].rearrange("c h q -> c (h q)")[:, ds(h * HD, HD)],
                   start=True, stop=True).then_inc(s["x_ready"], 1)

            def q_turn(par, x, H):
                x_wait(x)
                pe.wait_ge(s["rope_q"], H + 1)
                for t in range(NT):
                    last = tp(X[:, t * P:(t + 1) * P], qs[par][:, t, :], ident)
                last.then_inc(s["x_ready"], 1)

            def k_turn(par, x, H):
                x_wait(x)
                pe.wait_ge(s["rope_k"], H + 1)
                for t in range(NT):
                    last = tp(X[:, t * P:(t + 1) * P], kk[par][:, t, :], ident)
                last.then_inc(s["x_ready"], 1)

            def s_turn(par, x):
                x_wait(x)
                tp(X[:, 0:P], kk[par][:, 4, :], ident).then_inc(s["x_ready"], 1)

            def lead(kind, b, nxt):
                x = nxt + LEAD.index(kind)
                if kind == "cq":
                    x_wait(x)
                    pe.wait_ge(s["ld_lat"], b * 48 + 48)
                    for t in range(NT):
                        last = tp(X[0:CQ, t * P:(t + 1) * P], lat_b[:, t, 0:CQ], ident)
                    last.then_inc(s["x_ready"], 1)
                elif kind == "k1":
                    x_wait(x)
                    for t in range(NT):
                        last = tp(X[:, t * P:(t + 1) * P], lat_b[:, t, CQ:LATP], ident)
                    last.then_inc(s["x_ready"], 1)
                elif kind == "sel":
                    x_wait(x)
                    pe.wait_ge(s["onehot_ready"], b + 1)
                    for t in range(NT):
                        last = mm(X[0:C, 0:KEEP], xn_b[:, t, :], onehot[:, t, :], start=(t == 0), stop=(t == NT - 1))
                    last.then_inc(s["x_ready"], 1)
                elif kind[:2] == "qp":
                    q_proj(int(kind[2]), x)
                elif kind[:2] == "kp":
                    pe.wait_ge(s["ld_xnT"], b * 16 + 16)
                    k_proj(int(kind[2]), x)

            def scores(u, t, par, U):
                pe.wait_ge(s["probs_ready"], U + 1)
                z = S[u % 2]
                n1, n2, n3 = kblocks(t)
                q = qT[par][:, t * P:(t + 1) * P]
                mm(z[:, 0:n1], q, k1T[:, 0:n1], start=True, stop=True)
                mm(z[:, n1 - P:n1], identb[:], maskb[:, P:2 * P], start=False, stop=True, skip_group_check=True)
                mm(z[:, 4 * P:5 * P], q, ksT[par][:], start=True, stop=True)
                mm(z[:, 5 * P:5 * P + n3], q, kwT[par][:, (t + 1) * P - n3:(t + 1) * P], start=True, stop=True)
                mm(z[:, 5 * P:5 * P + n3], identb[:], maskb[:, 2 * P - n3:2 * P], start=False, stop=True, skip_group_check=True).then_inc(s["scores_ready"], 1)

            def turn_probs(u, t, U):
                pe.wait_ge(s["probs_ready"], U + 3)
                pe.wait_ge(s["pT_sb"], U + 1)
                n1, n2, n3 = kblocks(t)
                src = pr[u % 2]
                for lo in list(range(0, n1, P)) + list(range(4 * P, 5 * P + n3, P)):
                    last = tp(PT[:, lo:lo + P], src[:, lo:lo + P], ident)
                last.then_inc(s["pT_psum"], 1)

            def values(u, t, h, U, first):
                pe.wait_ge(s["pT_sb"], U + 2)
                if t == 0:
                    pe.wait_ge(s["comb_done"], first + 1)
                w = pT[u % 2]
                for k, (blocks, v0) in enumerate((([0, 1, 2, 3][:t + 1], 0), ([4], 8),
                                                  ([5] if t == 0 else [5, 6], 4 + max(t - 1, 0)))):
                    o = O[:, (t * 3 + k) * VD:(t * 3 + k + 1) * VD]
                    for i, blk in enumerate(blocks):
                        last = mm(o, w[:, blk, :], vall[:].rearrange("p n q -> p (n q)")[:, ds(h * VD + (v0 + i) * NH * VD, VD)],
                                  start=(i == 0), stop=(i == len(blocks) - 1))
                last.then_inc(s["pv_done"], 1)

            def turn(h, H, xb, p, last, b=None, nxt=None):
                U = H * NT
                for t in range(NT):
                    u = p * NT + t
                    if last < 2 and t == 0:
                        q_turn(1 - p, xb + x_index(0, "qT"), H + 1)
                    if last < 2 and t == 1:
                        s_turn(1 - p, xb + x_index(0, "sT"))
                    if last < 1 and t == 2:
                        q_proj(h + 2, xb + x_index(0, "qp"))
                    if last < 1 and t == 3:
                        k_proj(h + 2, xb + x_index(0, "kp"))
                    i = t - 2 if last == 1 else t + 2
                    if nxt is not None and 0 <= i < 6:
                        lead(LEAD[i], b, nxt)
                    if last < 2 or t < 2:
                        if t == 2:
                            pe.wait_ge(s["x_evac"], xb + x_index(0, "sT") + 2)
                        scores(u + 2, (t + 2) % NT, p if t < 2 else 1 - p, U + t + 2)
                    values(u, t, h, U + t, H)
                    if last < 2 and t == 0:
                        k_turn(1 - p, xb + x_index(0, "kT"), H + 1)
                    if last < 2 or t < 3:
                        turn_probs(u + 1, (t + 1) % NT, U + t + 1)

            def behind(b, nxt, H, first):
                def value(i):
                    if i >= 4 and i % 2 == 0:
                        pe.wait_ge(s["v_act"], b * 5 + (i - 4) // 2 + 1)
                    if i >= 4 and i % 2 == 1:
                        pe.wait_ge(s["v_dve"], b * 4 + (i - 5) // 2 + 1)
                    if i < 4:
                        lhs, rhs = k1n[0:CKV, i * P:(i + 1) * P], wv[:]
                    elif i < 8:
                        lhs, rhs = xnT_b[:, (i - 4) * P:(i - 3) * P], wvw[:]
                    else:
                        lhs, rhs = selxT[:], wvs[:]
                    mm(VBANK[i % 4], lhs, rhs, start=True, stop=True).then_inc(s["v_psum"], 1)

                def attended(c):
                    if c >= 2:
                        pe.wait_ge(s[["oT_act", "oT_dve"][c % 2]], (b - 1) * 2 + 1)
                    for t in range(NT):
                        last = tp(PT[:, (c % 2) * 512 + t * P:(c % 2) * 512 + (t + 1) * P], o_b[:, t, c * P:(c + 1) * P], ident)
                    last.then_inc(s["oT_psum"], 1)

                lead("kp1", b, nxt)
                pe.wait_ge(s["probs_ready"], H * NT + 2)
                value(0)
                value(1)
                q_turn(0, nxt + LEAD.index("qT0"), H)
                value(2)
                value(3)
                k_turn(0, nxt + LEAD.index("kT0"), H)
                value(4)
                value(5)
                s_turn(0, nxt + LEAD.index("sT0"))
                for i in range(6, 9):
                    value(i)
                if not first:
                    pe.wait_ge(s["osum_done"], H + 2)
                    pe.wait_ge(s["pT_sb"], H * NT + 1)
                    attended(0)
                    attended(1)
                pe.wait_ge(s["v_act"], b * 5 + 5)
                pe.wait_ge(s["v_dve"], b * 4 + 4)
                pe.wait_ge(s["k1_moved"], b + 1)
                pe.wait_ge(s["x_evac"], nxt + LEAD.index("sT0") + 2)
                scores(0, 0, 0, H * NT)
                if not first:
                    attended(2)
                    attended(3)
                scores(1, 1, 0, H * NT + 1)
                if not first:
                    project(b - 1, H)
                turn_probs(0, 0, H * NT)

            def project(b, H):
                pe.wait_ge(s["comb_done"], H + 1)
                pe.wait_ge(s["oT_act"], b * 2 + 2)
                pe.wait_ge(s["oT_dve"], b * 2 + 2)
                for t in range(NT):
                    for c in range(4):
                        last = mm(O[:, t * C:(t + 1) * C], oT[:, c, t * P:(t + 1) * P], wproj[:, c, :], start=(c == 0), stop=(c == 3))
                last.then_inc(s["attn_psum"], 1)

            def heads(b):
                with pe.Fori(0, NH // 2 - 1) as hp:
                    for p in range(2):
                        turn(hp * 2 + p, b * NH + hp * 2 + p, xbase(b) + hp * 10 + p * 5, p, 0)

            for kind in LEAD[:6]:
                lead(kind, 0, 0)
            behind(0, 0, 0, True)
            with pe.Fori(0, B - 1) as b:
                heads(b)
                nxt = xbase(b + 1) - len(LEAD)
                for p in range(2):
                    turn(NH - 2 + p, b * NH + (NH - 2 + p), xbase(b) + (NH - 2 + p) * 5, p, 1 + p, b + 1, nxt)
                behind(b + 1, nxt, (b + 1) * NH, False)
                pe.wait_ge(s["h_done"], b + 1)
            heads(B - 1)
            for p in range(2):
                turn(NH - 2 + p, B * NH - 2 + p, xbase(B - 1) + (NH - 2 + p) * 5, p, 1 + p)
            pe.wait_ge(s["osum_done"], B * NH + 2)
            pe.wait_ge(s["pT_sb"], B * NH * NT + 1)
            for c in range(4):
                if c >= 2:
                    pe.wait_ge(s[["oT_act", "oT_dve"][c % 2]], (B - 1) * 2 + 1)
                for t in range(NT):
                    last = tp(PT[:, (c % 2) * 512 + t * P:(c % 2) * 512 + (t + 1) * P], o_b[:, t, c * P:(c + 1) * P], ident)
                last.then_inc(s["oT_psum"], 1)
            project(B - 1, B * NH)
            pe.wait_ge(s["h_done"], B)

            pe.wait_ge(s["x_evac"], xbase(B) - len(LEAD) + 1)
            transposes(2, "t2_psum", "t2_sb")
            pe.wait_ge(s["t2_sb"], B)
            for n_ in range(TILES):
                last = mm(X[:, n_ * NE:(n_ + 1) * NE], xnT_all[:, n_ * P:(n_ + 1) * P], rwT[:], start=True, stop=True)
            last.then_inc(s["rl_psum"], 1)
            pe.wait_ge(s["comb_ready"], 1)
            for b in range(B):
                if b >= 2:
                    pe.wait_ge(s["cT_sb"], b - 1)
                for t in range(NT):
                    n_ = (b * NT + t) * NE + TILES * NE
                    last = tp([S[0], S[1]][b % 2][0:NE, t * P:(t + 1) * P], scr[:, n_:n_ + NE], ident)
                last.then_inc(s["cT_psum"], 1)
            pe.wait_ge(s["cT_sb"], B)
            def hidden(b):
                for c in range(4):
                    pe.wait_ge(s["ffn_hs"], b * 4 + c + 1)
                    pe.nop(nofuse=True)
                    mm(S[c // 2][:, (c % 2) * 512:(c % 2) * 512 + 512], w1[:, 2 * c:2 * c + 2, :].rearrange("i e o -> i (e o)"),
                       xnT_all[:, ds(b * T, T)], start=True, stop=True).then_inc(s["ffn_h"], 1)

            def weights(b):
                for c in range(4):
                    pe.wait_ge(s["ffn_hs"], b * 4 + c + 3)
                    pe.nop(nofuse=True)
                    mm(PT[:, (c % 2) * 512:(c % 2) * 512 + 512], pairsel[:, c, :], cT_all[:, ds(b * T, T)],
                       start=True, stop=True).then_inc(s["ffn_cb"], 1)

            def outputs(b, first):
                pe.wait_ge(s["ffn_hs"], b * 4 + 8)
                pe.wait_ge(s["ffn_cTb"], b + 1)
                if not first:
                    pe.wait_ge(s["ffn_out1"], b)
                for t in range(NT):
                    for c in range(4):
                        mm(O[:, t * C:(t + 1) * C], hs[c][:, t * P:(t + 1) * P], w2[:, c, :], start=(c == 0), stop=False)
                    last = mm(O[:, t * C:(t + 1) * C], cTb[:, t * P:(t + 1) * P], b2[:], start=False, stop=True)
                last.then_inc(s["ffn_y"], 1)

            hidden(0)
            weights(0)
            hidden(1)
            outputs(0, True)
            weights(1)
            with pe.Fori(0, B - 2) as b:
                hidden(b + 2)
                outputs(b + 1, False)
                weights(b + 2)
            outputs(B - 1, False)


N_W = 26


def _constants():
    import numpy as np
    c = np.zeros((P, K_END), np.float32)
    c[:, K_ID:K_ID + P] = np.eye(P)
    q, k = np.arange(P)[:, None], np.arange(P)[None, :]
    c[:, K_MASK:K_MASK + P] = np.where(k > q, 0.0, -1e30)
    c[:, K_MASK + P:K_MASK + 2 * P] = np.where(k <= q, 0.0, -1e30)
    f = 1.0 / 10000.0 ** (np.arange(0, ROPE, 2, dtype=np.float32) / ROPE)
    ang = np.outer(np.arange(T, dtype=np.float32), f)
    for col, tab in ((K_COS, np.cos(ang)), (K_SIN, np.sin(ang))):
        for t in range(5):
            rows = tab[(t % NT) * P:(t % NT) * P + P]
            c[:, col + t * ROPE:col + (t + 1) * ROPE] = np.concatenate([rows, rows], 1)
    c[:, K_IOTA:K_IOTA + P] = np.arange(P)
    c[:, K_TRI:K_TRI + NE * NE] = (np.arange(NE)[None, :] < np.arange(NE)[:, None]).astype(np.float32).reshape(-1)
    pos = np.tile(np.arange(T, dtype=np.float32), (B, 1))
    pair = np.zeros((NE, NE // 2, 2, P // 2), np.float32)
    for e in range(NE):
        pair[e, e // 2, e % 2] = 1.0
    return {"c_cst": c, "c_pos": pos, "c_pair": pair.reshape(NE, -1)}


def kernel(**inputs):
    import numpy as _np
    import concourse.bacc as _bacc
    from concourse import mybir as _mybir
    from concourse.bass_utils import run_bass_kernel_spmd as _run

    nc = _bacc.Bacc("TRN2", target_bir_lowering=False, num_devices=1)
    arrays, aps = {}, {}
    given = {n: _np.ascontiguousarray(inputs[n]) for n in ARGS}
    given.update(_constants())
    given["c_rwT"] = _np.ascontiguousarray(given["L0_ffn_router_w"].T)
    given["c_b1T"] = _np.ascontiguousarray(given["L0_ffn_b1"].reshape(NE // 2, P).T)
    for name, a in given.items():
        arrays[f"in_{name}_dram"] = a
        aps[name] = nc.dram_tensor(f"in_{name}_dram", a.shape, _mybir.dt.from_np(a.dtype), kind="ExternalInput").ap()
    out = nc.dram_tensor("out_0_dram", (B, T, C), _mybir.dt.float32, kind="ExternalOutput").ap()
    tower(nc, aps, out)
    r = _run(nc, [arrays], core_ids=[0])
    return r.results[0]["out_0_dram"]
```

```python
import concourse.bass as bass
from concourse import mybir
from contextlib import ExitStack

B, T, C = 8, 512, 64
P = 128
NT = T // P
TILES = B * NT
NH, NOPE, ROPE, VD = 16, 32, 64, 32
HD = NOPE + ROPE
CQ, CKV = 96, 32
KEEP = 128
QW = NOPE + ROPE + NOPE
LAT = CQ + CKV + ROPE
LATP = LAT + NOPE
NE = 8
NEXT_ID = 5
NEG = -3.0e38
PARTS = [(0, 4), (4, 6), (6, B)]
PARTS_FFN = [(0, 5), (5, B)]
PSCALE = 2.0 ** 15

K_ID, K_MASK, K_COS, K_SIN, K_IOTA, K_TRI, K_END = 0, 128, 384, 704, 1024, 1152, 1216

ARGS = ["x", "L0_tok_token_emb", "L0_tok_instr_emb", "L0_tok_arg_emb", "L0_tok_gamma", "L0_tok_beta",
        "L0_attn_Wcq", "L0_attn_q_norm_w", "L0_attn_Wq_nope", "L0_attn_Wq_rope", "L0_attn_Wckv",
        "L0_attn_kv_norm_w", "L0_attn_Wk_nope", "L0_attn_Wv", "L0_attn_Wk_rope", "L0_attn_W_imp",
        "L0_attn_Wsel_k", "L0_attn_Wsel_v", "L0_attn_Wwin_k", "L0_attn_Wwin_v", "L0_attn_Wgate",
        "L0_attn_Wproj", "L0_ffn_router_w", "L0_ffn_w1", "L0_ffn_b1", "L0_ffn_w2", "L0_ffn_b2"]


def tower(nc, d, out):
    fp32, bf16, fp16, i32 = mybir.dt.float32, mybir.dt.bfloat16, mybir.dt.float16, mybir.dt.int32
    ALU, ACT, AX = mybir.AluOpType, mybir.ActivationFunctionType, mybir.AxisListType
    ds = bass.ds
    ctx = ExitStack()
    with ctx:
        def sb(name, shape, dt=fp32):
            return ctx.enter_context(nc.sbuf_tensor(name, shape, dt))

        def ps(name, shape):
            return ctx.enter_context(nc.psum_tensor(name, shape, fp32))

        def sem(name):
            return ctx.enter_context(nc.semaphore(name))

        cst = sb("cst", [P, K_END])
        ident = cst[:, K_ID:K_ID + P]
        cos5 = cst[:, K_COS:K_COS + 5 * ROPE].rearrange("p (t r) -> p t r", t=5)
        sin5 = cst[:, K_SIN:K_SIN + 5 * ROPE].rearrange("p (t r) -> p t r", t=5)
        iota_row = cst[:, K_IOTA:K_IOTA + P]
        tri = cst[:, K_TRI:K_TRI + NE * NE].rearrange("p (a b) -> p a b", a=NE)
        identb = sb("identb", [P, P], bf16)
        maskb = sb("maskb", [P, 2 * P], bf16)
        ones = sb("ones", [P, P])
        gamma_b = sb("gamma_b", [P, C])
        beta_b = sb("beta_b", [P, C])
        wlat = sb("wlat", [P, LAT + 3])
        wimp = sb("wimp", [P, 2 * B - 1])
        wq = sb("wq", [P, NH, QW])
        qw_col = sb("qw_col", [CQ, 1])
        kvw_col = sb("kvw_col", [CKV, 1])
        o_b = sb("o_b", [P, NT, NH * VD])
        wqn_raw = o_b[0:CQ, 0, :]
        wkn = o_b[0:CKV, 1, :]
        wqnT = o_b[:, 2, 0:4 * CQ].rearrange("p (c q) -> p c q", c=4)
        wknBD = o_b[:, 3, :].rearrange("p (c q) -> p c q", c=4)
        wv = sb("wv", [P, NH * VD])
        wkw = sb("wkw", [P, NH, HD])
        wks = sb("wks", [P, NH, HD])
        wvw = sb("wvw", [P, NH * VD])
        wvs = sb("wvs", [P, NH * VD])
        wproj = sb("wproj", [P, 4, C])
        rwT = sb("rwT", [P, NE])
        w1 = sb("w1", [P, NE, C])
        w2 = sb("w2", [P, NE // 2, C])
        b1 = sb("b1", [P, NE // 2])
        b2 = sb("b2", [3 * NE, C])
        b2_rest = sb("b2_rest", [3 * NE, C])
        b2_parts = sb("b2_parts", [3 * NE, 3, P], bf16)
        pairsel_in = sb("pairsel_in", [3 * NE, NE // 2, P])
        pairsel = sb("pairsel", [3 * NE, NE // 2, P], bf16)

        h_all = sb("h_all", [P, TILES * C])
        xn_all = sb("xn_all", [P, TILES * C])
        xnT_all = sb("xnT_all", [P, B * T])
        lat_all = sb("lat_all", [P, TILES, LATP])
        gl_all = sb("gl_all", [P, TILES, 3])
        gate_all = sb("gate_all", [P, B, 3])
        rankT = sb("rankT", [P, B, NT])
        cT_all = lat_all[0:3 * NE].rearrange("p n c -> p (n c)")[:, 0:B * T // 2].bitcast(bf16)
        big = sb("big", [P, 3, TILES * C])
        cur = big[:, 0, :]
        scr = big[:, 1:3, :].rearrange("p a n -> p (a n)")
        st = sb("st", [P, 6, 2 * TILES])

        vall = sb("vall", [P, 9, NH * VD])
        oT = sb("oT", [P, 4, T])
        xi = vall[0:B, 0, :].bitcast(i32)
        xf, starts, instr, segst, lastst, argsf, onesr, pos = (vall[0:B, i, :] for i in range(1, 9))
        sc0, sc1, selm, rank = (o_b[0:B, i, :] for i in range(4))
        rankm = oT[0:B, 0, :]
        top8 = oT[0:B, 1, 0:KEEP]
        idx = sb("idx", [P, 3, NT, B], i32)

        lat_b = sb("lat_b", [P, NT, LATP])
        xn_b = sb("xn_b", [P, NT, C])
        xnT_b = sb("xnT_b", [P, T])
        rank_b = sb("rank_b", [P, NT])
        onehot = sb("onehot", [P, NT, KEEP])
        cqT = sb("cqT", [P, T])
        k1n = sb("k1n", [P, T])
        k1T = sb("k1T", [P, T])
        selxT = sb("selxT", [P, KEEP])

        qs = [sb(f"qs{i}", [P, NT, QW]) for i in range(2)]
        kk = [sb(f"kk{i}", [P, 5, P]) for i in range(2)]
        work = big[:].rearrange("p a n -> p (a n)")
        NPR, NRT, NOB = 7 * P, 2 * 5 * ROPE, NT * 3 * VD
        pr = [work[:, i * NPR:(i + 1) * NPR] for i in range(2)]
        pT = [work[:, (2 + i) * NPR:(3 + i) * NPR].bitcast(fp16).rearrange("p (c n) -> p c n", c=2) for i in range(2)]
        rt = [work[:, 4 * NPR + i * NRT:4 * NPR + (i + 1) * NRT].rearrange("p (a t r) -> p a t r", a=2, t=5)
              for i in range(2)]
        obr = [work[:, 4 * NPR + 2 * NRT + i * NOB:4 * NPR + 2 * NRT + (i + 1) * NOB].rearrange("p (t k d) -> p t k d", t=NT, k=3)
               for i in range(2)]
        qT = [sb(f"qT{i}", [P, T]) for i in range(2)]
        kwT = [sb(f"kwT{i}", [P, T]) for i in range(2)]
        ksT = [sb(f"ksT{i}", [P, KEEP]) for i in range(2)]
        vh = [sb(f"vh{i}", [P, 3, 9, VD], bf16) for i in range(2)]
        v_rest = sb("v_rest", [P, 9, VD])
        negm = [sb(f"negm{i}", [P, 3]) for i in range(2)]
        sums = [sb(f"sums{i}", [P, NT, 3]) for i in range(2)]
        rinv = sb("rinv", [P, NT, 3])
        coef = sb("coef", [P, NT, 3])
        osum = sb("osum", [P, NT, VD])

        hT = [vall[:, i, :] for i in range(4)]
        hs = [vall[:, 4 + i, :] for i in range(4)]
        yT = vall[0:C, 8, :]
        cparts = lat_b[:].rearrange("p t c -> p (t c)")[:, 0:TILES * 3 * NE].rearrange("p (n a e) -> p n a e", n=TILES, a=3)
        cpart_b = lat_all[:].rearrange("p n c -> p (n c)")[:, B * T // 2:B * T // 2 + TILES * NE // 2]
        cpart_b = cpart_b.bitcast(bf16).rearrange("p (n e) -> p n e", e=NE)
        y1 = [o_b[:, i, 0:NT * C] for i in range(2)]

        S = [ps(f"S{i}", [P, 1024]) for i in range(2)]
        PT = ps("PT", [P, 1024])
        O = ps("O", [P, 512])
        X = ps("X", [P, 512])

        s = {n: sem(n) for n in [
            "ld_x", "ld_cst", "ld_w", "ld_wimp", "gathered0", "gathered1", "gathered2", "kconst",
            "dve_chain", "pool_chain", 
            "pos_ready", "posT", "idx_ready", "var_ready", "std_ready", "xn_ready",
            "xnT_psum", "xnT_sb", "lat_psum", "lat_sb", "lat_rsqrt", "lat_done", "imp_sb", "imp_psum", "rank_ready", "rank_psum", 
            "gsum_psum", "gexp_in", "gexp_out", "wq_scaled", "wT_psum", "wT_sb", "wabs_psum", "wabs_sb",
            "phaseA", "zero_rows",
            "ld_lat", "ld_rank", "ld_xnT", "onehot_ready", "k1_moved",
            "v_psum", "v_act", "v_dve", "split_step", "v_split",
            "scores_ready", "max_ready", "probs_ready", "pT_psum", "pT_hi", "pT_sb", "pv_done", "comb_done",
            "coef_chain", "osum_part", "osum_done",
            "x_ready", "x_evac", "rope_tmp", "rope_q", "rope_k",
            "oT_psum", "oT_act", "oT_dve", "attn_psum", "h_done",
            "t2_psum", "t2_sb", "rl_psum", "rexp_in", "rexp_out", "comb_ready", "pairsel_ready", "cT_psum", "cT_sb",
            "ffn_h", "ffn_gelu", "ffn_cb", "ffn_hs", "ffn_y", "ffn_yT", "ffn_back", "ffn_out1", "ffn_out", "stored"]}
        block = ctx.enter_context(nc.Block())

        class Chain:

            def __init__(self, eng, name):
                self.eng, self.sem, self.n = eng, s[name], 0

            def link(self, ins):
                ins.then_inc(self.sem, 1)
                self.n += 1
                self.eng.wait_ge(self.sem, self.n)

        VBANK = [S[0][:, 0:512], S[0][:, 512:1024], S[1][:, 0:512], S[1][:, 512:1024]]
        TBANK = [X[0:C, :], S[0][0:C, 0:512]]
        LEAD = ["cq", "k1", "qp0", "qp1", "sel", "kp0", "kp1", "qT0", "kT0", "sT0", "qT1"]
        NX = (NH - 2) * 5 + 2 + len(LEAD)

        def x_index(p, kind):
            return 5 * p + ["sT", "kT", "qp", "kp", "qT"].index(kind)

        def x_lead(kind):
            return LEAD.index(kind) - len(LEAD)

        def xbase(b):
            return b * NX + len(LEAD)

        def kblocks(t):
            return (t + 1) * P, KEEP, (P if t == 0 else 2 * P)

        @block.sync
        def _(sp):
            def ld(dst, src, name):
                sp.dma_start(dst, src).then_inc(s[name], 16)

            ld(xi[:], d["x"], "ld_x")
            ld(pos[:], d["c_pos"], "ld_x")
            ld(cst[:], d["c_cst"], "ld_cst")
            w = "ld_w"
            ld(wqn_raw[:], d["L0_attn_Wq_nope"], w)
            ld(wkn[:], d["L0_attn_Wk_nope"], w)
            ld(qw_col[:], d["L0_attn_q_norm_w"].rearrange("(p o) -> p o", o=1), w)
            ld(kvw_col[:], d["L0_attn_kv_norm_w"].rearrange("(p o) -> p o", o=1), w)
            ld(gamma_b[:], d["L0_tok_gamma"].partition_broadcast(P), w)
            ld(beta_b[:], d["L0_tok_beta"].partition_broadcast(P), w)
            ld(wlat[0:C, 0:CQ], d["L0_attn_Wcq"], w)
            ld(wlat[0:C, CQ:CQ + CKV], d["L0_attn_Wckv"], w)
            ld(wlat[0:C, CQ + CKV:LAT], d["L0_attn_Wk_rope"], w)
            ld(wlat[0:C, LAT:LAT + 3], d["L0_attn_Wgate"], w)
            ld(wq[0:CQ, :, NOPE:HD], d["L0_attn_Wq_rope"].rearrange("c (h r) -> c h r", h=NH), w)
            ld(wq[0:CQ, :, HD:QW], d["L0_attn_Wq_nope"].rearrange("c (h r) -> c h r", h=NH), w)
            ld(wv[0:CKV], d["L0_attn_Wv"], w)
            for dst, name in ((wkw, "L0_attn_Wwin_k"), (wks, "L0_attn_Wsel_k")):
                src = d[name].rearrange("c (h r) -> c h r", h=NH)
                ld(dst[0:C, :, 0:ROPE], src[:, :, NOPE:HD], w)
                ld(dst[0:C, :, ROPE:HD], src[:, :, 0:NOPE], w)
            ld(wvw[0:C], d["L0_attn_Wwin_v"], w)
            ld(wvs[0:C], d["L0_attn_Wsel_v"], w)
            ld(wproj[:], d["L0_attn_Wproj"].rearrange("(c p) n -> p c n", p=P), w)
            ld(rwT[0:C], d["c_rwT"], w)
            ld(w1[0:C], d["L0_ffn_w1"].rearrange("e i o -> i e o"), w)
            ld(w2[:], d["L0_ffn_w2"].rearrange("(c e) i o -> (e i) c o", e=2), w)
            ld(b1[:], d["c_b1T"], w)
            for i in range(3):
                ld(b2[i * NE:(i + 1) * NE, :], d["L0_ffn_b2"], w)
                ld(pairsel_in[i * NE:(i + 1) * NE], d["c_pair"].rearrange("e (c m) -> e c m", c=NE // 2), w)
            sp.wait_ge(s["kconst"], 3)
            ld(wimp[0:C, B - 1:B], d["L0_attn_W_imp"], "ld_wimp")

            sp.wait_ge(s["lat_done"], 2)
            sp.wait_ge(s["xnT_sb"], B)

            def load_latents(b):
                sp.dma_start(lat_b[:], lat_all[:, ds(b * NT, NT), :]).then_inc(s["ld_lat"], 16)
                sp.dma_start(xn_b[:], xn_all[:, ds(b * NT * C, NT * C)].rearrange("p (t c) -> p t c", t=NT)).then_inc(s["ld_lat"], 16)

            def load_ranks(b):
                sp.dma_start(rank_b[:], rankT[:, ds(b, 1), :].rearrange("p a t -> p (a t)")).then_inc(s["ld_rank"], 16)

            def load_rows(b):
                sp.dma_start(xnT_b[0:C], xnT_all[0:C, ds(b * T, T)]).then_inc(s["ld_xnT"], 16)

            load_latents(0)
            load_rows(0)
            sp.wait_ge(s["phaseA"], 1)
            load_ranks(0)
            with sp.Fori(0, B - 1) as b:
                sp.wait_ge(s["x_ready"], xbase(b) + x_lead("sel") + 1)
                load_latents(b + 1)
                load_ranks(b + 1)
                sp.wait_ge(s["x_ready"], xbase(b) + x_index(NH - 3, "kp") + 1)
                load_rows(b + 1)

            out_v = out.rearrange("b (t p) c -> b p t c", p=P)
            with sp.Fori(0, B) as b:
                sp.wait_ge(s["ffn_out"], b + 1)
                sp.dma_start(out_v[ds(b, 1)].rearrange("a p t c -> (a p) t c"),
                             h_all[:, ds(b * NT * C, NT * C)].rearrange("p (t c) -> p t c", t=NT)).then_inc(s["stored"], 16)
            sp.wait_ge(s["stored"], 16 * B)

        @block.gpsimd
        def _(g):
            ch = Chain(g, "pool_chain")
            g.memset(ones[:], 1.0).then_inc(s["kconst"], 1)
            g.memset(wknBD[:], 0.0).then_inc(s["kconst"], 1)
            g.memset(wimp[:], 0.0).then_inc(s["kconst"], 1)
            for i in range(2):
                g.memset(kk[i][:, :, 0:NOPE], 0.0).then_inc(s["kconst"], 1)
            g.memset(lat_all[:, :, LAT:LATP], 0.0).then_inc(s["kconst"], 1)
            g.sem_inc(s["osum_done"], 2)

            g.wait_ge(s["idx_ready"], 1)
            tables = [d["L0_tok_token_emb"], d["L0_tok_instr_emb"], d["L0_tok_arg_emb"]]
            for b in range(B):
                for t in range(NT):
                    for a in range(3):
                        r = (b * NT + t) * C
                        g.indirect_dma_start(
                            out=big[:, a, r:r + C], out_offset=None, in_=tables[a],
                            in_offset=bass.IndirectOffsetOnAxis(ap=idx[:, a, t, b:b + 1], axis=0),
                        ).then_inc(s[f"gathered{[b_lo <= b < b_hi for b_lo, b_hi in PARTS].index(True)}"], 16)

            kr = lat_all[:, :, CQ + CKV:LAT].rearrange("p (b t) r -> p b t r", b=B)
            hf, hb = ROPE // 2, B // 2
            krc, krs = ([buf[i // 2].rearrange("p (b t r) -> p b t r", b=2, t=NT)[:, i % 2] for i in range(hb)]
                        for buf in ([q[:].rearrange("p t q -> p (t q)") for q in qs], [q[:] for q in qT]))
            for half in range(2):
                g.wait_ge(s["lat_sb"], B * (half + 1))
                for i in range(hb):
                    g.tensor_tensor(krc[i], kr[:, half * hb + i], cos5[:, 0:NT, :], ALU.mult)
                    last = g.tensor_tensor(krs[i], kr[:, half * hb + i], sin5[:, 0:NT, :], ALU.mult)
                ch.link(last)
                for i in range(hb):
                    k_ = kr[:, half * hb + i]
                    g.tensor_tensor(k_[:, :, 0:hf], krc[i][:, :, 0:hf], krs[i][:, :, hf:], ALU.subtract)
                    last = g.tensor_tensor(k_[:, :, hf:], krc[i][:, :, hf:], krs[i][:, :, 0:hf], ALU.add)
                ch.link(last)
            g.wait_ge(s["lat_rsqrt"], 1)
            for lo, hi, f in ((0, CQ, st[:, 2, 0:TILES]), (CQ, P, st[:, 2, TILES:])):
                g.tensor_tensor(lat_all[:, :, lo:hi], lat_all[:, :, lo:hi],
                                f.unsqueeze(2).to_broadcast([P, TILES, hi - lo]), ALU.mult).then_inc(s["lat_done"], 1)

            def rope(src, tmp, done, tiles, base_tmp):
                v = src[:, 0:tiles, NOPE:HD]
                g.tensor_tensor(tmp[:, 0, 0:tiles, :], v, cos5[:, 0:tiles, :], ALU.mult)
                g.tensor_tensor(tmp[:, 1, 0:tiles, :], v, sin5[:, 0:tiles, :], ALU.mult).then_inc(s["rope_tmp"], 1)
                g.wait_ge(s["rope_tmp"], base_tmp)
                hf = ROPE // 2
                g.tensor_tensor(src[:, 0:tiles, NOPE:NOPE + hf], tmp[:, 0, 0:tiles, 0:hf], tmp[:, 1, 0:tiles, hf:ROPE], ALU.subtract)
                g.tensor_tensor(src[:, 0:tiles, NOPE + hf:HD], tmp[:, 0, 0:tiles, hf:ROPE], tmp[:, 1, 0:tiles, 0:hf], ALU.add).then_inc(done, 1)

            def rope_q(par, b, hh, x):
                g.wait_ge(s["x_evac"], x + 2)
                rope(qs[par], rt[0], s["rope_q"], NT, b * (2 * NH) + hh * 2 + 1)

            def rope_k(par, b, hh, x):
                g.wait_ge(s["x_evac"], x + 2)
                rope(kk[par], rt[1], s["rope_k"], 5, b * (2 * NH) + hh * 2 + 2)

            def branch_sum(par, b, hh):
                g.wait_ge(s["comb_done"], b * NH + hh + 2)
                g.wait_ge(s["osum_done"], b * NH + hh + 2)
                g.tensor_tensor(osum[:], obr[par][:, :, 0, :], obr[par][:, :, 1, :], ALU.add).then_inc(s["osum_part"], 1)
                g.wait_ge(s["osum_part"], b * NH + hh + 1)
                g.tensor_tensor(o_b[:, :, ds(hh * VD, VD)], osum[:], obr[par][:, :, 2, :], ALU.add).then_inc(s["osum_done"], 1)

            def split_values(par, b, hh):
                H3 = (b * NH + hh) * 3
                V = vall[:, :, ds(hh * VD, VD)]
                g.tensor_copy(vh[par][:, 0], V).then_inc(s["split_step"], 1)
                g.wait_ge(s["split_step"], H3 + 1)
                g.nop(nofuse=True)
                g.tensor_tensor(v_rest[:], V, vh[par][:, 0], ALU.subtract).then_inc(s["split_step"], 1)
                g.wait_ge(s["split_step"], H3 + 2)
                g.nop(nofuse=True)
                g.tensor_copy(vh[par][:, 1], v_rest[:]).then_inc(s["split_step"], 1)
                g.wait_ge(s["split_step"], H3 + 3)
                g.tensor_tensor(vh[par][:, 2], v_rest[:], vh[par][:, 1], ALU.subtract).then_inc(s["v_split"], 1)

            def split_first(b):
                g.wait_ge(s["v_act"], b * 5 + 5)
                g.wait_ge(s["v_dve"], b * 4 + 4)
                g.nop(nofuse=True)
                split_values(0, b, 0)

            rope_q(0, 0, 0, xbase(0) + x_lead("qp0"))
            rope_k(0, 0, 0, xbase(0) + x_lead("kp0"))
            rope_q(1, 0, 1, xbase(0) + x_lead("qp1"))
            rope_k(1, 0, 1, xbase(0) + x_lead("kp1"))
            split_first(0)

            def heads(b):
                with g.Fori(0, NH // 2 - 1) as hp:
                    for par in range(2):
                        split_values(1 - par, b, hp * 2 + (par + 1))
                        rope_q(par, b, hp * 2 + (par + 2), xbase(b) + hp * 10 + x_index(par, "qp"))
                        rope_k(par, b, hp * 2 + (par + 2), xbase(b) + hp * 10 + x_index(par, "kp"))
                        branch_sum(par, b, hp * 2 + par)

            with g.Fori(0, B - 1) as b:
                heads(b)
                split_values(1, b, NH - 1)
                branch_sum(0, b, NH - 2)
                rope_q(0, b + 1, 0, xbase(b + 1) + x_lead("qp0"))
                rope_k(0, b + 1, 0, xbase(b + 1) + x_lead("kp0"))
                rope_q(1, b + 1, 1, xbase(b + 1) + x_lead("qp1"))
                branch_sum(1, b, NH - 1)
                rope_k(1, b + 1, 1, xbase(b + 1) + x_lead("kp1"))
                split_first(b + 1)
            heads(B - 1)
            split_values(1, B - 1, NH - 1)
            branch_sum(0, B - 1, NH - 2)
            branch_sum(1, B - 1, NH - 1)

        @block.scalar
        def _(act):
            def copy(dst, src):
                return nc.scalar.activation(dst, src, ACT.Copy)

            act.sem_inc(s["x_evac"], 1)
            act.sem_inc(s["probs_ready"], 2)
            k = 0
            for b_lo, b_hi in PARTS:
                n = (b_hi - b_lo) * NT
                for _i in range(2):
                    k += 1
                    act.wait_ge(s["var_ready"], k)
                    nc.scalar.activation(st[:, 1, 0:n], st[:, 0, 0:n], ACT.Sqrt).then_inc(s["std_ready"], 1)
                for b in range(b_lo, b_hi):
                    act.wait_ge(s["xnT_psum"], b + 1)
                    copy(xnT_all[0:C, b * T:(b + 1) * T], TBANK[b % 2]).then_inc(s["xnT_sb"], 1)
                for b in range(b_lo, b_hi):
                    for k2 in range(2):
                        act.wait_ge(s["lat_psum"], 2 * b + k2 + 1)
                        src = [S[1], PT][b % 2][:, 512 * k2:512 * k2 + 2 * (LAT + 3)].rearrange("p (t c) -> p t c", t=2)
                        n = b * NT + 2 * k2
                        for t in range(2):
                            row = (n + t) // NT if (n + t) // NT < 7 else 8
                            sq = vall[:, row, (n + t) % NT * P:(n + t) % NT * P + P]
                            nc.scalar.activation(sq[:, 0:CQ], src[:, t, 0:CQ], ACT.Square, accum_out=st[:, 5, n + t:n + t + 1])
                            nc.scalar.activation(sq[:, CQ:P], src[:, t, CQ:P], ACT.Square,
                                                 accum_out=st[:, 5, TILES + n + t:TILES + n + t + 1])
                        copy(gl_all[:, n:n + 2, :], src[:, :, LAT:LAT + 3])
                        copy(lat_all[:, n:n + 2, 0:LAT], src[:, :, 0:LAT]).then_inc(s["lat_sb"], 1)
            act.wait_ge(s["var_ready"], 2 * len(PARTS) + 1)
            nc.scalar.activation(st[:, 1, :], st[:, 0, :], ACT.Sqrt).then_inc(s["std_ready"], 1)
            act.wait_ge(s["gexp_in"], 1)
            nc.scalar.activation(gate_all[:], gate_all[:], ACT.Exp).then_inc(s["gexp_out"], 1)

            def evac(dst, src, x):
                act.wait_ge(s["x_ready"], x + 1)
                copy(dst, src).then_inc(s["x_evac"], 1)

            def evac_q(par, x):
                evac(qs[par][:], X[:, 0:512].rearrange("p (t q) -> p t q", t=NT), x)

            def evac_k(par, x):
                evac(kk[par][:, :, NOPE:P], X[:, 0:5 * HD].rearrange("p (t q) -> p t q", t=5), x)

            def probs(u, t, b, U):
                n1, n2, n3 = kblocks(t)
                par, hp2 = u % 2, (u // 4) % 2
                act.wait_ge(s["max_ready"], U + 1)
                act.wait_ge(s["pT_psum"], U + 1)
                for k, (lo, n) in enumerate(((0, n1), (4 * P, n2), (5 * P, n3))):
                    last = nc.scalar.activation(pr[par][:, lo:lo + n], S[par][:, lo:lo + n], ACT.Exp,
                                                bias=negm[par][:, k:k + 1], accum_out=sums[hp2][:, t, k:k + 1])
                last.then_inc(s["probs_ready"], 1)

            def take_hi(u, t, U):
                par = u % 2
                n1, n2, n3 = kblocks(t)
                act.wait_ge(s["pT_psum"], U + 3)
                act.wait_ge(s["pv_done"], U + 1)
                for lo, n in ((0, n1), (4 * P, P + n3)):
                    nc.scalar.activation(pT[par][:, 0, lo:lo + n], PT[:, lo:lo + n], ACT.Copy, scale=PSCALE).then_inc(s["pT_hi"], 1)

            def turn(b, U, xb, p, last, nxt=None):
                for t in range(NT):
                    u = p * NT + t
                    if t == 0 and last < 2:
                        evac(ksT[1 - p][:], X[:, 0:KEEP], xb + x_index(0, "sT"))
                        evac(kwT[1 - p][:], X[:, 0:T], xb + x_index(0, "kT"))
                    if t == 1 and last < 1:
                        evac_q(p, xb + x_index(0, "qp"))
                    if t == 2 and last < 1:
                        evac_k(p, xb + x_index(0, "kp"))
                    if t == 3 and last < 1:
                        evac(qT[p][:], X[:, 0:T], xb + x_index(0, "qT"))
                    if nxt is not None and last in (1, 2):
                        lead(LEAD[:7], (t - 1 if last == 1 else t + 3), nxt)
                    if last < 2 or t < 3:
                        take_hi(u + 1, (t + 1) % NT, U + t + 1)
                    if nxt is not None and last == 2 and t >= 2:
                        if t == 2:
                            act.wait_ge(s["v_split"], b * NH + NH)
                        value(b + 1, (t - 2) * 2)
                    if last < 2 or t < 1:
                        probs(u + 3, (t + 3) % NT, b, U + t + 3)

            def value(b, i):
                act.wait_ge(s["v_psum"], b * 9 + i + 1)
                copy(vall[:, i, :], VBANK[i % 4]).then_inc(s["v_act"], 1)

            def lead(kinds, i, nxt):
                if not 0 <= i < len(kinds):
                    return
                kind = kinds[i]
                x = nxt + LEAD.index(kind)
                if kind == "cq":
                    evac(cqT[0:CQ], X[0:CQ, 0:T], x)
                elif kind == "k1":
                    evac(k1n[:], X[:, 0:T], x)
                elif kind == "sel":
                    evac(selxT[0:C], X[0:C, 0:KEEP], x)
                elif kind[:2] == "qp":
                    evac_q(int(kind[2]), x)
                elif kind[:2] == "kp":
                    evac_k(int(kind[2]), x)

            def behind(b, nxt, U, first):
                def attended(c):
                    act.wait_ge(s["oT_psum"], (b - 1) * 4 + c + 1)
                    copy(oT[:, c, :], PT[:, 0:512]).then_inc(s["oT_act"], 1)

                evac(qT[0][:], X[:, 0:T], nxt + LEAD.index("qT0"))
                value(b, 4)
                evac(kwT[0][:], X[:, 0:T], nxt + LEAD.index("kT0"))
                value(b, 6)
                evac(ksT[0][:], X[:, 0:KEEP], nxt + LEAD.index("sT0"))
                value(b, 8)
                evac(qT[1][:], X[:, 0:T], nxt + LEAD.index("qT1"))
                if not first:
                    attended(0)
                probs(0, 0, b, U)
                if not first:
                    attended(2)
                probs(1, 1, b, U + 1)
                take_hi(0, 0, U)
                probs(2, 2, b, U + 2)

            for i in range(7):
                lead(LEAD, i, 0)
            value(0, 0)
            value(0, 2)
            behind(0, 0, 0, True)

            def heads(b):
                with act.Fori(0, NH // 2 - 1) as hp:
                    for p in range(2):
                        turn(b, b * (NH * NT) + hp * 8 + p * NT, xbase(b) + hp * 10 + p * 5, p, 0)

            def last_heads(b, nxt):
                for p in range(2):
                    turn(b, b * (NH * NT) + (NH - 2 + p) * NT, xbase(b) + (NH - 2 + p) * 5, p, 1 + p, nxt)

            with act.Fori(0, B - 1) as b:
                heads(b)
                nxt = xbase(b + 1) - len(LEAD)
                last_heads(b, nxt)
                behind(b + 1, nxt, (b + 1) * (NH * NT), False)
            heads(B - 1)
            last_heads(B - 1, None)
            for c in range(0, 4, 2):
                act.wait_ge(s["oT_psum"], (B - 1) * 4 + c + 1)
                copy(oT[:, c, :], PT[:, 0:512]).then_inc(s["oT_act"], 1)

            for b in range(B):
                for i, (b_lo, b_hi) in enumerate(PARTS_FFN):
                    if b == (0, 2)[i]:
                        act.wait_ge(s["var_ready"], 2 * len(PARTS) + 2 + i)
                        n = (b_hi - b_lo) * NT
                        nc.scalar.activation(st[:, 1, 0:n], st[:, 0, 0:n], ACT.Sqrt).then_inc(s["std_ready"], 1)
                act.wait_ge(s["t2_psum"], b + 1)
                copy(xnT_all[0:C, b * T:(b + 1) * T], TBANK[b % 2]).then_inc(s["t2_sb"], 1)
            act.wait_ge(s["rexp_in"], 1)
            nc.scalar.activation(scr[:, 0:TILES * NE], scr[:, 0:TILES * NE], ACT.Exp).then_inc(s["rexp_out"], 1)
            for b in range(B):
                act.wait_ge(s["cT_psum"], b + 1)
                copy(cT_all[:, b * T:(b + 1) * T], PT[0:3 * NE, (b % 2) * 512:(b % 2) * 512 + 512]).then_inc(s["cT_sb"], 1)
            def gelus(b):
                for c in range(4):
                    act.wait_ge(s["ffn_h"], b * 4 + c + 1)
                    act.wait_ge(s["ffn_hs"], b * 4 + c + 1)
                    nc.scalar.activation(hT[c], S[c // 2][:, (c % 2) * 512:(c % 2) * 512 + 512], ACT.Gelu,
                                         bias=b1[:, c:c + 1]).then_inc(s["ffn_gelu"], 1)

            def take_y(b, first):
                act.wait_ge(s["ffn_y"], b + 1)
                if not first:
                    act.wait_ge(s["ffn_back"], b)
                copy(yT, O[0:C, :]).then_inc(s["ffn_yT"], 1)

            gelus(0)
            gelus(1)
            take_y(0, True)
            with act.Fori(0, B - 2) as b:
                gelus(b + 2)
                take_y(b + 1, False)
            take_y(B - 1, False)

        @block.vector
        def _(dve):
            v = nc.vector
            ch = Chain(dve, "dve_chain")
            L = ch.link
            dve.sem_inc(s["comb_done"], 1)
            dve.sem_inc(s["pT_sb"], 1)
            dve.sem_inc(s["ffn_hs"], 4)

            L(v.memset(onesr[:], 1.0))
            L(v.memset(starts[:, 0:1], 0.0))
            dve.wait_ge(s["ld_x"], 32)
            L(v.tensor_copy(xf[:], xi[:]))
            L(v.tensor_scalar(starts[:, 1:T], xf[:, 0:T - 1], float(NEXT_ID), None, ALU.is_equal))
            v.tensor_tensor_scan(instr[:], onesr[:], starts[:], 0.0, ALU.mult, ALU.add)
            L(v.tensor_tensor(segst[:], starts[:], pos[:], ALU.mult))
            L(v.tensor_tensor_scan(lastst[:], onesr[:], segst[:], 0.0, ALU.mult, ALU.max))
            v.tensor_tensor(argsf[:], pos[:], lastst[:], ALU.subtract).then_inc(s["pos_ready"], 1)
            dve.wait_ge(s["posT"], 1)
            v.tensor_copy(idx[:], X[:, 0:3 * NT * B].rearrange("p (a t b) -> p a t b", a=3, t=NT)).then_inc(s["idx_ready"], 1)

            dve.wait_ge(s["ld_cst"], 16)
            v.tensor_copy(identb[:], ident)
            L(v.tensor_copy(maskb[:], cst[:, K_MASK:K_MASK + 2 * P]))
            dve.wait_ge(s["ld_w"], 16 * N_W)
            sm = float(HD) ** -0.5
            L(v.tensor_scalar(qw_col[:], qw_col[:], sm, None, ALU.mult))
            v.tensor_scalar(wq[0:CQ, :, NOPE:QW], wq[0:CQ, :, NOPE:QW], qw_col[:], None, ALU.mult)
            v.tensor_scalar(wqn_raw[:], wqn_raw[:], qw_col[:], None, ALU.mult)
            v.tensor_scalar(wkn[:], wkn[:], kvw_col[:], None, ALU.mult)
            v.tensor_scalar(wv[0:CKV], wv[0:CKV], kvw_col[:], None, ALU.mult)
            v.tensor_scalar(wlat[0:C, CQ + CKV:LAT], wlat[0:C, CQ + CKV:LAT], 1.0 / NH, None, ALU.mult).then_inc(s["wq_scaled"], 1)
            dve.wait_ge(s["wT_psum"], 1)
            v.tensor_copy(wqnT[:], S[0][:, 0:4 * CQ].rearrange("p (c q) -> p c q", c=4))
            dve.wait_ge(s["kconst"], 6)
            for g_ in range(4):
                last = v.tensor_copy(wknBD[32 * g_:32 * g_ + 32, :, 32 * g_:32 * g_ + 32],
                                     S[0][32 * g_:32 * g_ + 32, 512:512 + 4 * CKV].rearrange("p (c q) -> p c q", c=4))
            last.then_inc(s["wT_sb"], 1)
            dve.wait_ge(s["wabs_psum"], 1)
            v.tensor_copy(wq[0:CQ, :, 0:NOPE], S[1][0:CQ, 0:512].rearrange("p (h q) -> p h q", h=NH)).then_inc(s["wabs_sb"], 1)

            for buf, rows in ((xnT_all, C), (wlat, C), (wq, CQ), (wv, CKV), (wkw, C), (wks, C), (wvw, C), (wvs, C),
                              (rwT, C), (w1, C), (xnT_b, C), (cqT, CQ), (selxT, C)):
                if rows == CKV:
                    v.memset(buf[CKV:C], 0.0)
                    rows = C
                last = v.memset(buf[rows:P], 0.0)
            last.then_inc(s["zero_rows"], 1)

            def bc(ap, shape):
                return ap.to_broadcast(shape)

            def rsqrt(n, k):
                a, r, y, z = (st[:, i, 0:n] for i in (0, 1, 2, 3))
                dve.wait_ge(s["std_ready"], k)
                L(v.reciprocal(y, r))
                L(v.tensor_tensor(z, y, y, ALU.mult))
                L(v.tensor_tensor(z, z, a, ALU.mult))
                L(v.tensor_scalar(z, z, -0.5, 1.5, ALU.mult, ALU.add))
                L(v.tensor_tensor(y, y, z, ALU.mult))

            def layernorm(dst, src, k, n0=0, n1=TILES):
                n = n1 - n0
                s3, d3, q3 = (x[:, n0 * C:n1 * C].rearrange("p (n c) -> p n c", c=C) for x in (src, dst, scr))
                m = st[:, 4, 0:n]
                L(v.tensor_reduce(m, s3, op=ALU.add, axis=AX.X))
                L(v.tensor_scalar(m, m, 1.0 / C, None, ALU.mult))
                L(v.tensor_tensor(d3, s3, bc(m.unsqueeze(2), [P, n, C]), ALU.subtract))
                L(v.tensor_tensor(q3, d3, d3, ALU.mult))
                L(v.tensor_reduce(st[:, 0, 0:n], q3, op=ALU.add, axis=AX.X))
                ins = v.tensor_scalar(st[:, 0, 0:n], st[:, 0, 0:n], 1.0 / C, 1e-5, ALU.mult, ALU.add)
                ins.then_inc(s["var_ready"], 1)
                rsqrt(n, k)
                return v.tensor_tensor(d3, d3, bc(st[:, 2, 0:n].unsqueeze(2), [P, n, C]), ALU.mult)

            for i, (b_lo, b_hi) in enumerate(PARTS):
                n0, n1 = b_lo * NT, b_hi * NT
                cols = slice(n0 * C, n1 * C)
                dve.wait_ge(s[f"gathered{i}"], 16 * 3 * (n1 - n0))
                L(v.tensor_tensor(cur[:, cols], cur[:, cols], big[:, 1, cols], ALU.add))
                L(v.tensor_tensor(cur[:, cols], cur[:, cols], big[:, 2, cols], ALU.add))
                L(layernorm(h_all, cur, 2 * i + 1, n0, n1))
                h3 = h_all[:, cols].rearrange("p (n c) -> p n c", c=C)
                L(v.tensor_tensor(h3, h3, bc(gamma_b[:].unsqueeze(1), [P, n1 - n0, C]), ALU.mult))
                L(v.tensor_tensor(h3, h3, bc(beta_b[:].unsqueeze(1), [P, n1 - n0, C]), ALU.add))
                layernorm(xn_all, h_all, 2 * i + 2, n0, n1).then_inc(s["xn_ready"], 1)

            def latent_factors():
                dve.wait_ge(s["lat_sb"], 2 * B)
                v.tensor_scalar(st[:, 0, 0:TILES], st[:, 5, 0:TILES], 1.0 / CQ, 1e-6, ALU.mult, ALU.add)
                v.tensor_scalar(st[:, 0, TILES:], st[:, 5, TILES:], 1.0 / CKV, 1e-6, ALU.mult, ALU.add).then_inc(s["var_ready"], 1)
                rsqrt(2 * TILES, 2 * len(PARTS) + 1)
                dve.sem_inc(s["lat_rsqrt"], 1)

            def gates_in():
                dve.wait_ge(s["gsum_psum"], 1)
                L(v.tensor_reduce(gate_all[:], O[:, 0:TILES * 3].rearrange("p (b t g) -> p b g t", b=B, t=NT), op=ALU.add, axis=AX.X))
                L(v.tensor_reduce(st[:, 4, 0:B], gate_all[:], op=ALU.max, axis=AX.X))
                L(v.tensor_tensor(gate_all[:], gate_all[:], bc(st[:, 4, 0:B].unsqueeze(2), [P, B, 3]), ALU.subtract))
                v.tensor_scalar(gate_all[:], gate_all[:], 1.0 / T, None, ALU.mult).then_inc(s["gexp_in"], 1)

            def gates_out():
                dve.wait_ge(s["gexp_out"], 1)
                L(v.tensor_reduce(st[:, 4, 0:B], gate_all[:], op=ALU.add, axis=AX.X))
                L(v.reciprocal(st[:, 5, 0:B], st[:, 4, 0:B]))
                L(v.tensor_scalar(st[:, 5, 0:B], st[:, 5, 0:B], 1.0 / PSCALE, None, ALU.mult))
                L(v.tensor_tensor(gate_all[:], gate_all[:], bc(st[:, 5, 0:B].unsqueeze(2), [P, B, 3]), ALU.mult))

            dve.wait_ge(s["imp_psum"], B)
            L(v.tensor_copy(sc0[:], O[0:B, :]))
            dve.sem_inc(s["imp_sb"], 1)
            a, z = sc0, sc1
            for r in range(KEEP // 8):
                m8 = top8[:, 8 * r:8 * r + 8]
                L(v.max(m8, a[:]))
                L(v.match_replace(z[:], m8, a[:], NEG))
                a, z = z, a
                if r == 7:
                    latent_factors()
                if r == 9:
                    gates_in()
                if r == 12:
                    gates_out()
            L(v.tensor_scalar(selm[:], a[:], NEG, None, ALU.is_equal))
            L(v.tensor_tensor_scan(rank[:], onesr[:], selm[:], 0.0, ALU.mult, ALU.add))
            L(v.tensor_tensor(rankm[:], rank[:], selm[:], ALU.mult))
            v.tensor_scalar(rankm[:], rankm[:], -1.0, None, ALU.add).then_inc(s["rank_ready"], 1)
            dve.wait_ge(s["rank_psum"], 1)
            v.tensor_copy(rankT[:], S[0][:, 0:NT * B].rearrange("p (t b) -> p b t", t=NT)).then_inc(s["phaseA"], 1)

            def maxima(u, t, U):
                par = u % 2
                n1, n2, n3 = kblocks(t)
                dve.wait_ge(s["scores_ready"], U + 1)
                v.tensor_reduce(negm[par][:, 0:1], S[par][:, 0:n1], op=ALU.max, axis=AX.X, negate=True)
                v.tensor_reduce(negm[par][:, 1:2], S[par][:, 4 * P:4 * P + n2], op=ALU.max, axis=AX.X, negate=True)
                v.tensor_reduce(negm[par][:, 2:3], S[par][:, 5 * P:5 * P + n3], op=ALU.max, axis=AX.X, negate=True).then_inc(s["max_ready"], 1)

            def take_lo(u, t, U):
                par = u % 2
                n1, n2, n3 = kblocks(t)
                for k, (lo, n) in enumerate(((0, n1), (4 * P, P + n3))):
                    dve.wait_ge(s["pT_hi"], 2 * U + k + 1)
                    last = v.scalar_tensor_tensor(pT[par][:, 1, lo:lo + n], PT[:, lo:lo + n], PSCALE, pT[par][:, 0, lo:lo + n],
                                                  ALU.mult, ALU.subtract)
                last.then_inc(s["pT_sb"], 1)

            def combine(par, b, H):
                dve.wait_ge(s["probs_ready"], H * NT + 6)
                v.reciprocal(rinv[:], sums[par][:]).then_inc(s["coef_chain"], 1)
                dve.wait_ge(s["coef_chain"], H * 2 + 1)
                v.tensor_tensor(coef[:], rinv[:], bc(gate_all[:, ds(b, 1), :], [P, NT, 3]), ALU.mult).then_inc(s["coef_chain"], 1)
                dve.wait_ge(s["coef_chain"], H * 2 + 2)
                dve.wait_ge(s["osum_done"], H + 1)
                dve.wait_ge(s["pv_done"], H * NT + 6)
                v.tensor_tensor(obr[par][:].rearrange("p t k d -> p (t k) d"),
                                O[:, 0:NT * 3 * VD].rearrange("p (a d) -> p a d", d=VD),
                                bc(coef[:].rearrange("p t k -> p (t k)").unsqueeze(2), [P, NT * 3, VD]),
                                ALU.mult).then_inc(s["comb_done"], 1)

            def value(b, i):
                dve.wait_ge(s["v_psum"], b * 9 + i + 1)
                v.tensor_copy(vall[:, i, :], VBANK[i % 4]).then_inc(s["v_dve"], 1)

            def turn(b, H, p, last, more=False):
                U = H * NT
                for t in range(NT):
                    u = p * NT + t
                    if last < 2 or t < 1:
                        maxima(u + 3, (t + 3) % NT, U + t + 3)
                    if last < 2 or t < 3:
                        take_lo(u + 1, (t + 1) % NT, U + t + 1)
                    if more and t >= 2:
                        if t == 2:
                            dve.wait_ge(s["v_split"], H + 1)
                        value(b + 1, (t - 2) * 2 + 1)
                combine(p, b, H)

            def mark_selected(b):
                dve.wait_ge(s["ld_rank"], b * 16 + 16)
                v.tensor_tensor(onehot[:], bc(iota_row.unsqueeze(1), [P, NT, KEEP]),
                                bc(rank_b[:].unsqueeze(2), [P, NT, KEEP]), ALU.is_equal).then_inc(s["onehot_ready"], 1)

            def attended(b, c):
                dve.wait_ge(s["oT_psum"], b * 4 + c + 1)
                v.tensor_copy(oT[:, c, :], PT[:, 512:1024]).then_inc(s["oT_dve"], 1)

            def residual(b):
                dve.wait_ge(s["attn_psum"], b + 1)
                hb = h_all[:, ds(b * (NT * C), NT * C)]
                v.tensor_tensor(hb, O[:, 0:NT * C], hb, ALU.add).then_inc(s["h_done"], 1)

            def behind(b, U, first):
                dve.wait_ge(s["x_evac"], xbase(b) + x_lead("k1") + 2)
                v.tensor_copy(k1T[:], k1n[:]).then_inc(s["k1_moved"], 1)
                value(b, 5)
                value(b, 7)
                if not first:
                    attended(b - 1, 1)
                maxima(0, 0, U)
                if not first:
                    attended(b - 1, 3)
                maxima(1, 1, U + 1)
                if not first:
                    residual(b - 1)
                maxima(2, 2, U + 2)
                take_lo(0, 0, U)

            mark_selected(0)
            value(0, 1)
            value(0, 3)
            behind(0, 0, True)

            def heads(b):
                with dve.Fori(0, NH // 2 - 1) as hp:
                    turn(b, b * NH + hp * 2, 0, 0)
                    turn(b, b * NH + hp * 2 + 1, 1, 0)

            with dve.Fori(0, B - 1) as b:
                heads(b)
                mark_selected(b + 1)
                turn(b, b * NH + (NH - 2), 0, 1)
                turn(b, b * NH + (NH - 1), 1, 2, True)
                behind(b + 1, (b + 1) * (NH * NT), False)
            heads(B - 1)
            turn(B - 1, B * NH - 2, 0, 1)
            turn(B - 1, B * NH - 1, 1, 2)
            attended(B - 1, 1)
            attended(B - 1, 3)
            residual(B - 1)

            dve.wait_ge(s["h_done"], B)
            for i, (b_lo, b_hi) in enumerate(PARTS_FFN):
                layernorm(xn_all, h_all, 2 * len(PARTS) + 2 + i, b_lo * NT, b_hi * NT).then_inc(s["xn_ready"], 1)
            n = TILES * NE
            e3 = scr[:, 0:n].rearrange("p (n e) -> p n e", e=NE)
            c3 = scr[:, n:2 * n].rearrange("p (n e) -> p n e", e=NE)
            big4 = big[:, 0, :].rearrange("p (n a e) -> p n a e", n=TILES, a=NE)
            eq4 = big[:, 2, :].rearrange("p (n a e) -> p n a e", n=TILES, a=NE)
            m = st[:, 4, 0:TILES]
            r3 = st[:, 5, 0:TILES]
            dve.wait_ge(s["rl_psum"], B)
            l3 = PT[:, 0:n].rearrange("p (n e) -> p n e", e=NE)
            L(v.tensor_reduce(m, l3, op=ALU.max, axis=AX.X))
            v.tensor_tensor(e3, l3, bc(m.unsqueeze(2), [P, TILES, NE]), ALU.subtract).then_inc(s["rexp_in"], 1)
            dve.wait_ge(s["rexp_out"], 1)
            L(v.tensor_reduce(m, e3, op=ALU.add, axis=AX.X))
            L(v.reciprocal(r3, m))
            L(v.tensor_tensor(e3, e3, bc(r3.unsqueeze(2), [P, TILES, NE]), ALU.mult))
            for a_ in range(NE):
                mine = bc(e3[:, :, a_:a_ + 1], [P, TILES, NE])
                v.tensor_tensor(big4[:, :, a_, :], e3, mine, ALU.is_gt)
                last = v.tensor_tensor(eq4[:, :, a_, :], e3, mine, ALU.is_equal)
            L(last)
            for a_ in range(NE):
                last = v.tensor_tensor(eq4[:, :, a_, :], eq4[:, :, a_, :], bc(tri[:, a_:a_ + 1, :], [P, TILES, NE]), ALU.mult)
            L(last)
            L(v.tensor_tensor(big[:, 0, :], big[:, 0, :], big[:, 2, :], ALU.add))
            L(v.tensor_reduce(c3, big4, op=ALU.add, axis=AX.X))
            L(v.tensor_scalar(c3, c3, 2.0, None, ALU.is_lt))
            L(v.tensor_tensor(c3, c3, e3, ALU.mult))
            L(v.tensor_reduce(m, c3, op=ALU.add, axis=AX.X))
            L(v.tensor_scalar(m, m, 1e-12, None, ALU.max))
            L(v.reciprocal(r3, m))
            L(v.tensor_tensor(c3, c3, bc(r3.unsqueeze(2), [P, TILES, NE]), ALU.mult))
            for i in range(2):
                L(v.tensor_copy(cpart_b, c3))
                L(v.tensor_copy(cparts[:, :, i, :], cpart_b))
                last = v.tensor_tensor(c3 if i == 0 else cparts[:, :, 2, :], c3, cparts[:, :, i, :], ALU.subtract)
                if i == 0:
                    L(last)
            last.then_inc(s["comb_ready"], 1)
            L(v.memset(b2_parts[:], 0.0))
            L(v.tensor_copy(b2_parts[:, 0, 0:C], b2[:]))
            L(v.tensor_tensor(b2_rest[:], b2[:], b2_parts[:, 0, 0:C], ALU.subtract))
            L(v.tensor_copy(b2_parts[:, 1, 0:C], b2_rest[:]))
            v.tensor_tensor(b2_parts[:, 2, 0:C], b2_rest[:], b2_parts[:, 1, 0:C], ALU.subtract)
            v.tensor_copy(pairsel[:], pairsel_in[:]).then_inc(s["pairsel_ready"], 1)

            def expert_scale(b):
                for c in range(4):
                    dve.wait_ge(s["ffn_cb"], b * 4 + c + 1)
                    dve.wait_ge(s["ffn_gelu"], b * 4 + c + 1)
                    v.tensor_tensor(hs[c], hT[c], PT[:, (c % 2) * 512:(c % 2) * 512 + 512], ALU.mult).then_inc(s["ffn_hs"], 1)

            def finish(b, y):
                dve.wait_ge(s["ffn_back"], b + 1)
                v.tensor_tensor(y, X[:, 0:NT * C], xn_all[:, ds(b * (NT * C), NT * C)], ALU.add).then_inc(s["ffn_out1"], 1)
                dve.wait_ge(s["ffn_out1"], b + 1)
                hb = h_all[:, ds(b * (NT * C), NT * C)]
                v.tensor_tensor(hb, y, hb, ALU.add).then_inc(s["ffn_out"], 1)

            expert_scale(0)
            with dve.Fori(0, B - 1) as b:
                expert_scale(b + 1)
                finish(b, y1[0])
            finish(B - 1, y1[1])

        @block.tensor
        def _(pe):
            mm, tp = nc.tensor.matmul, nc.tensor.transpose
            pe.sem_inc(s["pv_done"], 2)
            pe.sem_inc(s["pT_psum"], 2)

            pe.wait_ge(s["ld_cst"], 16)
            pe.wait_ge(s["pos_ready"], 1)
            for a, src in enumerate((xf, instr, argsf)):
                for t in range(NT):
                    o = (a * NT + t) * B
                    last = tp(X[:, o:o + B], src[:, t * P:(t + 1) * P], cst[0:B, 0:B])
            last.then_inc(s["posT"], 1)

            pe.wait_ge(s["wq_scaled"], 1)
            for c in range(4):
                tp(S[0][:, c * CQ:(c + 1) * CQ], wqn_raw[:, c * P:(c + 1) * P], cst[0:CQ, 0:CQ])
            for c in range(4):
                last = tp(S[0][:, 512 + c * CKV:512 + (c + 1) * CKV], wkn[:, c * P:(c + 1) * P], cst[0:CKV, 0:CKV])
            last.then_inc(s["wT_psum"], 1)
            pe.wait_ge(s["wT_sb"], 1)
            for c in range(4):
                last = mm(S[1][0:CQ, c * P:(c + 1) * P], wqnT[:, c, :], wknBD[:, c, :], start=True, stop=True)
            last.then_inc(s["wabs_psum"], 1)
            pe.wait_ge(s["wabs_sb"], 1)

            def transposes(name, sb_name, b_lo=0, b_hi=B, behind_evac=None):
                for b in range(b_lo, b_hi):
                    if b >= 2:
                        pe.wait_ge(s[sb_name], b - 1)
                    for t in range(NT):
                        n_ = (b * NT + t) * C
                        last = tp(TBANK[b % 2][:, t * P:(t + 1) * P], xn_all[:, n_:n_ + C], ident)
                    last.then_inc(s[name], 1)
                    if behind_evac is not None and b >= 1:
                        pe.wait_ge(s[sb_name], b)
                        behind_evac(b - 1)

            pe.wait_ge(s["idx_ready"], 1)
            pe.wait_ge(s["ld_wimp"], 16)
            pe.wait_ge(s["zero_rows"], 1)
            for i, (b_lo, b_hi) in enumerate(PARTS):
                pe.wait_ge(s["xn_ready"], i + 1)
                transposes("xnT_psum", "xnT_sb", b_lo, b_hi)
                for b in range(b_lo, b_hi):
                    pe.wait_ge(s["xnT_sb"], b + 1)
                    mm(O[0:B, :], wimp[:, B - 1 - b:2 * B - 1 - b], xnT_all[:, b * T:(b + 1) * T], start=(b == 0),
                       stop=(b == B - 1)).then_inc(s["imp_psum"], 1)
                for b in range(b_lo, b_hi):
                    if b >= 2:
                        pe.wait_ge(s["lat_sb"], 2 * (b - 1))
                    for t in range(NT):
                        n_ = (b * NT + t) * P
                        o = (t // 2) * 512 + (t % 2) * (LAT + 3)
                        last = mm([S[1], PT][b % 2][:, o:o + LAT + 3], xnT_all[:, n_:n_ + P], wlat[:], start=True, stop=True)
                        if t % 2:
                            last.then_inc(s["lat_psum"], 1)
            pe.wait_ge(s["lat_sb"], 2 * B)
            pe.wait_ge(s["imp_sb"], 1)
            mm(O[:, 0:TILES * 3], ones[:], gl_all[:].rearrange("p n g -> p (n g)"), start=True, stop=True).then_inc(s["gsum_psum"], 1)

            def x_wait(x):
                pe.wait_ge(s["x_evac"], x + 1)

            def q_proj(h, x):
                x_wait(x)
                for t in range(NT):
                    last = mm(X[:, t * QW:(t + 1) * QW], cqT[:, t * P:(t + 1) * P],
                              wq[:].rearrange("c h q -> c (h q)")[:, ds(h * QW, QW)], start=True, stop=True)
                last.then_inc(s["x_ready"], 1)

            def k_proj(h, x):
                x_wait(x)
                pe.nop(nofuse=True)
                for t in range(NT):
                    mm(X[:, t * HD:(t + 1) * HD], xnT_b[:, t * P:(t + 1) * P],
                       wkw[:].rearrange("c h q -> c (h q)")[:, ds(h * HD, HD)], start=True, stop=True)
                mm(X[:, NT * HD:5 * HD], selxT[:], wks[:].rearrange("c h q -> c (h q)")[:, ds(h * HD, HD)],
                   start=True, stop=True).then_inc(s["x_ready"], 1)

            def q_turn(par, x, H):
                x_wait(x)
                pe.wait_ge(s["rope_q"], H + 1)
                for t in range(NT):
                    last = tp(X[:, t * P:(t + 1) * P], qs[par][:, t, :], ident)
                last.then_inc(s["x_ready"], 1)

            def k_turn(par, x, H):
                x_wait(x)
                pe.wait_ge(s["rope_k"], H + 1)
                for t in range(NT):
                    last = tp(X[:, t * P:(t + 1) * P], kk[par][:, t, :], ident)
                last.then_inc(s["x_ready"], 1)

            def s_turn(par, x, H):
                x_wait(x)
                pe.wait_ge(s["rope_k"], H + 1)
                tp(X[:, 0:P], kk[par][:, 4, :], ident).then_inc(s["x_ready"], 1)

            def lead(kind, b, nxt):
                x = nxt + LEAD.index(kind)
                if kind == "cq":
                    x_wait(x)
                    pe.wait_ge(s["ld_lat"], b * 32 + 32)
                    for t in range(NT):
                        last = tp(X[0:CQ, t * P:(t + 1) * P], lat_b[:, t, 0:CQ], ident)
                    last.then_inc(s["x_ready"], 1)
                elif kind == "k1":
                    x_wait(x)
                    for t in range(NT):
                        last = tp(X[:, t * P:(t + 1) * P], lat_b[:, t, CQ:LATP], ident)
                    last.then_inc(s["x_ready"], 1)
                elif kind == "sel":
                    x_wait(x)
                    pe.wait_ge(s["onehot_ready"], b + 1)
                    for t in range(NT):
                        last = mm(X[0:C, 0:KEEP], xn_b[:, t, :], onehot[:, t, :], start=(t == 0), stop=(t == NT - 1))
                    last.then_inc(s["x_ready"], 1)
                elif kind[:2] == "qp":
                    q_proj(int(kind[2]), x)
                elif kind[:2] == "kp":
                    pe.wait_ge(s["ld_xnT"], b * 16 + 16)
                    k_proj(int(kind[2]), x)

            def scores(u, t, par, U):
                pe.wait_ge(s["probs_ready"], U + 1)
                z = S[u % 2]
                n1, n2, n3 = kblocks(t)
                q = qT[par][:, t * P:(t + 1) * P]
                mm(z[:, 0:n1], q, k1T[:, 0:n1], start=True, stop=True)
                mm(z[:, n1 - P:n1], identb[:], maskb[:, P:2 * P], start=False, stop=True, skip_group_check=True)
                mm(z[:, 4 * P:5 * P], q, ksT[par][:], start=True, stop=True)
                mm(z[:, 5 * P:5 * P + n3], q, kwT[par][:, (t + 1) * P - n3:(t + 1) * P], start=True, stop=True)
                mm(z[:, 5 * P:5 * P + n3], identb[:], maskb[:, 2 * P - n3:2 * P], start=False, stop=True,
                   skip_group_check=True).then_inc(s["scores_ready"], 1)

            def turn_probs(u, t, U):
                pe.wait_ge(s["probs_ready"], U + 3)
                pe.wait_ge(s["pT_sb"], U + 1)
                n1, n2, n3 = kblocks(t)
                src = pr[u % 2]
                for lo in list(range(0, n1, P)) + list(range(4 * P, 5 * P + n3, P)):
                    last = tp(PT[:, lo:lo + P], src[:, lo:lo + P], ident)
                last.then_inc(s["pT_psum"], 1)

            def values(u, t, p, U, first):
                pe.wait_ge(s["pT_sb"], U + 2)
                if t == 0:
                    pe.wait_ge(s["comb_done"], first + 1)
                    pe.wait_ge(s["v_split"], first + 1)
                w = pT[u % 2]
                for k, (blocks, v0) in enumerate((([0, 1, 2, 3][:t + 1], 0), ([4], 8),
                                                  ([5] if t == 0 else [5, 6], 4 + max(t - 1, 0)))):
                    o = O[:, (t * 3 + k) * VD:(t * 3 + k + 1) * VD]
                    parts = [(i, c, a) for i in range(len(blocks)) for c, a in ((0, 0), (0, 1), (0, 2), (1, 0), (1, 1))]
                    for j, (i, c, a) in enumerate(parts):
                        last = mm(o, w[:, c, blocks[i] * P:(blocks[i] + 1) * P],
                                  vh[p][:, a, v0 + i, :],
                                  start=(j == 0), stop=(j == len(parts) - 1))
                last.then_inc(s["pv_done"], 1)

            def turn(h, H, xb, p, last, b=None, nxt=None):
                U = H * NT
                for t in range(NT):
                    u = p * NT + t
                    if last < 2 and t == 0:
                        s_turn(1 - p, xb + x_index(0, "sT"), H + 1)
                    if last < 1 and t == 1:
                        q_proj(h + 2, xb + x_index(0, "qp"))
                    if last < 1 and t == 2:
                        k_proj(h + 2, xb + x_index(0, "kp"))
                    if last < 1 and t == 3:
                        q_turn(p, xb + x_index(0, "qT"), H + 2)
                    i = t - 1 if last == 1 else t + 3
                    if nxt is not None and 0 <= i < 7:
                        lead(LEAD[i], b, nxt)
                    if last < 2 or t < 1:
                        if t == 1:
                            pe.wait_ge(s["x_evac"], xb + x_index(0, "kT") + 2)
                        scores(u + 3, (t + 3) % NT, p if t < 1 else 1 - p, U + t + 3)
                    if last < 2 and t == 0:
                        k_turn(1 - p, xb + x_index(0, "kT"), H + 1)
                    if last < 2 or t < 3:
                        turn_probs(u + 1, (t + 1) % NT, U + t + 1)
                    if nxt is not None and last == 2 and t >= 2:
                        value(b, (t - 2) * 2)
                        value(b, (t - 2) * 2 + 1)
                    values(u, t, p, U + t, H)

            def value(b, i):
                if i >= 4 and i % 2 == 0:
                    pe.wait_ge(s["v_act"], b * 5 + (i - 4) // 2 + 1)
                if i >= 4 and i % 2 == 1:
                    pe.wait_ge(s["v_dve"], b * 4 + (i - 5) // 2 + 1)
                if i < 4:
                    lhs, rhs = k1n[:, i * P:(i + 1) * P], wv[:]
                elif i < 8:
                    lhs, rhs = xnT_b[:, (i - 4) * P:(i - 3) * P], wvw[:]
                else:
                    lhs, rhs = selxT[:], wvs[:]
                mm(VBANK[i % 4], lhs, rhs, start=True, stop=True).then_inc(s["v_psum"], 1)

            def behind(b, nxt, H, first):
                def attended(c):
                    if c >= 2:
                        pe.wait_ge(s[["oT_act", "oT_dve"][c % 2]], (b - 1) * 2 + 1)
                    for t in range(NT):
                        last = tp(PT[:, (c % 2) * 512 + t * P:(c % 2) * 512 + (t + 1) * P], o_b[:, t, c * P:(c + 1) * P], ident)
                    last.then_inc(s["oT_psum"], 1)

                q_turn(0, nxt + LEAD.index("qT0"), H)
                value(b, 4)
                value(b, 5)
                k_turn(0, nxt + LEAD.index("kT0"), H)
                value(b, 6)
                value(b, 7)
                s_turn(0, nxt + LEAD.index("sT0"), H)
                value(b, 8)
                q_turn(1, nxt + LEAD.index("qT1"), H + 1)
                if not first:
                    pe.wait_ge(s["osum_done"], H + 2)
                    pe.wait_ge(s["pT_sb"], H * NT + 1)
                    attended(0)
                    attended(1)
                pe.wait_ge(s["v_act"], b * 5 + 5)
                pe.wait_ge(s["v_dve"], b * 4 + 4)
                pe.wait_ge(s["k1_moved"], b + 1)
                pe.wait_ge(s["x_evac"], nxt + LEAD.index("sT0") + 2)
                scores(0, 0, 0, H * NT)
                if not first:
                    attended(2)
                    attended(3)
                scores(1, 1, 0, H * NT + 1)
                if not first:
                    project(b - 1, H)
                scores(2, 2, 0, H * NT + 2)
                turn_probs(0, 0, H * NT)

            def project(b, H):
                pe.wait_ge(s["comb_done"], H + 1)
                pe.wait_ge(s["oT_act"], b * 2 + 2)
                pe.wait_ge(s["oT_dve"], b * 2 + 2)
                for t in range(NT):
                    for c in range(4):
                        last = mm(O[:, t * C:(t + 1) * C], oT[:, c, t * P:(t + 1) * P], wproj[:, c, :], start=(c == 0), stop=(c == 3))
                last.then_inc(s["attn_psum"], 1)

            def heads(b):
                with pe.Fori(0, NH // 2 - 1) as hp:
                    for p in range(2):
                        turn(hp * 2 + p, b * NH + hp * 2 + p, xbase(b) + hp * 10 + p * 5, p, 0)

            for kind in LEAD[:4]:
                lead(kind, 0, 0)
            pe.wait_ge(s["rank_ready"], 1)
            for t in range(NT):
                last = tp(S[0][:, t * B:(t + 1) * B], rankm[:, t * P:(t + 1) * P], cst[0:B, 0:B])
            last.then_inc(s["rank_psum"], 1)
            for kind in LEAD[4:7]:
                lead(kind, 0, 0)
            for i in range(4):
                value(0, i)
            behind(0, 0, 0, True)
            with pe.Fori(0, B - 1) as b:
                heads(b)
                nxt = xbase(b + 1) - len(LEAD)
                for p in range(2):
                    turn(NH - 2 + p, b * NH + (NH - 2 + p), xbase(b) + (NH - 2 + p) * 5, p, 1 + p, b + 1, nxt)
                behind(b + 1, nxt, (b + 1) * NH, False)
                pe.wait_ge(s["h_done"], b + 1)
            heads(B - 1)
            for p in range(2):
                turn(NH - 2 + p, B * NH - 2 + p, xbase(B - 1) + (NH - 2 + p) * 5, p, 1 + p)
            pe.wait_ge(s["osum_done"], B * NH + 2)
            pe.wait_ge(s["pT_sb"], B * NH * NT + 1)
            for c in range(4):
                if c >= 2:
                    pe.wait_ge(s[["oT_act", "oT_dve"][c % 2]], (B - 1) * 2 + 1)
                for t in range(NT):
                    last = tp(PT[:, (c % 2) * 512 + t * P:(c % 2) * 512 + (t + 1) * P], o_b[:, t, c * P:(c + 1) * P], ident)
                last.then_inc(s["oT_psum"], 1)
            project(B - 1, B * NH)
            pe.wait_ge(s["h_done"], B)

            pe.wait_ge(s["x_evac"], xbase(B) - len(LEAD) + 1)

            def router(b):
                for n_ in range(b * NT, b * NT + NT):
                    last = mm(PT[:, n_ * NE:(n_ + 1) * NE], xnT_all[:, n_ * P:(n_ + 1) * P], rwT[:], start=True, stop=True)
                last.then_inc(s["rl_psum"], 1)

            for i, (b_lo, b_hi) in enumerate(PARTS_FFN):
                pe.wait_ge(s["xn_ready"], len(PARTS) + 1 + i)
                transposes("t2_psum", "t2_sb", b_lo, b_hi, router)
            pe.wait_ge(s["t2_sb"], B)
            router(B - 1)

            def hidden(b, waits=True, between=None):
                for c in range(4):
                    if waits:
                        pe.wait_ge(s["ffn_gelu"], b * 4 + (c - 3))
                        pe.nop(nofuse=True)
                    mm(S[c // 2][:, (c % 2) * 512:(c % 2) * 512 + 512], w1[:, 2 * c:2 * c + 2, :].rearrange("i e o -> i (e o)"),
                       xnT_all[:, ds(b * T, T)], start=True, stop=True).then_inc(s["ffn_h"], 1)
                    if c == 1 and between is not None:
                        between()

            def weights(b, c):
                pe.wait_ge(s["ffn_hs"], b * 4 + c + 3)
                pe.nop(nofuse=True)
                mm(PT[:, (c % 2) * 512:(c % 2) * 512 + 512], pairsel[:, c, :], cT_all[:, ds(b * T, T)],
                   start=True, stop=True).then_inc(s["ffn_cb"], 1)

            def outputs(b, first, more=True):
                if not first:
                    pe.wait_ge(s["ffn_yT"], b)
                    pe.nop(nofuse=True)
                for i in range(3):
                    mm(O[:], b2_parts[:, i, :], cT_all[:, ds(b * T, T)], start=(i == 0), stop=(i == 2))
                for c in range(4):
                    pe.wait_ge(s["ffn_hs"], b * 4 + c + 5)
                    last = mm(O[0:C, :], w2[:, c, :], hs[c], start=False, stop=True, skip_group_check=True)
                    if c == 3:
                        last.then_inc(s["ffn_y"], 1)
                    if more:
                        weights(b + 1, c)

            def back(b, first=False):
                pe.wait_ge(s["ffn_yT"], b + 1)
                if not first:
                    pe.wait_ge(s["ffn_out1"], b)
                pe.nop(nofuse=True)
                for t in range(NT):
                    last = tp(X[:, t * C:(t + 1) * C], yT[:, t * P:(t + 1) * P], cst[0:C, 0:C])
                last.then_inc(s["ffn_back"], 1)

            hidden(0, False)
            pe.wait_ge(s["comb_ready"], 1)
            for b in range(B):
                if b >= 2:
                    pe.wait_ge(s["cT_sb"], b - 1)
                for t in range(NT):
                    last = tp(PT[0:3 * NE, (b % 2) * 512 + t * P:(b % 2) * 512 + (t + 1) * P],
                              cparts[:, b * NT + t].rearrange("p a e -> p (a e)"), ident)
                last.then_inc(s["cT_psum"], 1)
            pe.wait_ge(s["cT_sb"], B)
            pe.wait_ge(s["pairsel_ready"], 1)
            for c in range(4):
                weights(0, c)
            hidden(1)
            outputs(0, True)
            hidden(2, between=lambda: back(0, True))
            outputs(1, False)
            with pe.Fori(0, B - 3) as b:
                hidden(b + 3, between=lambda: back(b + 1))
                outputs(b + 2, False)
            back(B - 2)
            outputs(B - 1, False, False)
            back(B - 1)


N_W = 30


def _constants():
    import numpy as np
    c = np.zeros((P, K_END), np.float32)
    c[:, K_ID:K_ID + P] = np.eye(P)
    q, k = np.arange(P)[:, None], np.arange(P)[None, :]
    c[:, K_MASK:K_MASK + P] = np.where(k > q, 0.0, -1e30)
    c[:, K_MASK + P:K_MASK + 2 * P] = np.where(k <= q, 0.0, -1e30)
    f = 1.0 / 10000.0 ** (np.arange(0, ROPE, 2, dtype=np.float32) / ROPE)
    ang = np.outer(np.arange(T, dtype=np.float32), f)
    for col, tab in ((K_COS, np.cos(ang)), (K_SIN, np.sin(ang))):
        for t in range(5):
            rows = tab[(t % NT) * P:(t % NT) * P + P]
            c[:, col + t * ROPE:col + (t + 1) * ROPE] = np.concatenate([rows, rows], 1)
    c[:, K_IOTA:K_IOTA + P] = np.arange(P)
    c[:, K_TRI:K_TRI + NE * NE] = (np.arange(NE)[None, :] < np.arange(NE)[:, None]).astype(np.float32).reshape(-1)
    pos = np.tile(np.arange(T, dtype=np.float32), (B, 1))
    pair = np.zeros((NE, NE // 2, 2, P // 2), np.float32)
    for e in range(NE):
        pair[e, e // 2, e % 2] = 1.0
    return {"c_cst": c, "c_pos": pos, "c_pair": pair.reshape(NE, -1)}


def kernel(**inputs):
    import numpy as _np
    import concourse.bacc as _bacc
    from concourse import mybir as _mybir
    from concourse.bass_utils import run_bass_kernel_spmd as _run

    nc = _bacc.Bacc("TRN2", target_bir_lowering=False, num_devices=1)
    arrays, aps = {}, {}
    given = {n: _np.ascontiguousarray(inputs[n]) for n in ARGS}
    given.update(_constants())
    given["c_rwT"] = _np.ascontiguousarray(given["L0_ffn_router_w"].T)
    given["c_b1T"] = _np.ascontiguousarray(given["L0_ffn_b1"].reshape(NE // 2, P).T)
    for name, a in given.items():
        arrays[f"in_{name}_dram"] = a
        aps[name] = nc.dram_tensor(f"in_{name}_dram", a.shape, _mybir.dt.from_np(a.dtype), kind="ExternalInput").ap()
    out = nc.dram_tensor("out_0_dram", (B, T, C), _mybir.dt.float32, kind="ExternalOutput").ap()
    tower(nc, aps, out)
    r = _run(nc, [arrays], core_ids=[0])
    return r.results[0]["out_0_dram"]
```
